# Optimizing a Trainium2 kernel written in Bass

```python
import numpy as np
import jax
import jax.numpy as jnp

def _softmax(x, axis=-1):
    return jax.nn.softmax(x, axis=axis)

def _gelu(x):
    return jax.nn.gelu(x, approximate=True)

def _silu(x):
    return jax.nn.silu(x)

def _sigmoid(x):
    return jax.nn.sigmoid(x)

def _layernorm(x, axis=-1, eps=1e-05):
    m = jnp.mean(x, axis=axis, keepdims=True)
    v = jnp.var(x, axis=axis, keepdims=True)
    return (x - m) / jnp.sqrt(v + eps)

def _scatter_add(tgt, idx, src, axis=0):
    return tgt.at[idx].add(src)

def _segment_sum(src, seg, n):
    return jax.ops.segment_sum(src, seg, n)
kernel_name = 'mk_seq_postln_d1_jaxref_r8_594410'

def setup_inputs(seed: int=0):
    np.random.seed(seed)
    _w = jnp.asarray

    def _L0_attn_setup():
        import jax, jax.numpy as jnp
        import numpy as np
        B, T, D = (1, 256, 128)
        H, DH, DV, DF = (16, 64, 64, 512)
        EPS_LN = 1e-05
        EPS_DEN = 1e-06

        def _layernorm(x, g, b):
            m = jnp.mean(x, axis=-1, keepdims=True)
            v = jnp.mean((x - m) ** 2, axis=-1, keepdims=True)
            return (x - m) / jnp.sqrt(v + EPS_LN) * g + b

        def _phi(x):
            return jax.nn.elu(x) + 1.0

        def _linear_attention(x, Wq, Wk, Wv, Wo):
            b, t, d = x.shape
            Q = _phi((x @ Wq).reshape(b, t, H, DH)).transpose(0, 2, 1, 3)
            K = _phi((x @ Wk).reshape(b, t, H, DH)).transpose(0, 2, 1, 3)
            V = (x @ Wv).reshape(b, t, H, DV).transpose(0, 2, 1, 3)
            KV = jnp.einsum('bhti,bhtj->bhtij', K, V)
            S = jnp.cumsum(KV, axis=2)
            z = jnp.cumsum(K, axis=2)
            num = jnp.einsum('bhti,bhtij->bhtj', Q, S)
            den = jnp.maximum(jnp.einsum('bhti,bhti->bht', Q, z), EPS_DEN)[..., None]
            out = (num / den).transpose(0, 2, 1, 3).reshape(b, t, H * DV)
            return out @ Wo
        key = jax.random.key(seed)
        ks = jax.random.split(key, 8)
        s = 0.02
        return {'x': jax.random.normal(ks[0], (B, T, D), dtype=jnp.float32), 'ln1_g': jnp.ones((D,), jnp.float32), 'ln1_b': jnp.zeros((D,), jnp.float32), 'Wq': jax.random.normal(ks[1], (D, H * DH), jnp.float32) * s, 'Wk': jax.random.normal(ks[2], (D, H * DH), jnp.float32) * s, 'Wv': jax.random.normal(ks[3], (D, H * DV), jnp.float32) * s, 'Wo': jax.random.normal(ks[4], (H * DV, D), jnp.float32) * s, 'ln2_g': jnp.ones((D,), jnp.float32), 'ln2_b': jnp.zeros((D,), jnp.float32), 'Wf1': jax.random.normal(ks[5], (D, DF), jnp.float32) * s, 'Wf2': jax.random.normal(ks[6], (DF, D), jnp.float32) * s}
    _L0_attn_in = _L0_attn_setup()

    def _L0_ffn_setup():
        import jax, jax.numpy as jnp
        import numpy as np
        B, S, H, F, E, K = (4, 256, 128, 512, 8, 2)
        key = jax.random.key(seed)
        ks = jax.random.split(key, 4)
        sc = lambda d: 1.0 / np.sqrt(d)
        return {'x': jax.random.normal(ks[0], (B, S, H), jnp.float32), 'gate_w': jax.random.normal(ks[1], (H, E), jnp.float32) * sc(H), 'gate_b': jnp.zeros((E,), jnp.float32), 'w1': jax.random.normal(ks[2], (E, H, F), jnp.float32) * sc(H), 'b1': jnp.zeros((E, F), jnp.float32), 'w2': jax.random.normal(ks[3], (E, F, H), jnp.float32) * sc(F), 'b2': jnp.zeros((E, H), jnp.float32)}
    _L0_ffn_in = _L0_ffn_setup()
    _d = {'L0_attn_x': _L0_attn_in['x'], 'L0_attn_ln1_g': _L0_attn_in['ln1_g'], 'L0_attn_ln1_b': _L0_attn_in['ln1_b'], 'L0_attn_Wq': _L0_attn_in['Wq'], 'L0_attn_Wk': _L0_attn_in['Wk'], 'L0_attn_Wv': _L0_attn_in['Wv'], 'L0_attn_Wo': _L0_attn_in['Wo'], 'L0_attn_ln2_g': _L0_attn_in['ln2_g'], 'L0_attn_ln2_b': _L0_attn_in['ln2_b'], 'L0_attn_Wf1': _L0_attn_in['Wf1'], 'L0_attn_Wf2': _L0_attn_in['Wf2'], 'L0_ffn_gate_w': _L0_ffn_in['gate_w'], 'L0_ffn_gate_b': _L0_ffn_in['gate_b'], 'L0_ffn_w1': _L0_ffn_in['w1'], 'L0_ffn_b1': _L0_ffn_in['b1'], 'L0_ffn_w2': _L0_ffn_in['w2'], 'L0_ffn_b2': _L0_ffn_in['b2']}
    _x0 = _d['L0_attn_x']
    _d['L0_attn_x'] = jax.random.normal(jax.random.fold_in(jax.random.key(seed), 1), (8, 512, 128), dtype=_x0.dtype)
    del _x0
    return _d

def reference(L0_attn_x, L0_attn_ln1_g, L0_attn_ln1_b, L0_attn_Wq, L0_attn_Wk, L0_attn_Wv, L0_attn_Wo, L0_attn_ln2_g, L0_attn_ln2_b, L0_attn_Wf1, L0_attn_Wf2, L0_ffn_gate_w, L0_ffn_gate_b, L0_ffn_w1, L0_ffn_b1, L0_ffn_w2, L0_ffn_b2):

    def _L0_attn_ref(x, ln1_g, ln1_b, Wq, Wk, Wv, Wo, ln2_g, ln2_b, Wf1, Wf2):
        import jax, jax.numpy as jnp
        import numpy as np
        B, T, D = (1, 256, 128)
        H, DH, DV, DF = (16, 64, 64, 512)
        EPS_LN = 1e-05
        EPS_DEN = 1e-06

        def _layernorm(x, g, b):
            m = jnp.mean(x, axis=-1, keepdims=True)
            v = jnp.mean((x - m) ** 2, axis=-1, keepdims=True)
            return (x - m) / jnp.sqrt(v + EPS_LN) * g + b

        def _phi(x):
            return jax.nn.elu(x) + 1.0

        def _linear_attention(x, Wq, Wk, Wv, Wo):
            b, t, d = x.shape
            Q = _phi((x @ Wq).reshape(b, t, H, DH)).transpose(0, 2, 1, 3)
            K = _phi((x @ Wk).reshape(b, t, H, DH)).transpose(0, 2, 1, 3)
            V = (x @ Wv).reshape(b, t, H, DV).transpose(0, 2, 1, 3)
            KV = jnp.einsum('bhti,bhtj->bhtij', K, V)
            S = jnp.cumsum(KV, axis=2)
            z = jnp.cumsum(K, axis=2)
            num = jnp.einsum('bhti,bhtij->bhtj', Q, S)
            den = jnp.maximum(jnp.einsum('bhti,bhti->bht', Q, z), EPS_DEN)[..., None]
            out = (num / den).transpose(0, 2, 1, 3).reshape(b, t, H * DV)
            return out @ Wo
        x = x + _linear_attention(_layernorm(x, ln1_g, ln1_b), Wq, Wk, Wv, Wo)
        h = _layernorm(x, ln2_g, ln2_b)
        x = x + jax.nn.gelu(h @ Wf1, approximate=False) @ Wf2
        return x

    def _L0_ffn_ref(x, gate_w, gate_b, w1, b1, w2, b2):
        import jax, jax.numpy as jnp
        import numpy as np
        B, S, H, F, E, K = (4, 256, 128, 512, 8, 2)
        Bb, Ss, Hh = x.shape
        xf = x.reshape(-1, Hh)
        gate = jax.nn.softmax(xf @ gate_w + gate_b)
        topv, topi = jax.lax.top_k(gate, K)
        topv = topv / topv.sum(-1, keepdims=True)
        combine = (jax.nn.one_hot(topi, gate.shape[-1], dtype=xf.dtype) * topv[..., None]).sum(1)

        def body(acc, p):
            w1e, b1e, w2e, b2e, ce = p
            h = jax.nn.relu(xf @ w1e + b1e)
            y = h @ w2e + b2e
            return (acc + y * ce[:, None], None)
        acc0 = jnp.zeros_like(xf)
        out, _ = jax.lax.scan(body, acc0, (w1, b1, w2, b2, combine.T))
        return out.reshape(Bb, Ss, Hh)
    x = L0_attn_x
    x = _layernorm(x + _L0_attn_ref(x, L0_attn_ln1_g, L0_attn_ln1_b, L0_attn_Wq, L0_attn_Wk, L0_attn_Wv, L0_attn_Wo, L0_attn_ln2_g, L0_attn_ln2_b, L0_attn_Wf1, L0_attn_Wf2), axis=-1)
    x = _layernorm(x + _L0_ffn_ref(x, L0_ffn_gate_w, L0_ffn_gate_b, L0_ffn_w1, L0_ffn_b1, L0_ffn_w2, L0_ffn_b2), axis=-1)
    return x

_drawn_inputs = setup_inputs


def setup_inputs(seed=0):
    import zlib

    import numpy as np

    out = dict(_drawn_inputs(seed))
    spreads = {'L0_attn_ln1_g': (1.0, 0.6),
     'L0_attn_ln1_b': (0.0, 0.317),
     'L0_attn_ln2_g': (1.0, 0.587),
     'L0_attn_ln2_b': (0.0, 0.351),
     'L0_ffn_gate_b': (0.0, 0.1),
     'L0_ffn_b1': (0.0, 0.1),
     'L0_ffn_b2': (0.0, 0.1)}
    factors = {'L0_attn_Wq': 66.408, 'L0_attn_Wk': 22.733}
    for name, (base, spread) in spreads.items():
        noise = np.random.default_rng([zlib.crc32(name.encode()), seed]).standard_normal(out[name].shape)
        drawn = base * np.exp(spread * noise) if base else spread * noise
        out[name] = jnp.asarray(drawn.astype(out[name].dtype))
    for name, factor in factors.items():
        out[name] = (out[name] * factor).astype(out[name].dtype)
    return out
```

```python
from contextlib import ExitStack

import concourse.bass as bass
from concourse import mybir

F32 = mybir.dt.float32
F32R = mybir.dt.float32r
BF16 = mybir.dt.bfloat16
U32 = mybir.dt.uint32
I32 = mybir.dt.int32
ALU = mybir.AluOpType
ACT = mybir.ActivationFunctionType
AX = mybir.AxisListType

P = 128
B, T, D = 8, 512, 128
CH = T // P
H, DH = 16, 64
PAIRS = H // 2
DV1 = DH + 1
NF = 4
F = NF * P
E = 8
TOKENS = B * T
EPS_LN = 1e-5
EPS_DEN = 1e-6

REGION = TOKENS + P
DUMMY = 10
ROW = 132
TILES = 72
RING = 8
AHEAD = 2
PAIR_ROWS = 2 * TOKENS
PAD_DEST = PAIR_ROWS
DUMMY_DEST = PAD_DEST + E * P
WORK = 19
RESULTS = DUMMY_DEST + E * P


def build(nc, x_d, ln1_g, ln1_b, wq_d, wk_d, wv_d, wo_d, ln2_g, ln2_b, wf1_d, wf2_d,
          gate_w, gate_b, w1_d, b1_d, w2_d, b2_d, out_d):
    rows_d = nc.dram_tensor("routed_rows", (E * REGION + DUMMY * P, ROW), F32, kind="Internal").ap()
    res_d = nc.dram_tensor("expert_results", (RESULTS, D), F32, kind="Internal").ap()
    x3_d = nc.dram_tensor("moe_input", (TOKENS, D), F32, kind="Internal").ap()

    with ExitStack() as ctx:
        def sb(name, shape, dt=F32):
            return ctx.enter_context(nc.sbuf_tensor(name, shape, dt))

        def sem(name):
            return ctx.enter_context(nc.semaphore(name))

        wq = [sb(f"wq_{k}", [P, H * DH], F32R) for k in ("hi", "lo")]
        wk = [sb(f"wk_{k}", [P, H * DH], F32R) for k in ("hi", "lo")]
        wv = [sb(f"wv_{k}", [P, H * DH], F32R) for k in ("hi", "lo")]
        wo = [sb(f"wo_{k}", [P, PAIRS * D], F32R) for k in ("hi", "lo")]
        wf1 = [sb(f"wf1_{k}", [P, F], F32R) for k in ("hi", "lo")]
        wf2 = [sb(f"wf2_{k}", [P, F], F32R) for k in ("hi", "lo")]
        w1 = [sb(f"w1_{k}", [P, E * F], F32R) for k in ("hi", "lo")]
        w2 = sb("w2", [P, E * F])
        b1_rows = sb("b1_rows", [P, E * F])
        stage = sb("stage", [P, 2, F])
        b2_rows = stage[:, :, :].rearrange("p a f -> p (a f)")
        ident = sb("ident", [P, P])
        causal = sb("causal", [P, P])
        before = sb("before", [P, P], BF16)
        ones_b = sb("ones_b", [P, P], BF16)
        cols = sb("cols", [P, 4])
        neg_half = sb("neg_half", [P, CH])
        iota_e = sb("iota_e", [P, E])
        gw = sb("gw", [P, E])
        gb = sb("gb", [P, E])
        v_aug = sb("v_aug", [P, CH * H * DV1])
        va = v_aug[:, :].rearrange("p (c h j) -> p c h j", c=CH, h=H)
        hT = [[sb(f"hT{n}_{k}", [P, T], F32R) for k in ("hi", "lo")] for n in range(2)]
        h2T = [sb(f"h2T_{k}", [P, T], F32R) for k in ("hi", "lo")]
        gT = [sb(f"gT_{k}", [P, NF, T], F32R) for k in ("hi", "lo")]
        oT = [sb(f"oT_{k}", [P, T], F32R) for k in ("hi", "lo")]
        state = sb("state", [P, CH - 1, 2 * DV1])
        routed = sb("routed", [P, CH, 2, ROW])
        work = sb("work", [P, WORK * T])
        spot = [0]

        def take(n, back=None):
            if back is not None:
                spot[0] = back
            a = spot[0]
            spot[0] += n
            return work[:, a:a + n]

        def chunks(ap):
            return ap.rearrange("p (c d) -> p c d", c=CH)

        qT = [take(T) for _ in range(2)]
        kT = [take(T) for _ in range(2)]
        ktok = chunks(take(T))
        am = [chunks(take(T)) for _ in range(2)]
        on = chunks(take(T))
        e_q, e_k = take(T), take(T)
        xln = chunks(take(T))
        xres = chunks(take(T))
        h32 = take(T)
        g32 = [take(T) for _ in range(2)]
        behind = spot[0]
        x1 = chunks(take(T))
        xx1 = chunks(take(T))
        colT = take(T)
        pads = take(E * ROW, behind).rearrange("p (e w) -> p e w", e=E)
        gt32 = take(E * 32, 0).rearrange("p (e m) -> p e m", e=E)
        le = take((TILES + AHEAD) * E).rearrange("p (t e) -> p t e", e=E)
        xg = [take(ROW, 0 if n == 0 else None) for n in range(RING)]
        hb = [take(F) for _ in range(2)]
        hTe = [take(F) for _ in range(2)]
        yb = [take(D) for _ in range(2)]
        yw = [take(D) for _ in range(RING)]
        x3_all = take(B * T)
        xc = x3_all.rearrange("p (b c d) -> p b c d", b=B, c=CH)
        zs = [chunks(take(T)) for _ in range(2)]
        assert spot[0] <= WORK * T
        z = [v_aug[:, n * 2 * T:(n + 1) * 2 * T].rearrange("p (c k d) -> p c k d", c=CH, k=2) for n in range(2)]
        sc = [chunks(v_aug[:, n * T:(n + 1) * T]) for n in (4, 5)]
        oc = [chunks(v_aug[:, n * T:(n + 1) * T]) for n in (6, 7)]
        xT = [[sb(f"xT{n}_{k}", [P, P], F32R) for k in ("hi", "lo")] for n in range(2)]
        stats = [sb(f"stats{n}", [P, CH, 6]) for n in range(3)]
        mv = [sb(f"mv{n}", [P, CH, 2]) for n in range(3)]
        ve = [sb(f"ve{n}", [P, CH]) for n in range(3)]
        rstd = [sb(f"rstd{n}", [P, CH]) for n in range(3)]
        den = sb("den", [P, 4])
        rden = sb("rden", [P, 4])
        lg = sb("lg", [P, CH, E])
        lmax = sb("lmax", [P, CH])
        pe_ = sb("gate_exp", [P, CH, E])
        top = sb("top", [P, CH, 8])
        topi = sb("topi", [P, CH, 8], U32)
        wsum = sb("wsum", [P, CH])
        onehot = sb("onehot", [P, 2, CH, E])
        chosen = sb("chosen", [P, CH, E], BF16)
        base = sb("base", [P, CH + 1, E])
        rank = sb("rank", [P, CH, E])
        prod = sb("prod", [P, 2, CH, E])
        slot_f = sb("slot_f", [P, 2, CH])
        slot = sb("slot", [P, 2, CH], U32)
        dest = sb("dest", [P, CH, 2])
        cnt = sb("cnt", [P, E])
        nt = sb("nt", [P, E])
        ntc = sb("ntc", [P, E])
        one_e = sb("one_e", [P, E])
        m32 = sb("m32", [P, 32])
        tidx = sb("tidx", [P, TILES + AHEAD])
        en = sb("en", [P, TILES + AHEAD])
        cx = sb("cx", [P, TILES + AHEAD])
        tile_e = sb("tile_e", [P, TILES + AHEAD], I32)
        tile_r = sb("tile_r", [P, TILES + AHEAD], I32)
        padi = sb("padi", [P, E], U32)
        pcol = sb("pcol", [P, 1])
        padf = sb("padf", [P, 2 * E])
        rs_c = [sb(f"rs_c{n}", [P, CH]) for n in range(2)]
        nmr = [sb(f"nmr{n}", [P, CH]) for n in range(2)]

        bank = [ctx.enter_context(nc.psum_tensor(f"bank{n}", [P, 512], F32)) for n in range(8)]
        bkA, bkB, bkC, bkE, bkF, bkG, bkH, bkY = bank

        ld_stage = [sem(f"ld_stage{n}") for n in range(2)]
        ld_w, ld_small, ld_b1, ld_w2, ld_b2 = (sem(n) for n in ("ld_w", "ld_small", "ld_b1", "ld_w2", "ld_b2"))
        ld_xln, ld_xres = sem("ld_xln"), sem("ld_xres")
        cst, cst_dve, whi, wlo, w1hi, w1lo = (sem(n) for n in ("cst", "cst_dve", "whi", "wlo", "w1hi", "w1lo"))
        q_mm, k_mm, v_mm, sc_mm, kt_mm, u_mm, o_mm, ot_mm, wo_mm = (
            sem(n) for n in ("q_mm", "k_mm", "v_mm", "sc_mm", "kt_mm", "u_mm", "o_mm", "ot_mm", "wo_mm"))
        q_relu, q_exp, k_relu, k_exp, v_sb, kt_sb, ot_hi, yT_sb = (
            sem(n) for n in ("q_relu", "q_exp", "k_relu", "k_exp", "v_sb", "kt_sb", "ot_hi", "yT_sb"))
        q_phi, k_phi, a_msk, s_part, s_sb, o_den, o_sb, ot_lo = (
            sem(n) for n in ("q_phi", "k_phi", "a_msk", "s_part", "s_sb", "o_den", "o_sb", "ot_lo"))
        ln_st, ln_mv, ln_ve, ln_r, ln_x = ([sem(f"{a}{n}") for n in range(3)]
                                           for a in ("ln_st", "ln_mv", "ln_ve", "ln_r", "ln_x"))
        f1_mm, yt_mm, h2_mm, ff1_mm, ff2_mm, y2_mm, x3_mm, gate_mm, rank_mm = (
            sem(n) for n in ("f1_mm", "yt_mm", "h2_mm", "ff1_mm", "ff2_mm", "y2_mm", "x3_mm", "gate_mm", "rank_mm"))
        h32_sb, h_hi, h_lo, x1_sb, xx_sb, h232_sb, h2_hi, h2_lo, gelu_sb, g_hi, g_lo = (
            sem(n) for n in ("h32_sb", "h_hi", "h_lo", "x1_sb", "xx_sb", "h232_sb", "h2_hi", "h2_lo", "gelu_sb",
                             "g_hi", "g_lo"))
        y2_sb, s3_sb, x3T_sb, lg_sb, lg_st, ex_sb, tp, rk, rt_sb, dup_sb, x3_st, sct = (
            sem(n) for n in ("y2_sb", "s3_sb", "x3T_sb", "lg_sb", "lg_st", "ex_sb", "tp", "rk", "rt_sb", "dup_sb",
                             "x3_st", "sct"))
        plan, nh_set, pads_dmy, dmy_st, pad_st = (sem(n) for n in ("plan", "nh_set", "pads_dmy", "dmy_st", "pad_st"))
        ld_xg = [sem(f"ld_xg{n}") for n in range(RING)]
        res_st = [sem(f"res_st{n}") for n in range(RING)]
        xt_mm, l1_mm, ht_mm, l2_mm, xt_hi, xt_lo, hb_sb, ht_a, ht_v, yb_sb, yw_sb = (
            sem(n) for n in ("xt_mm", "l1_mm", "ht_mm", "l2_mm", "xt_hi", "xt_lo", "hb_sb", "ht_a", "ht_v", "yb_sb",
                             "yw_sb"))
        ld_x3 = sem("ld_x3")
        ld_z = [sem(f"ld_z{n}") for n in range(2)]
        z_sum, c_sb, c_st, c_mv, c_ve, c_r, c_nb, c_out = (
            sem(n) for n in ("z_sum", "c_sb", "c_st", "c_mv", "c_ve", "c_r", "c_nb", "c_out"))
        out_st = [sem(f"out_st{n}") for n in range(2)]

        def x_of(b):
            return x_d[bass.ds(b, 1), :, :].rearrange("o (c p) d -> p (o c) d", p=P)

        CST_ALL = 15
        PLAN_DONE = 14
        TP_STEPS = 4
        RK_STEPS = CH + 7

        def apart(eng):
            eng.wait_ge(nh_set, 1)

        block = ctx.enter_context(nc.Block())

        @block.sync
        def _(sp):
            sp.dma_start(xln, x_of(0)).then_inc(ld_xln, 16)
            sp.dma_start(cols[:, 0:1], ln1_g.rearrange("(p o) -> p o", o=1)).then_inc(ld_small, 16)
            sp.dma_start(cols[:, 1:2], ln1_b.rearrange("(p o) -> p o", o=1)).then_inc(ld_small, 16)
            sp.dma_start(v_aug[:, 0:1024], wq_d).then_inc(ld_w, 16)
            sp.dma_start(v_aug[:, 1024:2048], wk_d).then_inc(ld_w, 16)
            sp.dma_start(v_aug[:, 2048:3072], wv_d).then_inc(ld_w, 16)
            sp.dma_start(v_aug[:, 3072:4096].rearrange("p (t n) -> p t n", t=PAIRS),
                         wo_d.rearrange("(t p) n -> p t n", p=P)).then_inc(ld_w, 16)
            sp.dma_start(stage[:, 0, :], wf1_d).then_inc(ld_stage[0], 16)
            sp.dma_start(stage[:, 1, :].rearrange("p (t n) -> p t n", t=NF),
                         wf2_d.rearrange("(t p) n -> p t n", p=P)).then_inc(ld_stage[1], 16)
            sp.dma_start(cols[:, 2:3], ln2_g.rearrange("(p o) -> p o", o=1)).then_inc(ld_small, 16)
            sp.dma_start(cols[:, 3:4], ln2_b.rearrange("(p o) -> p o", o=1)).then_inc(ld_small, 16)
            sp.dma_start(gw[:], gate_w).then_inc(ld_small, 16)
            sp.dma_start(gb[:], gate_b.partition_broadcast(P)).then_inc(ld_small, 16)
            sp.wait_ge(wlo, 6)
            for e in range(2):
                sp.dma_start(stage[:, e, :], w1_d[e]).then_inc(ld_stage[e], 16)
            sp.dma_start(w2[:, :].rearrange("p (e t n) -> p e t n", e=E, t=NF),
                         w2_d.rearrange("e (t p) n -> p e t n", p=P)).then_inc(ld_w2, 16)
            sp.dma_start(b1_rows[:, :], b1_d.rearrange("e f -> (e f)").partition_broadcast(P)).then_inc(ld_b1, 16)
            sp.wait_ge(pads_dmy, 1)
            for block0, n in ((0, E), (E, DUMMY - E)):
                at = E * REGION + block0 * P
                sp.dma_start(rows_d[at:at + n * P, :].rearrange("(e p) w -> p e w", p=P),
                             pads[:, 0:n, :]).then_inc(dmy_st, 16)

            def sequence(b, first, last):
                if not last:
                    sp.wait_ge(f1_mm, b + 1)
                    sp.dma_start(xln, x_of(b + 1)).then_inc(ld_xln, 16)
                if not first:
                    sp.wait_ge(xx_sb, b)
                sp.dma_start(xres, x_of(b)).then_inc(ld_xres, 16)
                if not first and not last:
                    store_x3(b - 1)

            def store_x3(b):
                sp.wait_ge(ln_x[2], b + 1)
                sp.dma_start(x3_d[bass.ds(b * T, T), :].rearrange("(c p) d -> p c d", p=P),
                             routed[:, :, 0, 0:D]).then_inc(x3_st, 16)

            sequence(0, True, False)
            with sp.Fori(1, B - 1) as b:
                sequence(b, False, False)
            sequence(B - 1, False, True)
            for e in range(2, E):
                sp.wait_ge(w1lo, e - 1)
                sp.dma_start(stage[:, e % 2, :], w1_d[e]).then_inc(ld_stage[e % 2], 16)
            store_x3(B - 2)
            store_x3(B - 1)
            sp.wait_ge(w1lo, E)
            sp.dma_start(b2_rows, b2_d.rearrange("e f -> (e f)").partition_broadcast(P)).then_inc(ld_b2, 16)

            sp.wait_ge(plan, PLAN_DONE)
            for e in range(E):
                at = sp.value_load(padi[0:1, e:e + 1], min_val=0, max_val=E * REGION - P)
                sp.dma_start(rows_d[bass.ds(at, P), :], pads[:, e, :]).then_inc(pad_st, 16)

            sp.wait_ge(sct, 16 * 2 * CH * B)
            sp.wait_ge(pad_st, 16 * E)
            sp.wait_ge(dmy_st, 32)

            def load_tile(t0, n, reuse):
                at = sp.value_load(tile_r[0:1, bass.ds(t0 + n, 1)], min_val=0, max_val=E * REGION + (DUMMY - 1) * P)
                if reuse:
                    sp.wait_ge(res_st[n], t0 * (16 // RING))
                sp.dma_start(xg[n], rows_d[bass.ds(at, P), :]).then_inc(ld_xg[n], 16)

            for t in range(RING):
                load_tile(0, t, False)
            sp.wait_ge(x3_st, 16 * B)
            sp.dma_start(xc, x3_d.rearrange("(b c p) d -> p b c d", p=P, c=CH)).then_inc(ld_x3, 16)
            with sp.Fori(RING, TILES - RING + 1, RING) as t:
                for n in range(RING):
                    load_tile(t, n, True)
            for n in range(AHEAD):
                load_tile(TILES, n, True)

            for n in range(RING):
                sp.wait_ge(res_st[n], 16 * (TILES // RING))

            def load_group(i, n, reuse):
                if reuse:
                    sp.wait_ge(z_sum, i - 1)
                sp.dma_start(z[n], res_d[bass.ds(i * 2 * T, 2 * T), :].rearrange("(c p k) d -> p c k d", p=P, k=2)
                             ).then_inc(ld_z[n], 16)

            def store_group(i, n):
                sp.wait_ge(c_out, (i + 1) * CH)
                out_b = out_d[bass.ds(i, 1), :, :].rearrange("o (c p) d -> p (o c) d", p=P)
                sp.dma_start(out_b, oc[n]).then_inc(out_st[n], 16)

            load_group(0, 0, False)
            load_group(1, 1, False)
            with sp.Fori(2, B - 1, 2) as i:
                for n in range(2):
                    load_group(i + n, n, True)
                    store_group(i + n - 2, n)
            store_group(B - 2, 0)
            store_group(B - 1, 1)
            for n in range(2):
                sp.wait_ge(out_st[n], 16 * (B // 2))

        @block.tensor
        def _(pe):
            def split3(out, w, wcols, m, mcols, first=True, last=True):
                pe.matmul(out, w[0][:, wcols], m[0][:, mcols], start=first, stop=False)
                pe.matmul(out, w[1][:, wcols], m[0][:, mcols], start=False, stop=False)
                return pe.matmul(out, w[0][:, wcols], m[1][:, mcols], start=False, stop=last)

            def blk(c, n=P):
                return slice(c * n, (c + 1) * n)

            ALLT = slice(0, T)

            def turn(out, src):
                for c in range(CH):
                    mm = pe.transpose(out[:, blk(c)], src(c), ident[:, :])
                return mm

            def q_proj(par, p):
                split3(bkA[:, :], wq, blk(p), hT[par], ALLT).then_inc(q_mm, 1)

            def k_proj(par, p):
                split3(bkB[:, :], wk, blk(p), hT[par], ALLT).then_inc(k_mm, 1)

            def v_proj(par, half, c):
                h, out = hT[par], bkC[:, :]
                pe.matmul(out, h[0][:, blk(c)], wv[0][:, blk(half, 512)], start=True, stop=False)
                pe.matmul(out, h[1][:, blk(c)], wv[0][:, blk(half, 512)], start=False, stop=False)
                pe.matmul(out, h[0][:, blk(c)], wv[1][:, blk(half, 512)], start=False, stop=True).then_inc(v_mm, 1)

            def front_t(b):
                pe.wait_ge(ln_x[0], b + 1)
                turn(bkE, lambda c: xln[:, c, :]).then_inc(f1_mm, 1)

            def otr():
                turn(bkC, lambda c: on[:, c, :]).then_inc(ot_mm, 1)

            def wo_acc(p):
                split3(bkY[:, :], wo, blk(p), oT, ALLT, first=(p == 0), last=(p == PAIRS - 1)).then_inc(wo_mm, 1)

            def y_t(b, out):
                pe.wait_ge(yT_sb, b + 1)
                turn(out, lambda c: colT[:, blk(c)]).then_inc(yt_mm, 1)

            def h2_t(b, out):
                pe.wait_ge(ln_x[1], b + 1)
                turn(out, lambda c: x1[:, c, :]).then_inc(h2_mm, 1)

            def ffn1(b, f, out):
                if f == 0:
                    pe.wait_ge(h2_lo, b + 1)
                split3(out[:, :], wf1, blk(f), h2T, ALLT).then_inc(ff1_mm, 1)

            def ffn2(b, out):
                for f in range(NF):
                    pe.wait_ge(g_lo, b * NF + f + 1)
                    g = [gT[0][:, f, :], gT[1][:, f, :]]
                    mm = split3(out[:, :], wf2, blk(f), g, ALLT, first=(f == 0), last=(f == NF - 1))
                mm.then_inc(ff2_mm, 1)

            def y2_t(b, out):
                pe.wait_ge(y2_sb, b + 1)
                turn(out, lambda c: colT[:, blk(c)]).then_inc(y2_mm, 1)

            def x3_t(b, out):
                pe.wait_ge(ln_x[2], b + 1)
                turn(out, lambda c: routed[:, c, 0, 0:D]).then_inc(x3_mm, 1)

            def gate(b, out):
                pe.wait_ge(x3T_sb, b + 1)
                for c in range(CH):
                    mm = pe.matmul(out[:, blk(c, E)], colT[:, blk(c)], gw[:, :], start=True, stop=True)
                mm.then_inc(gate_mm, 1)

            def ranks(b, out):
                pe.wait_ge(tp, (b + 1) * TP_STEPS)
                flat = chosen[:, :, :].rearrange("p c e -> p (c e)")
                pe.matmul(out[:, 0:CH * E], before[:, :], flat, start=True, stop=True)
                pe.matmul(out[:, CH * E:2 * CH * E], ones_b[:, :], flat, start=True, stop=True).then_inc(rank_mm, 1)

            def step(b, par, p, first, last):
                g = b * PAIRS + p
                begin = first and p == 0
                cur = g_par = p % 2
                pe.wait_ge(v_sb, 2 * CH * B if last and p > CH else CH + g)
                if not begin:
                    pe.wait_ge(o_sb, 2 * g)
                    otr()
                pe.wait_ge(q_phi, g + 1)
                pe.wait_ge(k_phi, g + 1)
                if p == 2 and not last:
                    pe.wait_ge(h32_sb, b + 2)
                if not first:
                    done = {3: (gelu_sb, b * NF - 2), 4: (gelu_sb, b * NF), 5: (y2_sb, b), 6: (x3T_sb, b)}
                    if p in done:
                        pe.wait_ge(*done[p])
                for h in range(2):
                    if h == 1 and not first:
                        done = {1: (x1_sb, b), 2: (h232_sb, b), 3: (gelu_sb, b * NF - 2), 4: (gelu_sb, b * NF),
                                5: (s3_sb, b), 6: (lg_sb, b), 7: (rt_sb, b)}
                        if p in done:
                            pe.wait_ge(*done[p])
                    hs = slice(h * DH, (h + 1) * DH)
                    for c in range(CH):
                        mm = pe.matmul((bkE, bkF)[h][:, blk(c)], kT[cur][hs, blk(c)], qT[cur][hs, blk(c)],
                                       start=True, stop=True)
                    mm.then_inc(sc_mm, 1)
                if not begin:
                    pe.wait_ge(ot_lo, g)
                turn(bkC, lambda c: kT[cur][:, blk(c)]).then_inc(kt_mm, 1)
                if not begin:
                    if p == 1 and not first:
                        pe.wait_ge(yT_sb, b)
                    wo_acc((p - 1) % PAIRS)
                pe.wait_ge(kt_sb, g + 1)
                pe.wait_ge(v_sb, 2 * CH * b + (CH if p < PAIRS // 2 else 2 * CH))
                for c in range(CH - 1):
                    for h in range(2):
                        hs = slice(h * DH, (h + 1) * DH)
                        mm = pe.matmul(bkH[hs, 260 + c * DV1:260 + (c + 1) * DV1], ktok[:, c, hs],
                                       va[:, c, 2 * p + h, :], start=True, stop=True)
                mm.then_inc(u_mm, 1)
                nxt = not (last and p == PAIRS - 1)
                npar = par if p < PAIRS - 1 else 1 - par
                if nxt:
                    q_proj(npar, (p + 1) % PAIRS)
                pe.wait_ge(a_msk, 2 * g + 1)
                if p == 1 and not last:
                    front_t(b + 1)
                if not first:
                    if p == 2:
                        ffn1(b - 1, 0, bkE)
                    if p == 3:
                        ffn1(b - 1, 2, bkE)
                    if p == 4:
                        ffn2(b - 1, bkE)
                    if p == 5:
                        x3_t(b - 1, bkE)
                pe.wait_ge(a_msk, 2 * g + 2)

                def outputs(c, out):
                    if c > 0:
                        pe.matmul(out[:, 0:2 * DV1], qT[cur][:, blk(c)], state[:, c - 1, :], start=True, stop=False)
                    for h in range(2):
                        mm = pe.matmul(out[:, blk(h, DV1)], am[h][:, c, :], va[:, c, 2 * p + h, :],
                                       start=(c == 0), stop=(c == 0 or h == 1))
                    return mm

                outputs(0, bkG[:, 0:130])
                pe.wait_ge(s_sb, g + 1)
                outputs(1, bkG[:, 130:260]).then_inc(o_mm, 1)
                if nxt:
                    k_proj(npar, (p + 1) % PAIRS)
                if not first:
                    if p == 0:
                        y_t(b - 1, bkF)
                    if p == 1:
                        h2_t(b - 1, bkF)
                    if p == 2:
                        ffn1(b - 1, 1, bkF)
                    if p == 3:
                        ffn1(b - 1, 3, bkF)
                    if p == 4:
                        y2_t(b - 1, bkF)
                    if p == 5:
                        gate(b - 1, bkF)
                    if p == 6:
                        ranks(b - 1, bkF)
                if p < CH:
                    v_proj(par, 1, p)
                elif not last:
                    pe.wait_ge(h_lo, b + 2)
                    v_proj(1 - par, 0, p - CH)
                outputs(2, bkH[:, 0:130])
                outputs(3, bkH[:, 130:260]).then_inc(o_mm, 1)

            def sequence(b, par, first, last):
                for p in range(PAIRS):
                    step(b, par, p, first, last)

            pe.wait_ge(cst, CST_ALL)
            front_t(0)
            pe.wait_ge(h_lo, 1)
            pe.wait_ge(wlo, 4)
            q_proj(0, 0)
            k_proj(0, 0)
            for c in range(CH):
                if c > 0:
                    pe.wait_ge(v_sb, c)
                v_proj(0, 0, c)
            sequence(0, 0, True, False)
            with pe.Fori(1, B - 2, 2) as b:
                sequence(b, 1, False, False)
                sequence(b + 1, 0, False, False)
            sequence(B - 1, 1, False, True)

            b = B - 1
            pe.wait_ge(o_sb, 2 * B * PAIRS)
            otr()
            pe.wait_ge(ot_lo, B * PAIRS)
            wo_acc(PAIRS - 1)
            y_t(b, bkF)
            h2_t(b, bkE)
            ffn1(b, 0, bkA)
            ffn1(b, 1, bkB)
            ffn1(b, 2, bkG)
            ffn1(b, 3, bkH)
            ffn2(b, bkC)
            y2_t(b, bkY)
            x3_t(b, bkA)
            gate(b, bkB)
            ranks(b, bkG)

            pe.wait_ge(plan, PLAN_DONE)
            pe.wait_ge(ld_w2, 16)
            pe.wait_ge(w1lo, E)
            X, L, M, Y = bank[0:2], bank[2:4], bank[4:6], bank[6:8]

            def expert(t):
                return pe.value_load(tile_e[0:1, bass.ds(t, 1)], min_val=0, max_val=E - 1)

            def rows_t(t0, n, reuse):
                if n >= RING:
                    t0, n = t0 + RING, n - RING
                if reuse:
                    pe.wait_ge(xt_lo, t0 + n - 1)
                pe.wait_ge(ld_xg[n], t0 * (16 // RING) + 16)
                pe.transpose(X[n % 2][:, 0:P], xg[n][:, 0:D], ident[:, :]).then_inc(xt_mm, 1)

            def layer1(t, n, e, reuse):
                if reuse:
                    pe.wait_ge(hb_sb, t - 1)
                pe.wait_ge(xt_lo, t + 1)
                a, out = xT[n % 2], L[n % 2][:, :]
                pe.matmul(out, a[0][:, :], w1[0][:, bass.ds(e * F, F)], start=True, stop=False)
                pe.matmul(out, a[1][:, :], w1[0][:, bass.ds(e * F, F)], start=False, stop=False)
                pe.matmul(out, a[0][:, :], w1[1][:, bass.ds(e * F, F)], start=False, stop=True).then_inc(l1_mm, 1)

            def hidden_t(t, n, reuse):
                if reuse:
                    pe.wait_ge(ht_a, t - 1)
                pe.wait_ge(hb_sb, t + 1)
                for f in range(NF):
                    mm = pe.transpose(M[n % 2][:, blk(f)], hb[n % 2][:, blk(f)], ident[:, :])
                mm.then_inc(ht_mm, 1)

            def layer2(t, n, e, reuse):
                if reuse:
                    pe.wait_ge(yb_sb, t - 1)
                pe.wait_ge(ht_a, t + 1)
                for f in range(NF):
                    mm = pe.matmul(Y[n % 2][:, 0:D], hTe[n % 2][:, blk(f)], w2[:, bass.ds(e * F + f * D, D)],
                                   start=(f == 0), stop=(f == NF - 1))
                mm.then_inc(l2_mm, 1)

            def round_(t0, first):
                e = {} if first else {-1: expert(t0 - 1)}
                e[0] = expert(t0)
                for n in range(RING):
                    e[n + 1] = expert(t0 + n + 1)
                    rows_t(t0, n + 2, not (first and n == 0))
                    layer1(t0 + n + 1, n + 1, e[n + 1], not (first and n == 0))
                    hidden_t(t0 + n, n, not (first and n < 2))
                    if not (first and n == 0):
                        layer2(t0 + n - 1, n - 1, e[n - 1], not (first and n <= 2))

            rows_t(0, 0, False)
            rows_t(0, 1, False)
            layer1(0, 0, expert(0), False)
            round_(0, True)
            with pe.Fori(RING, TILES - RING + 1, RING) as t0:
                round_(t0, False)
            layer2(TILES - 1, RING - 1, expert(TILES - 1), True)

        @block.scalar
        def _(act):
            def copy(out, src):
                return act.activation(out, src, ACT.Copy)

            def y_copy(b):
                act.wait_ge(wo_mm, PAIRS * (b + 1))
                copy(colT, bkY[:, :]).then_inc(yT_sb, 1)

            def h2_copy(b):
                act.wait_ge(h232_sb, b + 1)
                copy(h2T[0][:, :], h32).then_inc(h2_hi, 1)

            def gelus(b, fs, banks):
                for f in fs:
                    if f >= 2:
                        act.wait_ge(g_lo, b * NF + f - 1)
                    act.wait_ge(ff1_mm, b * NF + f + 1)
                    act.activation(g32[f % 2], banks[f][:, :], ACT.Gelu).then_inc(gelu_sb, 1)

            def y2_copy(b, src):
                act.wait_ge(ff2_mm, b + 1)
                copy(colT, src[:, :]).then_inc(y2_sb, 1)

            def x3_copy(b, src):
                act.wait_ge(x3_mm, b + 1)
                copy(colT, src[:, :]).then_inc(x3T_sb, 1)

            def gate_exp(b):
                act.wait_ge(lg_st, 2 * (b + 1))
                act.activation(pe_[:, :, :], lg[:, :, :], ACT.Exp).then_inc(ex_sb, 1)

            def ot_high(g):
                act.wait_ge(ot_mm, g)
                copy(oT[0][:, :], bkC[:, :]).then_inc(ot_hi, 1)

            def q_exps(g):
                act.wait_ge(q_mm, g + 1)
                act.activation(e_q, bkA[:, :], ACT.Relu, scale=-1.0).then_inc(q_relu, 1)
                act.wait_ge(q_relu, g + 1)
                act.activation(e_q, e_q, ACT.Exp, scale=-1.0).then_inc(q_exp, 1)

            def k_exps(g):
                act.wait_ge(k_mm, g + 1)
                act.activation(e_k, bkB[:, :], ACT.Relu, scale=-1.0).then_inc(k_relu, 1)
                act.wait_ge(k_relu, g + 1)
                act.activation(e_k, e_k, ACT.Exp, scale=-1.0).then_inc(k_exp, 1)

            def v_copy(n, half, c):
                act.wait_ge(v_mm, n)
                copy(va[:, c, half * 8:(half + 1) * 8, 0:DH],
                     bkC[:, :].rearrange("p (h j) -> p h j", h=8)).then_inc(v_sb, 1)

            def step(b, par, p, first, last):
                g = b * PAIRS + p
                if not (first and p == 0):
                    ot_high(g)
                act.wait_ge(kt_mm, g + 1)
                copy(ktok, bkC[:, :].rearrange("p (c d) -> p c d", c=CH)).then_inc(kt_sb, 1)
                if not first:
                    if p == 0:
                        y_copy(b - 1)
                    if p == 6:
                        gate_exp(b - 1)
                nxt = not (last and p == PAIRS - 1)
                if nxt:
                    act.wait_ge(q_phi, g + 1)
                    q_exps(g + 1)
                if p == 1 and not last:
                    act.wait_ge(h32_sb, b + 2)
                    copy(hT[1 - par][0][:, :], h32).then_inc(h_hi, 1)
                if not first:
                    if p == 4:
                        y2_copy(b - 1, bkE)
                    if p == 5:
                        x3_copy(b - 1, bkE)
                if nxt:
                    act.wait_ge(k_phi, g + 1)
                    k_exps(g + 1)
                if p < CH:
                    v_copy(g + CH + 1, 1, p)
                elif not last:
                    v_copy(g + CH + 1, 0, p - CH)
                if last:
                    act.wait_ge(ld_stage[p % 2], 16 * (p // 2 + 2))
                    copy(w1[0][:, p * F:(p + 1) * F], stage[:, p % 2, :]).then_inc(w1hi, 1)
                if not first:
                    if p == 1:
                        h2_copy(b - 1)
                    if p == 2:
                        gelus(b - 1, (0, 1), {0: bkE, 1: bkF})
                    if p == 3:
                        gelus(b - 1, (2, 3), {2: bkE, 3: bkF})

            def sequence(b, par, first, last):
                for p in range(PAIRS):
                    step(b, par, p, first, last)

            act.wait_ge(ld_w, 64)
            for n, w in enumerate((wq, wk, wv, wo)):
                copy(w[0][:, :], v_aug[:, n * 1024:(n + 1) * 1024]).then_inc(whi, 1)
                if n == 1:
                    act.wait_ge(h32_sb, 1)
                    copy(hT[0][0][:, :], h32).then_inc(h_hi, 1)
            for n, w in enumerate((wf1, wf2)):
                act.wait_ge(ld_stage[n], 16)
                copy(w[0][:, :], stage[:, n, :]).then_inc(whi, 1)
            q_exps(0)
            k_exps(0)
            act.wait_ge(cst_dve, 1)
            for c in range(CH):
                v_copy(c + 1, 0, c)
            sequence(0, 0, True, False)
            with act.Fori(1, B - 2, 2) as b:
                sequence(b, 1, False, False)
                sequence(b + 1, 0, False, False)
            sequence(B - 1, 1, False, True)

            b = B - 1
            ot_high(B * PAIRS)
            y_copy(b)
            h2_copy(b)
            gelus(b, range(NF), {0: bkA, 1: bkB, 2: bkG, 3: bkH})
            y2_copy(b, bkC)
            x3_copy(b, bkA)
            gate_exp(b)

            X, M = bank[0:2], bank[4:6]
            HALF = F // 2

            def rows_hi(t, n, reuse):
                if reuse:
                    act.wait_ge(l1_mm, t - 1)
                act.wait_ge(xt_mm, t + 1)
                copy(xT[n % 2][0][:, :], X[n % 2][:, 0:P]).then_inc(xt_hi, 1)

            def hidden_relu(t, n, reuse):
                if reuse:
                    act.wait_ge(l2_mm, t - 1)
                act.wait_ge(ht_mm, t + 1)
                act.activation(hTe[n % 2][:, 0:F], M[n % 2][:, 0:F], ACT.Relu).then_inc(ht_a, 1)

            def weigh(t, n):
                act.wait_ge(yb_sb, t + 1)
                act.activation(yw[n], yb[n % 2], ACT.Copy, scale=xg[n][:, D + 1:D + 2]).then_inc(yw_sb, 1)

            def tile(t, n, first):
                rows_hi(t + 2, (n + 2) % RING, True)
                hidden_relu(t, n, not (first and n < 2))
                if not (first and n == 0):
                    weigh(t - 1, (n - 1) % RING)

            rows_hi(0, 0, False)
            rows_hi(1, 1, False)
            for n in range(RING):
                tile(n, n, True)
            with act.Fori(RING, TILES - RING + 1, RING) as t:
                for n in range(RING):
                    tile(t + n, n, False)
            weigh(TILES - 1, RING - 1)

            def group(i0, n, reuse):
                act.wait_ge(c_nb, i0 + n + 1)
                if reuse:
                    act.wait_ge(out_st[n], i0 * 8)
                for c in range(CH):
                    act.activation(oc[n][:, c, :], sc[n][:, c, :], ACT.Identity, bias=nmr[n][:, c:c + 1],
                                   scale=rs_c[n][:, c:c + 1]).then_inc(c_out, 1)

            for n in range(2):
                group(0, n, False)
            with act.Fori(2, B - 1, 2) as i:
                for n in range(2):
                    group(i, n, True)

        @block.vector
        def _(dve):
            def f32(ap):
                return ap.bitcast(F32)

            def low(out, whole, high):
                return dve.tensor_tensor(out, whole, f32(high), ALU.subtract)

            def ln_stats(k, src, i):
                for c in range(CH):
                    ins = dve.bn_stats(stats[k][:, c, :], src[:, c, :])
                ins.then_inc(ln_st[k], 1)
                apart(dve)
                dve.wait_ge(ln_st[k], i + 1)
                for c in range(CH):
                    ins = dve.bn_aggr(mv[k][:, c, :], stats[k][:, c, :])
                ins.then_inc(ln_mv[k], 1)

            def ln_apply(k, out, src, i):
                dve.wait_ge(ln_r[k], i + 1)
                for c in range(CH):
                    ins = dve.tensor_scalar(out(c), src[:, c, :], mv[k][:, c, 0:1], rstd[k][:, c:c + 1],
                                            ALU.subtract, ALU.mult)
                ins.then_inc(ln_x[k], 1)

            def bank_chunks(bk):
                return bk[:, :].rearrange("p (c d) -> p c d", c=CH)

            def front_stats(b):
                dve.wait_ge(ld_xln, 16 * (b + 1))
                ln_stats(0, xln, b)

            def front_apply(b):
                ln_apply(0, lambda c: xln[:, c, :], xln, b)

            def front_scale(b, reuse):
                dve.wait_ge(f1_mm, b + 1)
                if reuse:
                    dve.wait_ge(h_lo, b)
                dve.tensor_scalar(h32, bkE[:, :], cols[:, 0:1], cols[:, 1:2], ALU.mult, ALU.add).then_inc(h32_sb, 1)

            def front_low(b, par):
                dve.wait_ge(h_hi, b + 1)
                dve.wait_ge(h32_sb, b + 1)
                low(hT[par][1][:, :], h32, hT[par][0][:, :]).then_inc(h_lo, 1)

            def residual1(b, src):
                dve.wait_ge(yt_mm, b + 1)
                dve.wait_ge(ld_xres, 16 * (b + 1))
                dve.tensor_tensor(x1, bank_chunks(src), xres, ALU.add).then_inc(x1_sb, 1)
                dve.wait_ge(x1_sb, b + 1)
                dve.tensor_tensor(xx1, x1, xres, ALU.add).then_inc(xx_sb, 1)
                ln_stats(1, x1, b)

            def norm2(b):
                dve.wait_ge(xx_sb, b + 1)
                ln_apply(1, lambda c: x1[:, c, :], x1, b)

            def scale2(b, src, fronts):
                dve.wait_ge(h2_mm, b + 1)
                dve.wait_ge(h_lo, fronts)
                dve.tensor_scalar(h32, src[:, :], cols[:, 2:3], cols[:, 3:4], ALU.mult, ALU.add).then_inc(h232_sb, 1)

            def low2(b):
                dve.wait_ge(h2_hi, b + 1)
                dve.wait_ge(h232_sb, b + 1)
                low(h2T[1][:, :], h32, h2T[0][:, :]).then_inc(h2_lo, 1)

            def split_g(b, fs):
                for f in fs:
                    dve.wait_ge(gelu_sb, b * NF + f + 1)
                    dve.tensor_copy(gT[0][:, f, :], g32[f % 2]).then_inc(g_hi, 1)
                for f in fs:
                    dve.wait_ge(g_hi, b * NF + f + 1)
                    low(gT[1][:, f, :], g32[f % 2], gT[0][:, f, :]).then_inc(g_lo, 1)

            def residual2(b, src):
                dve.wait_ge(y2_mm, b + 1)
                dve.tensor_tensor(xx1, bank_chunks(src), xx1, ALU.add).then_inc(s3_sb, 1)
                dve.wait_ge(s3_sb, b + 1)
                ln_stats(2, xx1, b)

            def norm3(b):
                ln_apply(2, lambda c: routed[:, c, 0, 0:D], xx1, b)

            def logits(b, src):
                dve.wait_ge(gate_mm, b + 1)
                dve.tensor_tensor(lg[:, :, :], src[:, 0:CH * E].rearrange("p (c e) -> p c e", c=CH),
                                  gb[:, :].unsqueeze(1).broadcast_to([P, CH, E]), ALU.add
                                  ).then_inc(lg_sb, 1)
                dve.wait_ge(lg_sb, b + 1)
                dve.tensor_reduce(lmax[:, :], lg[:, :, :], AX.X, ALU.max).then_inc(lg_st, 1)
                dve.wait_ge(lg_st, 2 * b + 1)
                dve.tensor_tensor(lg[:, :, :], lg[:, :, :], lmax[:, :].unsqueeze(2).broadcast_to([P, CH, E]),
                                  ALU.subtract).then_inc(lg_st, 1)

            def top2(b):
                apart(dve)
                dve.wait_ge(ex_sb, b + 1)
                for c in range(CH):
                    ins = dve.max(top[:, c, :], pe_[:, c, :])
                ins.then_inc(tp, 1)
                apart(dve)
                dve.wait_ge(tp, TP_STEPS * b + 1)
                for c in range(CH):
                    ins = dve.max_index(topi[:, c, :], top[:, c, :], pe_[:, c, :])
                dve.tensor_tensor(wsum[:, :], top[:, :, 0], top[:, :, 1], ALU.add).then_inc(tp, 1)
                dve.wait_ge(tp, TP_STEPS * b + 2)
                dve.reciprocal(wsum[:, :], wsum[:, :])
                for k in range(2):
                    ins = dve.tensor_tensor(onehot[:, k, :, :],
                                            topi[:, :, k:k + 1].broadcast_to([P, CH, E]),
                                            iota_e[:, :].unsqueeze(1).broadcast_to([P, CH, E]), ALU.is_equal)
                ins.then_inc(tp, 1)
                dve.wait_ge(tp, TP_STEPS * b + 3)
                dve.tensor_tensor(routed[:, :, :, D + 1], top[:, :, 0:2],
                                  wsum[:, :].unsqueeze(2).broadcast_to([P, CH, 2]), ALU.mult)
                dve.tensor_tensor(chosen[:, :, :], onehot[:, 0, :, :], onehot[:, 1, :, :], ALU.add).then_inc(tp, 1)

            def place(b, src):
                dve.wait_ge(rank_mm, b + 1)
                n = [b * RK_STEPS]

                def then(ins):
                    n[0] = n[0] + 1
                    ins.then_inc(rk, 1)
                    dve.wait_ge(rk, n[0])

                tot = src[:, CH * E:2 * CH * E].rearrange("p (c e) -> p c e", c=CH)
                then(dve.tensor_copy(base[:, 0, :], base[:, CH, :]))
                for c in range(CH):
                    then(dve.tensor_tensor(base[:, c + 1, :], tot[:, c, :], base[:, c, :], ALU.add))
                then(dve.tensor_tensor(rank[:, :, :], src[:, 0:CH * E].rearrange("p (c e) -> p c e", c=CH),
                                       base[:, 0:CH, :], ALU.add))
                for k in range(2):
                    then(dve.tensor_tensor(prod[:, k, :, :], rank[:, :, :], onehot[:, k, :, :], ALU.mult))
                then(dve.tensor_copy(routed[:, :, :, D].bitcast(U32), dest[:, :, :]))
                then(dve.tensor_scalar(dest[:, :, :], dest[:, :, :], float(2 * T), None, ALU.add))
                then(dve.tensor_reduce(slot_f[:, :, :], prod[:, :, :, :], AX.X, ALU.add))
                dve.tensor_copy(slot[:, :, :], slot_f[:, :, :]).then_inc(rt_sb, 1)

            def phi(out, pre, e):
                return dve.scalar_tensor_tensor(out=out, in0=pre[:, :], scalar=0.0, in1=e, op0=ALU.max, op1=ALU.add)

            def q_phis(g, gp):
                dve.wait_ge(q_exp, g + 1)
                phi(qT[gp], bkA, e_q).then_inc(q_phi, 1)

            def k_phis(g, gp):
                dve.wait_ge(k_exp, g + 1)
                phi(kT[gp], bkB, e_k).then_inc(k_phi, 1)

            def ot_low(g):
                dve.wait_ge(ot_hi, g)
                low(oT[1][:, :], bkC[:, :], oT[0][:, :]).then_inc(ot_lo, 1)

            def normalise(g, bk, half):
                dve.wait_ge(o_mm, 2 * g + half + 1)
                o4 = bk[:, 0:4 * DV1].rearrange("p (x j) -> p x j", x=4)
                i = 4 * g + 2 * half
                dve.tensor_scalar(den[:, :], o4[:, :, DH], EPS_DEN, None, ALU.max).then_inc(o_den, 1)
                dve.wait_ge(o_den, i + 1)
                dve.reciprocal(rden[:, :], den[:, :]).then_inc(o_den, 1)
                dve.wait_ge(o_den, i + 2)
                dve.tensor_tensor(on[:, 2 * half:2 * half + 2, :].rearrange("p c (h j) -> p (c h) j", h=2),
                                  o4[:, :, 0:DH], rden[:, :].unsqueeze(2).broadcast_to([P, 4, DH]),
                                  ALU.mult).then_inc(o_sb, 1)

            def states(g):
                dve.wait_ge(u_mm, g + 1)
                for c in range(CH - 1):
                    for h in range(2):
                        hs, js = slice(h * DH, (h + 1) * DH), slice(h * DV1, (h + 1) * DV1)
                        u = bkH[hs, 260 + c * DV1:260 + (c + 1) * DV1]
                        if c == 0:
                            ins = dve.tensor_copy(state[hs, 0, js], u)
                        else:
                            ins = dve.tensor_tensor(state[hs, c, js], u, state[hs, c - 1, js], ALU.add)
                    if c < CH - 2:
                        ins.then_inc(s_part, 1)
                        dve.wait_ge(s_part, 2 * g + c + 1)
                ins.then_inc(s_sb, 1)

            def step(b, par, p, first, last):
                g = b * PAIRS + p
                if not (first and p == 0):
                    ot_low(g)
                for h in range(2):
                    dve.wait_ge(sc_mm, 2 * g + h + 1)
                    dve.tensor_tensor(am[h], bank_chunks((bkE, bkF)[h]),
                                      causal[:, :].unsqueeze(1).broadcast_to([P, CH, P]), ALU.mult).then_inc(a_msk, 1)
                if p == 0 and not last:
                    front_stats(b + 1)
                if not first:
                    if p == 1:
                        norm2(b - 1)
                    if p == 2:
                        low2(b - 1)
                    if p == 3:
                        split_g(b - 1, (0, 1))
                    if p == 4:
                        split_g(b - 1, (2, 3))
                    if p == 5:
                        norm3(b - 1)
                states(g)
                if p == 1 and not last:
                    front_scale(b + 1, True)
                if not first and p == 6:
                    top2(b - 1)
                normalise(g, bkG, 0)
                nxt = not (last and p == PAIRS - 1)
                if nxt:
                    q_phis(g + 1, (p + 1) % 2)
                normalise(g, bkH, 1)
                if nxt:
                    k_phis(g + 1, (p + 1) % 2)
                if p == 0 and not last:
                    front_apply(b + 1)
                if p == 1 and not last:
                    front_low(b + 1, 1 - par)
                if last:
                    dve.wait_ge(w1hi, p + 1)
                    low(w1[1][:, p * F:(p + 1) * F], stage[:, p % 2, :], w1[0][:, p * F:(p + 1) * F]).then_inc(w1lo, 1)
                if not first:
                    if p == 0:
                        residual1(b - 1, bkF)
                    if p == 1:
                        scale2(b - 1, bkF, B if last else b + 2)
                    if p == 4:
                        residual2(b - 1, bkF)
                    if p == 5:
                        logits(b - 1, bkF)
                    if p == 6:
                        place(b - 1, bkF)

            def sequence(b, par, first, last):
                for p in range(PAIRS):
                    step(b, par, p, first, last)

            dve.memset(state[:, :, :], 0.0)
            dve.memset(neg_half[:, :], -0.5).then_inc(nh_set, 1)
            front_stats(0)
            front_apply(0)
            dve.wait_ge(ld_small, 16 * 6)
            front_scale(0, False)
            for n, w in enumerate((wq, wk)):
                dve.wait_ge(whi, n + 1)
                low(w[1][:, :], v_aug[:, n * 1024:(n + 1) * 1024], w[0][:, :]).then_inc(wlo, 1)
            front_low(0, 0)
            for n, w in ((2, wv), (3, wo)):
                dve.wait_ge(whi, n + 1)
                low(w[1][:, :], v_aug[:, n * 1024:(n + 1) * 1024], w[0][:, :]).then_inc(wlo, 1)
            dve.wait_ge(wlo, 4)
            dve.memset(va[:, :, :, DH:DV1], 1.0).then_inc(cst_dve, 1)
            for n, w in enumerate((wf1, wf2)):
                dve.wait_ge(whi, n + 5)
                low(w[1][:, :], stage[:, n, :], w[0][:, :]).then_inc(wlo, 1)
            q_phis(0, 0)
            k_phis(0, 0)
            dve.wait_ge(cst, CST_ALL)
            dve.tensor_scalar(base[:, CH, :], iota_e[:, :], float(REGION), None, ALU.mult)
            dve.tensor_copy(pads[:, :, D].bitcast(U32), padf[:, E:2 * E]).then_inc(pads_dmy, 1)
            dve.wait_ge(dmy_st, 32)
            sequence(0, 0, True, False)
            with dve.Fori(1, B - 2, 2) as b:
                sequence(b, 1, False, False)
                sequence(b + 1, 0, False, False)
            sequence(B - 1, 1, False, True)

            b = B - 1
            ot_low(B * PAIRS)
            residual1(b, bkF)
            norm2(b)
            scale2(b, bkE, B)
            low2(b)
            split_g(b, (0, 1))
            split_g(b, (2, 3))
            residual2(b, bkY)
            norm3(b)
            logits(b, bkB)
            top2(b)
            place(b, bkG)

            n = [0]

            def then(ins):
                n[0] += 1
                ins.then_inc(plan, 1)
                dve.wait_ge(plan, n[0])

            EB = [P, TILES + AHEAD, E]
            then(dve.scalar_tensor_tensor(out=cnt[:, :], in0=iota_e[:, :], scalar=-float(REGION), in1=base[:, CH, :],
                                          op0=ALU.mult, op1=ALU.add))
            then(dve.tensor_tensor(gt32[:, :, :], cnt[:, :].unsqueeze(2).broadcast_to([P, E, 32]),
                                   m32[:, :].unsqueeze(1).broadcast_to([P, E, 32]), ALU.is_gt))
            then(dve.tensor_reduce(nt[:, :], gt32[:, :, :], AX.X, ALU.add))
            then(dve.tensor_tensor_scan(ntc[:, :], one_e[:, :], nt[:, :], 0.0, ALU.mult, ALU.add))
            then(dve.tensor_tensor(le[:, :, :], ntc[:, :].unsqueeze(1).broadcast_to(EB),
                                   tidx[:, :].unsqueeze(2).broadcast_to(EB), ALU.is_le))
            then(dve.tensor_reduce(en[:, :], le[:, :, :], AX.X, ALU.add))
            then(dve.tensor_tensor(le[:, :, :], le[:, :, :], nt[:, :].unsqueeze(1).broadcast_to(EB), ALU.mult))
            then(dve.tensor_reduce(cx[:, :], le[:, :, :], AX.X, ALU.add))
            then(dve.tensor_tensor(cx[:, :], tidx[:, :], cx[:, :], ALU.subtract))
            then(dve.tensor_scalar(cx[:, :], cx[:, :], float(P), None, ALU.mult))
            dve.scalar_tensor_tensor(out=tile_r[:, :], in0=en[:, :], scalar=float(REGION), in1=cx[:, :],
                                     op0=ALU.mult, op1=ALU.add)
            then(dve.memset(pads[:, :, :], 0.0))
            then(dve.tensor_copy(pads[:, :, D].bitcast(U32), padf[:, 0:E]))
            then(dve.tensor_scalar(padi[:, :], base[:, CH, :], pcol[:, 0:1], None, ALU.add))
            then(dve.tensor_scalar(tile_e[:, :], en[:, :], float(E - 1), None, ALU.min))

            X, L, M, Y = bank[0:2], bank[2:4], bank[4:6], bank[6:8]

            def expert(t):
                return dve.value_load(tile_e[0:1, bass.ds(t, 1)], min_val=0, max_val=E - 1)

            def rows_lo(t, k):
                dve.wait_ge(xt_hi, t + 1)
                low(xT[k % 2][1][:, :], X[k % 2][:, 0:P], xT[k % 2][0][:, :]).then_inc(xt_lo, 1)

            def bias1(t, k, e, reuse):
                if reuse:
                    dve.wait_ge(ht_mm, t - 1)
                dve.wait_ge(l1_mm, t + 1)
                dve.tensor_tensor(hb[k % 2], L[k % 2][:, :], b1_rows[:, bass.ds(e * F, F)], ALU.add).then_inc(hb_sb, 1)

            def bias2(t, k, e, reuse):
                if reuse:
                    dve.wait_ge(yw_sb, t - 1)
                dve.wait_ge(l2_mm, t + 1)
                dve.tensor_tensor(yb[k % 2], Y[k % 2][:, 0:D], b2_rows[:, bass.ds(e * D, D)], ALU.add
                                  ).then_inc(yb_sb, 1)

            def round_(t0, first):
                e = {} if first else {-1: expert(t0 - 1)}
                e[0] = expert(t0)
                for k in range(RING):
                    e[k + 1] = expert(t0 + k + 1)
                    rows_lo(t0 + k + 2, k)
                    bias1(t0 + k + 1, k + 1, e[k + 1], not (first and k == 0))
                    if not (first and k == 0):
                        bias2(t0 + k - 1, k - 1, e[k - 1], not (first and k <= 2))

            dve.wait_ge(ld_b1, 16)
            dve.wait_ge(ld_b2, 16)
            rows_lo(0, 0)
            rows_lo(1, 1)
            bias1(0, 0, expert(0), False)
            round_(0, True)
            with dve.Fori(RING, TILES - RING + 1, RING) as t:
                round_(t, False)
            bias2(TILES - 1, RING - 1, expert(TILES - 1), True)

            def group(i, k, reuse):
                if reuse:
                    dve.wait_ge(c_out, (i - 1) * CH)
                dve.wait_ge(z_sum, i + 1)
                x3_of = chunks(x3_all[:, bass.ds(i * T, T)])
                dve.tensor_tensor(sc[k], x3_of, zs[k], ALU.add).then_inc(c_sb, 1)
                dve.wait_ge(c_sb, i + 1)
                for c in range(CH):
                    ins = dve.bn_stats(stats[k][:, c, :], sc[k][:, c, :])
                ins.then_inc(c_st, 1)
                apart(dve)
                dve.wait_ge(c_st, i + 1)
                for c in range(CH):
                    ins = dve.bn_aggr(mv[k][:, c, :], stats[k][:, c, :])
                ins.then_inc(c_mv, 1)

            def bias_of(i, k):
                dve.wait_ge(c_r, i + 1)
                dve.scalar_tensor_tensor(out=nmr[k][:, :], in0=mv[k][:, :, 0], scalar=-1.0, in1=rs_c[k][:, :], op0=ALU.mult,
                                         op1=ALU.mult).then_inc(c_nb, 1)

            dve.wait_ge(ld_x3, 16)
            group(0, 0, False)
            group(1, 1, False)
            bias_of(0, 0)
            bias_of(1, 1)
            with dve.Fori(2, B - 1, 2) as i:
                for k in range(2):
                    group(i + k, k, True)
                for k in range(2):
                    bias_of(i + k, k)

        @block.gpsimd
        def _(pool):
            def count(v):
                return v if isinstance(v, int) else pool.snap(pool.to_reg(v))

            def rstds(k, i):
                nth = count(i + 1)
                apart(pool)
                pool.wait_ge(ln_mv[k], nth)
                pool.tensor_scalar(ve[k][:, :], mv[k][:, :, 1], EPS_LN, 1.0, ALU.add, ALU.mult).then_inc(ln_ve[k], 1)
                apart(pool)
                pool.wait_ge(ln_ve[k], nth)
                pool.tensor_tensor(rstd[k][:, :], ve[k][:, :], neg_half[:, :], ALU.pow).then_inc(ln_r[k], 1)

            def scatter(b):
                nth, stored = count(b + 1), count(16 * (b + 1))
                apart(pool)
                pool.wait_ge(ln_x[2], nth)
                pool.tensor_copy(routed[:, :, 1, 0:D], routed[:, :, 0, 0:D]).then_inc(dup_sb, 1)
                apart(pool)
                pool.wait_ge(rt_sb, nth)
                pool.wait_ge(dup_sb, nth)
                pool.wait_ge(x3_st, stored)
                for c in range(CH):
                    for k in range(2):
                        pool.indirect_dma_start(rows_d, bass.IndirectOffsetOnAxis(slot[:, k, c:c + 1], 0),
                                                routed[:, c, k, :], None).then_inc(sct, 16)
                pool.wait_ge(sct, count(2 * CH * 16 * (b + 1)))

            pool.wait_ge(nh_set, 1)
            rstds(0, 0)

            n = [0]

            def then(ins, wait=True):
                n[0] += 1
                ins.then_inc(cst, 1)
                if wait:
                    pool.wait_ge(cst, n[0])

            then(pool.memset(ident[:, :], 0.0))
            then(pool.affine_select(out=ident[:, :], in_=ident[:, :], compare_op=ALU.not_equal, fill=1.0, base=0,
                                    pattern=[[-1, P]], channel_multiplier=1), False)
            then(pool.memset(causal[:, :], 1.0))
            then(pool.affine_select(out=causal[:, :], in_=causal[:, :], compare_op=ALU.is_ge, fill=0.0, base=0,
                                    pattern=[[1, P]], channel_multiplier=-1), False)
            then(pool.memset(ones_b[:, :], 1.0))
            then(pool.affine_select(out=before[:, :], in_=ones_b[:, :], compare_op=ALU.is_gt, fill=0.0, base=0,
                                    pattern=[[1, P]], channel_multiplier=-1), False)
            fl = dict(allow_small_or_imprecise_dtypes=True)
            then(pool.iota(iota_e[:, :], [[1, E]], base=0, channel_multiplier=0, **fl), False)
            then(pool.iota(dest[:, :, :], [[2 * P, CH], [1, 2]], base=0, channel_multiplier=2, **fl), False)
            then(pool.iota(m32[:, :], [[P, 32]], base=0, channel_multiplier=0, **fl), False)
            then(pool.iota(tidx[:, :], [[1, TILES + AHEAD]], base=0, channel_multiplier=0, **fl), False)
            then(pool.iota(pcol[:, :], [[0, 1]], base=0, channel_multiplier=1, **fl), False)
            then(pool.iota(padf[:, :], [[P, 2 * E]], base=PAD_DEST, channel_multiplier=1, **fl), False)
            then(pool.memset(one_e[:, :], 1.0), False)
            then(pool.memset(routed[:, :, :, D + 2:ROW], 0.0), False)
            then(pool.memset(pads[:, :, :], 0.0), False)
            pool.wait_ge(cst, n[0])
            assert n[0] == CST_ALL

            def sequence(b, first, last):
                if not last:
                    rstds(0, b + 1)
                if not first:
                    rstds(1, b - 1)
                    rstds(2, b - 1)
                    scatter(b - 1)

            sequence(0, True, False)
            with pool.Fori(1, B - 1) as b:
                sequence(b, False, False)
            sequence(B - 1, False, True)
            rstds(1, B - 1)
            rstds(2, B - 1)
            scatter(B - 1)

            def store(t, k):
                nth = count(t + 1)
                apart(pool)
                pool.wait_ge(yw_sb, nth)
                pool.indirect_dma_start(res_d, bass.IndirectOffsetOnAxis(xg[k][:, D:D + 1].bitcast(U32), 0),
                                        yw[k], None).then_inc(res_st[k], 16)

            with pool.Fori(0, TILES - RING + 1, RING) as t:
                for k in range(RING):
                    store(t + k, k)

            def group(i0, k, reuse):
                i = i0 + k
                pool.wait_ge(ld_z[k], i0 * 8 + 16)
                if reuse:
                    pool.wait_ge(c_sb, i - 1)
                pool.tensor_tensor(zs[k], z[k][:, :, 0, :], z[k][:, :, 1, :], ALU.add).then_inc(z_sum, 1)

            def rs(i, k):
                nth = count(i + 1)
                apart(pool)
                pool.wait_ge(c_mv, nth)
                pool.tensor_scalar(ve[k][:, :], mv[k][:, :, 1], EPS_LN, 1.0, ALU.add, ALU.mult).then_inc(c_ve, 1)
                pool.wait_ge(c_ve, nth)
                pool.tensor_tensor(rs_c[k][:, :], ve[k][:, :], neg_half[:, :], ALU.pow).then_inc(c_r, 1)

            for k in range(2):
                group(0, k, False)
            for k in range(2):
                rs(k, k)
            with pool.Fori(2, B - 1, 2) as i:
                for k in range(2):
                    group(i, k, True)
                for k in range(2):
                    rs(i + k, k)


_INS = ["L0_attn_x", "L0_attn_ln1_g", "L0_attn_ln1_b", "L0_attn_Wq", "L0_attn_Wk", "L0_attn_Wv", "L0_attn_Wo",
        "L0_attn_ln2_g", "L0_attn_ln2_b", "L0_attn_Wf1", "L0_attn_Wf2", "L0_ffn_gate_w", "L0_ffn_gate_b",
        "L0_ffn_w1", "L0_ffn_b1", "L0_ffn_w2", "L0_ffn_b2"]


def kernel(**inputs):
    import numpy as np
    import concourse.bacc as bacc
    from concourse.bass_utils import run_bass_kernel_spmd

    nc = bacc.Bacc("TRN2", target_bir_lowering=False, num_devices=1)
    arrays, args = {}, []
    for name in _INS:
        a = np.ascontiguousarray(inputs[name])
        arrays[f"in_{name}"] = a
        args.append(nc.dram_tensor(f"in_{name}", a.shape, mybir.dt.from_np(a.dtype), kind="ExternalInput").ap())
    args.append(nc.dram_tensor("out", (B, T, D), F32, kind="ExternalOutput").ap())
    build(nc, *args)
    r = run_bass_kernel_spmd(nc, [arrays], core_ids=[0])
    return r.results[0]["out"]
```

```python
from contextlib import ExitStack

import concourse.bass as bass
from concourse import mybir

F32 = mybir.dt.float32
F32R = mybir.dt.float32r
BF16 = mybir.dt.bfloat16
U32 = mybir.dt.uint32
I32 = mybir.dt.int32
ALU = mybir.AluOpType
ACT = mybir.ActivationFunctionType
AX = mybir.AxisListType

P = 128
B, T, D = 8, 512, 128
CH = T // P
H, DH = 16, 64
PAIRS = H // 2
DV1 = DH + 1
NF = 4
F = NF * P
E = 8
TOKENS = B * T
EPS_LN = 1e-5
EPS_DEN = 1e-6

REGION = TOKENS + P
DUMMY = 10
ROW = 132
TILES = 72
RING = 8
AHEAD = 2
PAIR_ROWS = 2 * TOKENS
PAD_DEST = PAIR_ROWS
DUMMY_DEST = PAD_DEST + E * P
ZBUF = 4
WORK = 19
RESULTS = DUMMY_DEST + E * P


def build(nc, x_d, ln1_g, ln1_b, wq_d, wk_d, wv_d, wo_d, ln2_g, ln2_b, wf1_d, wf2_d,
          gate_w, gate_b, w1_d, b1_d, w2_d, b2_d, out_d):
    rows_d = nc.dram_tensor("routed_rows", (E * REGION + DUMMY * P, ROW), F32, kind="Internal").ap()
    res_d = nc.dram_tensor("expert_results", (RESULTS, D), F32, kind="Internal").ap()
    x3_d = nc.dram_tensor("moe_input", (TOKENS, D), F32, kind="Internal").ap()

    with ExitStack() as ctx:
        def sb(name, shape, dt=F32):
            return ctx.enter_context(nc.sbuf_tensor(name, shape, dt))

        def sem(name):
            return ctx.enter_context(nc.semaphore(name))

        wq = [sb(f"wq_{k}", [P, H * DH], F32R) for k in ("hi", "lo")]
        wk = [sb(f"wk_{k}", [P, H * DH], F32R) for k in ("hi", "lo")]
        wv = [sb(f"wv_{k}", [P, H * DH], F32R) for k in ("hi", "lo")]
        wo = [sb(f"wo_{k}", [P, PAIRS * D], F32R) for k in ("hi", "lo")]
        wf1 = [sb(f"wf1_{k}", [P, F], F32R) for k in ("hi", "lo")]
        wf2 = [sb(f"wf2_{k}", [P, F], F32R) for k in ("hi", "lo")]
        w1 = [sb(f"w1_{k}", [P, E * F], F32R) for k in ("hi", "lo")]
        w2 = sb("w2", [P, E * F])
        b1_rows = sb("b1_rows", [P, E * F])
        stage = sb("stage", [P, 2, F])
        b2_rows = stage[:, :, :].rearrange("p a f -> p (a f)")
        ident = sb("ident", [P, P])
        causal = sb("causal", [P, P])
        before = sb("before", [P, P], BF16)
        ones_b = sb("ones_b", [P, P], BF16)
        cols = sb("cols", [P, 4])
        neg_half = sb("neg_half", [P, CH])
        iota_e = sb("iota_e", [P, E])
        gw = sb("gw", [P, E])
        gb = sb("gb", [P, E])
        v_aug = sb("v_aug", [P, CH * H * DV1])
        va = v_aug[:, :].rearrange("p (c h j) -> p c h j", c=CH, h=H)
        hT = [[sb(f"hT{n}_{k}", [P, T], F32R) for k in ("hi", "lo")] for n in range(2)]
        h2T = [sb(f"h2T_{k}", [P, T], F32R) for k in ("hi", "lo")]
        gT = [sb(f"gT_{k}", [P, NF, T], F32R) for k in ("hi", "lo")]
        oT = [sb(f"oT_{k}", [P, T], F32R) for k in ("hi", "lo")]
        state = sb("state", [P, CH - 1, 2 * DV1])
        routed = sb("routed", [P, CH, 2, ROW])
        work = sb("work", [P, WORK * T])
        spot = [0]

        def take(n, back=None):
            if back is not None:
                spot[0] = back
            a = spot[0]
            spot[0] += n
            return work[:, a:a + n]

        def chunks(ap):
            return ap.rearrange("p (c d) -> p c d", c=CH)

        qT = [take(T) for _ in range(2)]
        kT = [take(T) for _ in range(2)]
        ktok = chunks(take(T))
        am = [chunks(take(T)) for _ in range(2)]
        on = chunks(take(T))
        e_q, e_k = take(T), take(T)
        xln = chunks(take(T))
        xres = chunks(take(T))
        h32 = take(T)
        g32 = [take(T) for _ in range(2)]
        behind = spot[0]
        x1 = chunks(take(T))
        xx1 = chunks(take(T))
        colT = take(T)
        pads = take(E * ROW, behind).rearrange("p (e w) -> p e w", e=E)
        gt32 = take(E * 32, 0).rearrange("p (e m) -> p e m", e=E)
        le = take((TILES + AHEAD) * E).rearrange("p (t e) -> p t e", e=E)
        xg = [take(ROW, 0 if n == 0 else None) for n in range(RING)]
        hb = [take(F) for _ in range(2)]
        hTe = [take(F) for _ in range(2)]
        yb = [take(D) for _ in range(2)]
        yw = [take(D) for _ in range(RING)]
        x3_all = take(B * T)
        xc = x3_all.rearrange("p (b c d) -> p b c d", b=B, c=CH)
        zs = [chunks(take(T)) for _ in range(2)]
        assert spot[0] <= WORK * T
        z = [v_aug[:, n * 2 * T:(n + 1) * 2 * T].rearrange("p (c k d) -> p c k d", c=CH, k=2) for n in range(ZBUF)]
        sc = [chunks(take(T, 0 if n == 0 else None)) for n in range(2)]
        oc = [chunks(take(T)) for _ in range(2)]
        xT = [[sb(f"xT{n}_{k}", [P, P], F32R) for k in ("hi", "lo")] for n in range(2)]
        stats = [sb(f"stats{n}", [P, CH, 6]) for n in range(3)]
        mv = [sb(f"mv{n}", [P, CH, 2]) for n in range(3)]
        ve = [sb(f"ve{n}", [P, CH]) for n in range(3)]
        rstd = [sb(f"rstd{n}", [P, CH]) for n in range(3)]
        den = sb("den", [P, 4])
        rden = sb("rden", [P, 4])
        lg = sb("lg", [P, CH, E])
        lmax = sb("lmax", [P, CH])
        pe_ = sb("gate_exp", [P, CH, E])
        top = sb("top", [P, CH, 8])
        topi = sb("topi", [P, CH, 8], U32)
        wsum = sb("wsum", [P, CH])
        onehot = sb("onehot", [P, 2, CH, E])
        chosen = sb("chosen", [P, CH, E], BF16)
        base = sb("base", [P, E])
        rank = sb("rank", [P, CH, E])
        prod = sb("prod", [P, 2, CH, E])
        slot_f = sb("slot_f", [P, 2, CH])
        slot = sb("slot", [P, 2, CH], U32)
        dest = sb("dest", [P, CH, 2])
        cnt = sb("cnt", [P, E])
        nt = sb("nt", [P, E])
        ntc = sb("ntc", [P, E])
        one_e = sb("one_e", [P, E])
        m32 = sb("m32", [P, 32])
        tidx = sb("tidx", [P, TILES + AHEAD])
        en = sb("en", [P, TILES + AHEAD])
        cx = sb("cx", [P, TILES + AHEAD])
        tile_e = sb("tile_e", [P, TILES + AHEAD], I32)
        tile_r = sb("tile_r", [P, TILES + AHEAD], I32)
        padi = sb("padi", [P, E], U32)
        pcol = sb("pcol", [P, 1])
        padf = sb("padf", [P, 2 * E])
        rs_c = [sb(f"rs_c{n}", [P, CH]) for n in range(2)]
        nmr = [sb(f"nmr{n}", [P, CH]) for n in range(2)]

        bank = [ctx.enter_context(nc.psum_tensor(f"bank{n}", [P, 512], F32)) for n in range(8)]
        bkA, bkB, bkC, bkE, bkF, bkG, bkH, bkY = bank

        ld_stage = [sem(f"ld_stage{n}") for n in range(2)]
        ld_w, ld_small, ld_b1, ld_w2, ld_b2 = (sem(n) for n in ("ld_w", "ld_small", "ld_b1", "ld_w2", "ld_b2"))
        ld_xln, ld_xres = sem("ld_xln"), sem("ld_xres")
        cst, cst_dve, whi, wlo, w1hi, w1lo = (sem(n) for n in ("cst", "cst_dve", "whi", "wlo", "w1hi", "w1lo"))
        q_mm, k_mm, v_mm, sc_mm, kt_mm, u_mm, o_mm, ot_mm, wo_mm = (
            sem(n) for n in ("q_mm", "k_mm", "v_mm", "sc_mm", "kt_mm", "u_mm", "o_mm", "ot_mm", "wo_mm"))
        q_relu, q_exp, k_relu, k_exp, v_sb, kt_sb, ot_hi, yT_sb = (
            sem(n) for n in ("q_relu", "q_exp", "k_relu", "k_exp", "v_sb", "kt_sb", "ot_hi", "yT_sb"))
        q_phi, k_phi, a_msk, s_part, s_sb, o_den, o_sb, ot_lo = (
            sem(n) for n in ("q_phi", "k_phi", "a_msk", "s_part", "s_sb", "o_den", "o_sb", "ot_lo"))
        ln_st, ln_mv, ln_ve, ln_r, ln_x = ([sem(f"{a}{n}") for n in range(3)]
                                           for a in ("ln_st", "ln_mv", "ln_ve", "ln_r", "ln_x"))
        f1_mm, yt_mm, h2_mm, ff1_mm, ff2_mm, y2_mm, x3_mm, gate_mm, rank_mm = (
            sem(n) for n in ("f1_mm", "yt_mm", "h2_mm", "ff1_mm", "ff2_mm", "y2_mm", "x3_mm", "gate_mm", "rank_mm"))
        h32_sb, h_hi, h_lo, x1_sb, xx_sb, h232_sb, h2_hi, h2_lo, gelu_sb, g_hi, g_lo = (
            sem(n) for n in ("h32_sb", "h_hi", "h_lo", "x1_sb", "xx_sb", "h232_sb", "h2_hi", "h2_lo", "gelu_sb",
                             "g_hi", "g_lo"))
        y2_sb, s3_sb, x3T_sb, lg_sb, lg_st, ex_sb, tp, rk, cnt_sb, rt_sb, dup_sb, x3_st, sct = (
            sem(n) for n in ("y2_sb", "s3_sb", "x3T_sb", "lg_sb", "lg_st", "ex_sb", "tp", "rk", "cnt_sb", "rt_sb", "dup_sb",
                             "x3_st", "sct"))
        plan, nh_set, pads_dmy, dmy_st, pad_st = (sem(n) for n in ("plan", "nh_set", "pads_dmy", "dmy_st", "pad_st"))
        ld_xg = [sem(f"ld_xg{n}") for n in range(RING)]
        res_st = [sem(f"res_st{n}") for n in range(RING)]
        xt_mm, l1_mm, ht_mm, l2_mm, xt_hi, xt_lo, hb_sb, ht_a, ht_v, yb_sb, yw_sb = (
            sem(n) for n in ("xt_mm", "l1_mm", "ht_mm", "l2_mm", "xt_hi", "xt_lo", "hb_sb", "ht_a", "ht_v", "yb_sb",
                             "yw_sb"))
        ld_x3 = sem("ld_x3")
        ld_z = [sem(f"ld_z{n}") for n in range(ZBUF)]
        z_sum, c_sb, c_st, c_mv, c_ve, c_r, c_nb, c_out = (
            sem(n) for n in ("z_sum", "c_sb", "c_st", "c_mv", "c_ve", "c_r", "c_nb", "c_out"))
        out_st = [sem(f"out_st{n}") for n in range(2)]

        def x_of(b):
            return x_d[bass.ds(b, 1), :, :].rearrange("o (c p) d -> p (o c) d", p=P)

        CST_ALL = 15
        PLAN_DONE = 14
        TP_STEPS = 4
        RK_STEPS = 5

        def apart(eng):
            eng.wait_ge(nh_set, 1)

        block = ctx.enter_context(nc.Block())

        @block.sync
        def _(sp):
            sp.dma_start(xln, x_of(0)).then_inc(ld_xln, 16)
            sp.dma_start(cols[:, 0:1], ln1_g.rearrange("(p o) -> p o", o=1)).then_inc(ld_small, 16)
            sp.dma_start(cols[:, 1:2], ln1_b.rearrange("(p o) -> p o", o=1)).then_inc(ld_small, 16)
            sp.dma_start(v_aug[:, 0:1024], wq_d).then_inc(ld_w, 16)
            sp.dma_start(v_aug[:, 1024:2048], wk_d).then_inc(ld_w, 16)
            sp.dma_start(v_aug[:, 2048:3072], wv_d).then_inc(ld_w, 16)
            sp.dma_start(v_aug[:, 3072:4096].rearrange("p (t n) -> p t n", t=PAIRS),
                         wo_d.rearrange("(t p) n -> p t n", p=P)).then_inc(ld_w, 16)
            sp.dma_start(stage[:, 0, :], wf1_d).then_inc(ld_stage[0], 16)
            sp.dma_start(stage[:, 1, :].rearrange("p (t n) -> p t n", t=NF),
                         wf2_d.rearrange("(t p) n -> p t n", p=P)).then_inc(ld_stage[1], 16)
            sp.dma_start(cols[:, 2:3], ln2_g.rearrange("(p o) -> p o", o=1)).then_inc(ld_small, 16)
            sp.dma_start(cols[:, 3:4], ln2_b.rearrange("(p o) -> p o", o=1)).then_inc(ld_small, 16)
            sp.dma_start(gw[:], gate_w).then_inc(ld_small, 16)
            sp.dma_start(gb[:], gate_b.partition_broadcast(P)).then_inc(ld_small, 16)
            sp.wait_ge(wlo, 6)
            for e in range(2):
                sp.dma_start(stage[:, e, :], w1_d[e]).then_inc(ld_stage[e], 16)
            sp.dma_start(w2[:, :].rearrange("p (e t n) -> p e t n", e=E, t=NF),
                         w2_d.rearrange("e (t p) n -> p e t n", p=P)).then_inc(ld_w2, 16)
            sp.dma_start(b1_rows[:, :], b1_d.rearrange("e f -> (e f)").partition_broadcast(P)).then_inc(ld_b1, 16)
            sp.wait_ge(pads_dmy, 1)
            for block0, n in ((0, E), (E, DUMMY - E)):
                at = E * REGION + block0 * P
                sp.dma_start(rows_d[at:at + n * P, :].rearrange("(e p) w -> p e w", p=P),
                             pads[:, 0:n, :]).then_inc(dmy_st, 16)

            def sequence(b, first, last):
                if not last:
                    sp.wait_ge(f1_mm, b + 1)
                    sp.dma_start(xln, x_of(b + 1)).then_inc(ld_xln, 16)
                if not first:
                    sp.wait_ge(xx_sb, b)
                sp.dma_start(xres, x_of(b)).then_inc(ld_xres, 16)
                if not first and not last:
                    store_x3(b - 1)

            def store_x3(b):
                sp.wait_ge(ln_x[2], b + 1)
                sp.dma_start(x3_d[bass.ds(b * T, T), :].rearrange("(c p) d -> p c d", p=P),
                             routed[:, :, 0, 0:D]).then_inc(x3_st, 16)

            sequence(0, True, False)
            with sp.Fori(1, B - 1) as b:
                sequence(b, False, False)
            sequence(B - 1, False, True)
            for e in range(2, E):
                sp.wait_ge(w1lo, e - 1)
                sp.dma_start(stage[:, e % 2, :], w1_d[e]).then_inc(ld_stage[e % 2], 16)
            store_x3(B - 2)
            store_x3(B - 1)
            sp.wait_ge(w1lo, E)
            sp.dma_start(b2_rows, b2_d.rearrange("e f -> (e f)").partition_broadcast(P)).then_inc(ld_b2, 16)

            sp.wait_ge(plan, PLAN_DONE)
            for e in range(E):
                at = sp.value_load(padi[0:1, e:e + 1], min_val=0, max_val=E * REGION - P)
                sp.dma_start(rows_d[bass.ds(at, P), :], pads[:, e, :]).then_inc(pad_st, 16)

            sp.wait_ge(sct, 16 * 2 * CH * B)
            sp.wait_ge(pad_st, 16 * E)
            sp.wait_ge(dmy_st, 32)

            def load_tile(t0, n, reuse):
                at = sp.value_load(tile_r[0:1, bass.ds(t0 + n, 1)], min_val=0, max_val=E * REGION + (DUMMY - 1) * P)
                if reuse:
                    sp.wait_ge(res_st[n], t0 * (16 // RING))
                sp.dma_start(xg[n], rows_d[bass.ds(at, P), :]).then_inc(ld_xg[n], 16)

            for t in range(RING):
                load_tile(0, t, False)
            sp.wait_ge(x3_st, 16 * B)
            sp.dma_start(xc, x3_d.rearrange("(b c p) d -> p b c d", p=P, c=CH)).then_inc(ld_x3, 16)
            with sp.Fori(RING, TILES - RING + 1, RING) as t:
                for n in range(RING):
                    load_tile(t, n, True)
            for n in range(AHEAD):
                load_tile(TILES, n, True)

            for n in range(RING):
                sp.wait_ge(res_st[n], 16 * (TILES // RING))

            def load_group(i):
                if i >= ZBUF:
                    sp.wait_ge(z_sum, i - ZBUF + 1)
                sp.dma_start(z[i % ZBUF], res_d[i * 2 * T:(i + 1) * 2 * T, :].rearrange(
                    "(c p k) d -> p c k d", p=P, k=2)).then_inc(ld_z[i % ZBUF], 16)

            def store_group(i):
                sp.wait_ge(c_out, (i + 1) * CH)
                sp.dma_start(out_d[i].rearrange("(c p) d -> p c d", p=P), oc[i % 2]).then_inc(out_st[i % 2], 16)

            for i in range(B + ZBUF):
                if i < B:
                    load_group(i)
                if i >= ZBUF:
                    store_group(i - ZBUF)
            for n in range(2):
                sp.wait_ge(out_st[n], 16 * (B // 2))

        @block.tensor
        def _(pe):
            def split3(out, w, wcols, m, mcols, first=True, last=True):
                pe.matmul(out, w[0][:, wcols], m[0][:, mcols], start=first, stop=False)
                pe.matmul(out, w[1][:, wcols], m[0][:, mcols], start=False, stop=False)
                return pe.matmul(out, w[0][:, wcols], m[1][:, mcols], start=False, stop=last)

            def blk(c, n=P):
                return slice(c * n, (c + 1) * n)

            ALLT = slice(0, T)

            def turn(out, src):
                for c in range(CH):
                    mm = pe.transpose(out[:, blk(c)], src(c), ident[:, :])
                return mm

            def q_proj(par, p):
                split3(bkA[:, :], wq, blk(p), hT[par], ALLT).then_inc(q_mm, 1)

            def k_proj_high(par, p):
                pe.matmul(bkB[:, :], wk[0][:, blk(p)], hT[par][0][:, ALLT], start=True, stop=False)

            def k_proj_rest(par, p):
                pe.matmul(bkB[:, :], wk[1][:, blk(p)], hT[par][0][:, ALLT], start=False, stop=False)
                pe.matmul(bkB[:, :], wk[0][:, blk(p)], hT[par][1][:, ALLT], start=False, stop=True).then_inc(k_mm, 1)

            def v_proj(par, half, c):
                h, out = hT[par], bkC[:, :]
                pe.matmul(out, h[0][:, blk(c)], wv[0][:, blk(half, 512)], start=True, stop=False)
                pe.matmul(out, h[1][:, blk(c)], wv[0][:, blk(half, 512)], start=False, stop=False)
                pe.matmul(out, h[0][:, blk(c)], wv[1][:, blk(half, 512)], start=False, stop=True).then_inc(v_mm, 1)

            def front_t(b):
                pe.wait_ge(ln_x[0], b + 1)
                turn(bkE, lambda c: xln[:, c, :]).then_inc(f1_mm, 1)

            def otr():
                turn(bkC, lambda c: on[:, c, :]).then_inc(ot_mm, 1)

            def wo_acc(p):
                split3(bkY[:, :], wo, blk(p), oT, ALLT, first=(p == 0), last=(p == PAIRS - 1)).then_inc(wo_mm, 1)

            def y_t(b, out):
                pe.wait_ge(yT_sb, b + 1)
                turn(out, lambda c: colT[:, blk(c)]).then_inc(yt_mm, 1)

            def h2_t(b, out):
                pe.wait_ge(ln_x[1], b + 1)
                turn(out, lambda c: x1[:, c, :]).then_inc(h2_mm, 1)

            def ffn1(b, f, out):
                if f == 0:
                    pe.wait_ge(h2_lo, b + 1)
                split3(out[:, :], wf1, blk(f), h2T, ALLT).then_inc(ff1_mm, 1)

            def ffn2(b, out):
                for f in range(NF):
                    pe.wait_ge(g_lo, b * NF + f + 1)
                    g = [gT[0][:, f, :], gT[1][:, f, :]]
                    mm = split3(out[:, :], wf2, blk(f), g, ALLT, first=(f == 0), last=(f == NF - 1))
                mm.then_inc(ff2_mm, 1)

            def y2_t(b, out):
                pe.wait_ge(y2_sb, b + 1)
                turn(out, lambda c: colT[:, blk(c)]).then_inc(y2_mm, 1)

            def x3_t(b, out):
                pe.wait_ge(ln_x[2], b + 1)
                turn(out, lambda c: routed[:, c, 0, 0:D]).then_inc(x3_mm, 1)

            def gate(b, out):
                pe.wait_ge(x3T_sb, b + 1)
                for c in range(CH):
                    mm = pe.matmul(out[:, blk(c, E)], colT[:, blk(c)], gw[:, :], start=True, stop=True)
                mm.then_inc(gate_mm, 1)

            def ranks(b, out):
                pe.wait_ge(tp, (b + 1) * TP_STEPS)
                flat = chosen[:, :, :].rearrange("p c e -> p (c e)")
                pe.matmul(out[:, 0:CH * E], before[:, :], flat, start=True, stop=False)
                for c in range(1, CH):
                    pe.matmul(out[:, c * E:CH * E], ones_b[:, :], flat[:, 0:(CH - c) * E], start=False,
                              stop=(c == CH - 1))
                for c in range(CH):
                    mm = pe.matmul(out[:, CH * E:(CH + 1) * E], ones_b[:, :], chosen[:, c, :], start=(c == 0),
                                   stop=(c == CH - 1))
                mm.then_inc(rank_mm, 1)

            def step(b, par, p, first, last):
                g = b * PAIRS + p
                cur = p % 2
                begin = first and p == 0
                nxt = not (last and p == PAIRS - 1)
                npar = par if p < PAIRS - 1 else 1 - par

                pe.wait_ge(q_phi, g + 1)
                pe.wait_ge(k_phi, g + 1)
                if p == 3 and not last:
                    pe.wait_ge(h32_sb, b + 2)
                f_read = []
                if not first:
                    e_read = {2: [(x1_sb, b)], 4: [(gelu_sb, b * NF - 2)], 6: [(s3_sb, b)], 7: [(x3T_sb, b)]}.get(p, [])
                    f_read = {0: [(cnt_sb, b)], 3: [(h232_sb, b)], 5: [(y2_sb, b)], 7: [(lg_sb, b)]}.get(p, [])
                    for what, count in e_read:
                        pe.wait_ge(what, count)
                for h in range(2):
                    if h == 1:
                        for what, count in f_read:
                            pe.wait_ge(what, count)
                    hs = slice(h * DH, (h + 1) * DH)
                    for c in range(CH):
                        mm = pe.matmul((bkE, bkF)[h][:, blk(c)], kT[cur][hs, blk(c)], qT[cur][hs, blk(c)],
                                       start=True, stop=True)
                    mm.then_inc(sc_mm, 1)
                pe.wait_ge(v_sb, 2 * CH * B if last and p > CH else CH + g)
                turn(bkC, lambda c: kT[cur][:, blk(c)]).then_inc(kt_mm, 1)
                if p == 4 and not first:
                    pe.wait_ge(gelu_sb, b * NF)
                if nxt:
                    q_proj(npar, (p + 1) % PAIRS)
                    k_proj_high(npar, (p + 1) % PAIRS)
                pe.wait_ge(a_msk, 2 * g + 2)
                pe.wait_ge(kt_sb, g + 1)
                pe.wait_ge(v_sb, 2 * CH * b + (CH if p < PAIRS // 2 else 2 * CH))
                for c in range(CH - 1):
                    for h in range(2):
                        hs = slice(h * DH, (h + 1) * DH)
                        mm = pe.matmul(bkF[hs, blk(c, DV1)], ktok[:, c, hs],
                                       va[:, c, 2 * p + h, :], start=True, stop=True)
                mm.then_inc(u_mm, 1)
                if nxt:
                    k_proj_rest(npar, (p + 1) % PAIRS)
                if not begin:
                    pe.wait_ge(o_sb, 2 * g)
                    otr()

                def outputs(c, out):
                    if c > 0:
                        pe.matmul(out[:, 0:2 * DV1], qT[cur][:, blk(c)], state[:, c - 1, :], start=True, stop=False)
                    for h in range(2):
                        mm = pe.matmul(out[:, blk(h, DV1)], am[h][:, c, :], va[:, c, 2 * p + h, :],
                                       start=(c == 0), stop=(c == 0 or h == 1))
                    return mm

                outputs(0, bkG[:, 0:130])
                if not first:
                    if p == 1:
                        y_t(b - 1, bkE)
                    if p == 3:
                        ffn1(b - 1, 0, bkE)
                    if p == 5:
                        y2_t(b - 1, bkE)
                    if p == 6:
                        x3_t(b - 1, bkE)
                pe.wait_ge(s_sb, g + 1)
                if not first and p == 3:
                    ffn1(b - 1, 1, bkF)
                outputs(1, bkG[:, 130:260]).then_inc(o_mm, 1)
                outputs(2, bkH[:, 0:130])
                outputs(3, bkH[:, 130:260]).then_inc(o_mm, 1)
                if p == 2 and not last:
                    front_t(b + 1)
                if p == 6 and not first:
                    gate(b - 1, bkF)
                if not begin:
                    pe.wait_ge(ot_lo, g)
                    if p == 1 and not first:
                        pe.wait_ge(yT_sb, b)
                    wo_acc((p - 1) % PAIRS)
                if not first:
                    if p == 2:
                        h2_t(b - 1, bkF)
                    if p == 4:
                        ffn2(b - 1, bkF)
                if p < CH:
                    v_proj(par, 1, p)
                elif not last:
                    pe.wait_ge(h_lo, b + 2)
                    v_proj(1 - par, 0, p - CH)
                if p == 7 and not first:
                    ranks(b - 1, bkF)
                if p == 3 and not first:
                    pe.wait_ge(q_phi, g + 2)
                    ffn1(b - 1, 2, bkA)
                    pe.wait_ge(k_phi, g + 2)
                    ffn1(b - 1, 3, bkB)

            def sequence(b, par, first, last):
                for p in range(PAIRS):
                    step(b, par, p, first, last)

            pe.wait_ge(cst, CST_ALL)
            front_t(0)
            pe.wait_ge(h_lo, 1)
            pe.wait_ge(wlo, 4)
            q_proj(0, 0)
            k_proj_high(0, 0)
            k_proj_rest(0, 0)
            for c in range(CH):
                if c > 0:
                    pe.wait_ge(v_sb, c)
                v_proj(0, 0, c)
            sequence(0, 0, True, False)
            with pe.Fori(1, B - 2, 2) as b:
                sequence(b, 1, False, False)
                sequence(b + 1, 0, False, False)
            sequence(B - 1, 1, False, True)

            b = B - 1
            pe.wait_ge(o_sb, 2 * B * PAIRS)
            otr()
            pe.wait_ge(ot_lo, B * PAIRS)
            wo_acc(PAIRS - 1)
            pe.wait_ge(cnt_sb, B)
            y_t(b, bkF)
            h2_t(b, bkE)
            ffn1(b, 0, bkA)
            ffn1(b, 1, bkB)
            ffn1(b, 2, bkG)
            ffn1(b, 3, bkH)
            ffn2(b, bkC)
            y2_t(b, bkY)
            x3_t(b, bkA)
            gate(b, bkB)
            ranks(b, bkG)

            pe.wait_ge(plan, PLAN_DONE)
            pe.wait_ge(ld_w2, 16)
            pe.wait_ge(w1lo, E)
            X, L, M, Y = bank[0:2], bank[2:4], bank[4:6], bank[6:8]

            def expert(t):
                return pe.value_load(tile_e[0:1, bass.ds(t, 1)], min_val=0, max_val=E - 1)

            def rows_t(t0, n, reuse):
                if n >= RING:
                    t0, n = t0 + RING, n - RING
                if reuse:
                    pe.wait_ge(xt_lo, t0 + n - 1)
                pe.wait_ge(ld_xg[n], t0 * (16 // RING) + 16)
                pe.transpose(X[n % 2][:, 0:P], xg[n][:, 0:D], ident[:, :]).then_inc(xt_mm, 1)

            def layer1(t, n, e, reuse):
                if reuse:
                    pe.wait_ge(hb_sb, t - 1)
                pe.wait_ge(xt_lo, t + 1)
                a, out = xT[n % 2], L[n % 2][:, :]
                pe.matmul(out, a[0][:, :], w1[0][:, bass.ds(e * F, F)], start=True, stop=False)
                pe.matmul(out, a[1][:, :], w1[0][:, bass.ds(e * F, F)], start=False, stop=False)
                pe.matmul(out, a[0][:, :], w1[1][:, bass.ds(e * F, F)], start=False, stop=True).then_inc(l1_mm, 1)

            def hidden_t(t, n, reuse):
                if reuse:
                    pe.wait_ge(ht_a, t - 1)
                pe.wait_ge(hb_sb, t + 1)
                for f in range(NF):
                    mm = pe.transpose(M[n % 2][:, blk(f)], hb[n % 2][:, blk(f)], ident[:, :])
                mm.then_inc(ht_mm, 1)

            def layer2(t, n, e, reuse):
                if reuse:
                    pe.wait_ge(yb_sb, t - 1)
                pe.wait_ge(ht_a, t + 1)
                for f in range(NF):
                    mm = pe.matmul(Y[n % 2][:, 0:D], hTe[n % 2][:, blk(f)], w2[:, bass.ds(e * F + f * D, D)],
                                   start=(f == 0), stop=(f == NF - 1))
                mm.then_inc(l2_mm, 1)

            def round_(t0, first):
                e = {} if first else {-1: expert(t0 - 1)}
                e[0] = expert(t0)
                for n in range(RING):
                    e[n + 1] = expert(t0 + n + 1)
                    rows_t(t0, n + 2, not (first and n == 0))
                    layer1(t0 + n + 1, n + 1, e[n + 1], not (first and n == 0))
                    hidden_t(t0 + n, n, not (first and n < 2))
                    if not (first and n == 0):
                        layer2(t0 + n - 1, n - 1, e[n - 1], not (first and n <= 2))

            rows_t(0, 0, False)
            rows_t(0, 1, False)
            layer1(0, 0, expert(0), False)
            round_(0, True)
            with pe.Fori(RING, TILES - RING + 1, RING) as t0:
                round_(t0, False)
            layer2(TILES - 1, RING - 1, expert(TILES - 1), True)

        @block.scalar
        def _(act):
            def copy(out, src):
                return act.activation(out, src, ACT.Copy)

            def y_copy(b):
                act.wait_ge(wo_mm, PAIRS * (b + 1))
                copy(colT, bkY[:, :]).then_inc(yT_sb, 1)

            def front_scale(b, reuse):
                act.wait_ge(f1_mm, b + 1)
                if reuse:
                    act.wait_ge(h_lo, b)
                act.activation(h32, bkE[:, :], ACT.Identity, bias=cols[:, 1:2], scale=cols[:, 0:1]).then_inc(h32_sb, 1)

            def front_high(b, par):
                act.wait_ge(h32_sb, b + 1)
                copy(hT[par][0][:, :], h32).then_inc(h_hi, 1)

            def scale2(b, src, fronts):
                act.wait_ge(h2_mm, b + 1)
                act.wait_ge(h_lo, fronts)
                act.activation(h32, src[:, :], ACT.Identity, bias=cols[:, 3:4], scale=cols[:, 2:3]).then_inc(h232_sb, 1)

            def h2_copy(b):
                act.wait_ge(h232_sb, b + 1)
                copy(h2T[0][:, :], h32).then_inc(h2_hi, 1)

            def gelus(b, fs, banks):
                for f in fs:
                    if f >= 2:
                        act.wait_ge(g_lo, b * NF + f - 1)
                    act.wait_ge(ff1_mm, b * NF + f + 1)
                    act.activation(g32[f % 2], banks[f][:, :], ACT.Gelu).then_inc(gelu_sb, 1)

            def y2_copy(b, src):
                act.wait_ge(ff2_mm, b + 1)
                copy(colT, src[:, :]).then_inc(y2_sb, 1)

            def x3_copy(b, src):
                act.wait_ge(x3_mm, b + 1)
                copy(colT, src[:, :]).then_inc(x3T_sb, 1)

            def gate_exp(b):
                act.wait_ge(lg_st, 2 * (b + 1))
                act.activation(pe_[:, :, :], lg[:, :, :], ACT.Exp).then_inc(ex_sb, 1)

            def ot_high(g):
                act.wait_ge(ot_mm, g)
                copy(oT[0][:, :], bkC[:, :]).then_inc(ot_hi, 1)

            def q_exps(g):
                act.wait_ge(q_mm, g + 1)
                act.activation(e_q, bkA[:, :], ACT.Relu, scale=-1.0).then_inc(q_relu, 1)
                act.wait_ge(q_relu, g + 1)
                act.activation(e_q, e_q, ACT.Exp, scale=-1.0).then_inc(q_exp, 1)

            def k_exps(g):
                act.wait_ge(k_mm, g + 1)
                act.activation(e_k, bkB[:, :], ACT.Relu, scale=-1.0).then_inc(k_relu, 1)
                act.wait_ge(k_relu, g + 1)
                act.activation(e_k, e_k, ACT.Exp, scale=-1.0).then_inc(k_exp, 1)

            def v_copy(n, half, c):
                act.wait_ge(v_mm, n)
                copy(va[:, c, half * 8:(half + 1) * 8, 0:DH],
                     bkC[:, :].rearrange("p (h j) -> p h j", h=8)).then_inc(v_sb, 1)

            def step(b, par, p, first, last):
                g = b * PAIRS + p
                act.wait_ge(kt_mm, g + 1)
                copy(ktok, bkC[:, :].rearrange("p (c d) -> p c d", c=CH)).then_inc(kt_sb, 1)
                if not (last and p == PAIRS - 1):
                    act.wait_ge(q_phi, g + 1)
                    q_exps(g + 1)
                if not (first and p == 0):
                    ot_high(g)
                if not (last and p == PAIRS - 1):
                    act.wait_ge(k_phi, g + 1)
                    k_exps(g + 1)
                if p == 2 and not last:
                    front_scale(b + 1, True)
                    front_high(b + 1, 1 - par)
                if not first:
                    if p == 0:
                        y_copy(b - 1)
                    if p == 3:
                        gelus(b - 1, (0, 1), {0: bkE, 1: bkF})
                    if p == 2:
                        scale2(b - 1, bkF, B if last else b + 2)
                    if p == 4:
                        y2_copy(b - 1, bkF)
                    if p == 6:
                        x3_copy(b - 1, bkE)
                if p < CH:
                    v_copy(g + CH + 1, 1, p)
                elif not last:
                    v_copy(g + CH + 1, 0, p - CH)
                if not first:
                    if p == 2:
                        h2_copy(b - 1)
                    if p == 3:
                        gelus(b - 1, (2, 3), {2: bkA, 3: bkB})
                    if p == 6:
                        gate_exp(b - 1)
                if last:
                    act.wait_ge(ld_stage[p % 2], 16 * (p // 2 + 2))
                    copy(w1[0][:, p * F:(p + 1) * F], stage[:, p % 2, :]).then_inc(w1hi, 1)

            def sequence(b, par, first, last):
                for p in range(PAIRS):
                    step(b, par, p, first, last)

            act.wait_ge(ld_small, 16 * 6)
            act.wait_ge(ld_w, 64)
            for n, w in enumerate((wq, wk, wv, wo)):
                copy(w[0][:, :], v_aug[:, n * 1024:(n + 1) * 1024]).then_inc(whi, 1)
                if n == 1:
                    front_scale(0, False)
                    front_high(0, 0)
            for n, w in enumerate((wf1, wf2)):
                act.wait_ge(ld_stage[n], 16)
                copy(w[0][:, :], stage[:, n, :]).then_inc(whi, 1)
            q_exps(0)
            k_exps(0)
            act.wait_ge(cst_dve, 1)
            for c in range(CH):
                v_copy(c + 1, 0, c)
            sequence(0, 0, True, False)
            with act.Fori(1, B - 2, 2) as b:
                sequence(b, 1, False, False)
                sequence(b + 1, 0, False, False)
            sequence(B - 1, 1, False, True)

            b = B - 1
            ot_high(B * PAIRS)
            y_copy(b)
            scale2(b, bkE, B)
            h2_copy(b)
            gelus(b, range(NF), {0: bkA, 1: bkB, 2: bkG, 3: bkH})
            y2_copy(b, bkC)
            x3_copy(b, bkA)
            gate_exp(b)

            X, M = bank[0:2], bank[4:6]
            HALF = F // 2

            def rows_hi(t, n, reuse):
                if reuse:
                    act.wait_ge(l1_mm, t - 1)
                act.wait_ge(xt_mm, t + 1)
                copy(xT[n % 2][0][:, :], X[n % 2][:, 0:P]).then_inc(xt_hi, 1)

            def hidden_relu(t, n, reuse):
                if reuse:
                    act.wait_ge(l2_mm, t - 1)
                act.wait_ge(ht_mm, t + 1)
                act.activation(hTe[n % 2][:, 0:F], M[n % 2][:, 0:F], ACT.Relu).then_inc(ht_a, 1)

            def weigh(t, n):
                act.wait_ge(yb_sb, t + 1)
                act.activation(yw[n], yb[n % 2], ACT.Copy, scale=xg[n][:, D + 1:D + 2]).then_inc(yw_sb, 1)

            def tile(t, n, first):
                rows_hi(t + 2, (n + 2) % RING, True)
                hidden_relu(t, n, not (first and n < 2))
                if not (first and n == 0):
                    weigh(t - 1, (n - 1) % RING)

            rows_hi(0, 0, False)
            rows_hi(1, 1, False)
            for n in range(RING):
                tile(n, n, True)
            with act.Fori(RING, TILES - RING + 1, RING) as t:
                for n in range(RING):
                    tile(t + n, n, False)
            weigh(TILES - 1, RING - 1)

            def group(i0, n, reuse):
                act.wait_ge(c_nb, i0 + n + 1)
                if reuse:
                    act.wait_ge(out_st[n], i0 * 8)
                for c in range(CH):
                    act.activation(oc[n][:, c, :], sc[n][:, c, :], ACT.Identity, bias=nmr[n][:, c:c + 1],
                                   scale=rs_c[n][:, c:c + 1]).then_inc(c_out, 1)

            for n in range(2):
                group(0, n, False)
            with act.Fori(2, B - 1, 2) as i:
                for n in range(2):
                    group(i, n, True)

        @block.vector
        def _(dve):
            def f32(ap):
                return ap.bitcast(F32)

            def low(out, whole, high):
                return dve.tensor_tensor(out, whole, f32(high), ALU.subtract)

            def ln_stats(k, src, i):
                for c in range(CH):
                    ins = dve.bn_stats(stats[k][:, c, :], src[:, c, :])
                ins.then_inc(ln_st[k], 1)
                apart(dve)
                dve.wait_ge(ln_st[k], i + 1)
                for c in range(CH):
                    ins = dve.bn_aggr(mv[k][:, c, :], stats[k][:, c, :])
                ins.then_inc(ln_mv[k], 1)

            def ln_apply(k, out, src, i):
                dve.wait_ge(ln_r[k], i + 1)
                for c in range(CH):
                    ins = dve.tensor_scalar(out(c), src[:, c, :], mv[k][:, c, 0:1], rstd[k][:, c:c + 1],
                                            ALU.subtract, ALU.mult)
                ins.then_inc(ln_x[k], 1)

            def bank_chunks(bk):
                return bk[:, :].rearrange("p (c d) -> p c d", c=CH)

            def front_stats(b):
                dve.wait_ge(ld_xln, 16 * (b + 1))
                ln_stats(0, xln, b)

            def front_apply(b):
                ln_apply(0, lambda c: xln[:, c, :], xln, b)

            def front_low(b, par):
                dve.wait_ge(h_hi, b + 1)
                dve.wait_ge(h32_sb, b + 1)
                low(hT[par][1][:, :], h32, hT[par][0][:, :]).then_inc(h_lo, 1)

            def residual1(b, src):
                dve.wait_ge(yt_mm, b + 1)
                dve.wait_ge(ld_xres, 16 * (b + 1))
                dve.tensor_tensor(x1, bank_chunks(src), xres, ALU.add).then_inc(x1_sb, 1)
                dve.wait_ge(x1_sb, b + 1)
                ln_stats(1, x1, b)

            def norm2(b):
                dve.wait_ge(xx_sb, b + 1)
                ln_apply(1, lambda c: x1[:, c, :], x1, b)

            def low2(b):
                dve.wait_ge(h2_hi, b + 1)
                dve.wait_ge(h232_sb, b + 1)
                low(h2T[1][:, :], h32, h2T[0][:, :]).then_inc(h2_lo, 1)

            def split_g(b, fs):
                for f in fs:
                    dve.wait_ge(gelu_sb, b * NF + f + 1)
                    dve.tensor_copy(gT[0][:, f, :], g32[f % 2]).then_inc(g_hi, 1)
                for f in fs:
                    dve.wait_ge(g_hi, b * NF + f + 1)
                    low(gT[1][:, f, :], g32[f % 2], gT[0][:, f, :]).then_inc(g_lo, 1)

            def residual2(b, src):
                dve.wait_ge(y2_mm, b + 1)
                dve.tensor_tensor(xx1, bank_chunks(src), xx1, ALU.add).then_inc(s3_sb, 1)
                dve.wait_ge(s3_sb, b + 1)
                ln_stats(2, xx1, b)

            def norm3(b):
                ln_apply(2, lambda c: routed[:, c, 0, 0:D], xx1, b)

            def logits(b, src):
                dve.wait_ge(gate_mm, b + 1)
                dve.tensor_tensor(lg[:, :, :], src[:, 0:CH * E].rearrange("p (c e) -> p c e", c=CH),
                                  gb[:, :].unsqueeze(1).broadcast_to([P, CH, E]), ALU.add
                                  ).then_inc(lg_sb, 1)
                dve.wait_ge(lg_sb, b + 1)
                dve.tensor_reduce(lmax[:, :], lg[:, :, :], AX.X, ALU.max).then_inc(lg_st, 1)
                dve.wait_ge(lg_st, 2 * b + 1)
                dve.tensor_tensor(lg[:, :, :], lg[:, :, :], lmax[:, :].unsqueeze(2).broadcast_to([P, CH, E]),
                                  ALU.subtract).then_inc(lg_st, 1)

            def top2(b):
                apart(dve)
                dve.wait_ge(ex_sb, b + 1)
                for c in range(CH):
                    ins = dve.max(top[:, c, :], pe_[:, c, :])
                ins.then_inc(tp, 1)
                apart(dve)
                dve.wait_ge(tp, TP_STEPS * b + 1)
                for c in range(CH):
                    ins = dve.max_index(topi[:, c, :], top[:, c, :], pe_[:, c, :])
                dve.tensor_tensor(wsum[:, :], top[:, :, 0], top[:, :, 1], ALU.add).then_inc(tp, 1)
                dve.wait_ge(tp, TP_STEPS * b + 2)
                dve.reciprocal(wsum[:, :], wsum[:, :])
                for k in range(2):
                    ins = dve.tensor_tensor(onehot[:, k, :, :],
                                            topi[:, :, k:k + 1].broadcast_to([P, CH, E]),
                                            iota_e[:, :].unsqueeze(1).broadcast_to([P, CH, E]), ALU.is_equal)
                ins.then_inc(tp, 1)
                dve.wait_ge(tp, TP_STEPS * b + 3)
                dve.tensor_tensor(routed[:, :, :, D + 1], top[:, :, 0:2],
                                  wsum[:, :].unsqueeze(2).broadcast_to([P, CH, 2]), ALU.mult)
                dve.tensor_tensor(chosen[:, :, :], onehot[:, 0, :, :], onehot[:, 1, :, :], ALU.add).then_inc(tp, 1)

            def place(b, src):
                dve.wait_ge(rank_mm, b + 1)
                dve.tensor_tensor(rank[:, :, :], src[:, 0:CH * E].rearrange("p (c e) -> p c e", c=CH),
                                  base[:, :].unsqueeze(1).broadcast_to([P, CH, E]), ALU.add).then_inc(rk, 1)
                dve.tensor_copy(routed[:, :, :, D].bitcast(U32), dest[:, :, :]).then_inc(rk, 1)
                dve.wait_ge(rk, RK_STEPS * b + 1)
                dve.tensor_tensor(base[:, :], src[:, CH * E:(CH + 1) * E], base[:, :], ALU.add).then_inc(cnt_sb, 1)
                dve.tensor_tensor(prod[:, :, :, :], onehot[:, :, :, :],
                                  rank[:, :, :].unsqueeze(1).broadcast_to([P, 2, CH, E]), ALU.mult).then_inc(rk, 1)
                dve.wait_ge(rk, RK_STEPS * b + 2)
                dve.tensor_scalar(dest[:, :, :], dest[:, :, :], float(2 * T), None, ALU.add).then_inc(rk, 1)
                dve.wait_ge(rk, RK_STEPS * b + 3)
                dve.tensor_reduce(slot_f[:, :, :], prod[:, :, :, :], AX.X, ALU.add).then_inc(rk, 1)
                dve.wait_ge(rk, RK_STEPS * b + 5)
                dve.tensor_copy(slot[:, :, :], slot_f[:, :, :]).then_inc(rt_sb, 1)

            def phi(out, pre, e):
                return dve.scalar_tensor_tensor(out=out, in0=pre[:, :], scalar=0.0, in1=e, op0=ALU.max, op1=ALU.add)

            def q_phis(g, gp):
                dve.wait_ge(q_exp, g + 1)
                phi(qT[gp], bkA, e_q).then_inc(q_phi, 1)

            def k_phis(g, gp):
                dve.wait_ge(k_exp, g + 1)
                phi(kT[gp], bkB, e_k).then_inc(k_phi, 1)

            def ot_low(g):
                dve.wait_ge(ot_hi, g)
                low(oT[1][:, :], bkC[:, :], oT[0][:, :]).then_inc(ot_lo, 1)

            def normalise(g, bk, half):
                dve.wait_ge(o_mm, 2 * g + half + 1)
                o4 = bk[:, 0:4 * DV1].rearrange("p (x j) -> p x j", x=4)
                i = 4 * g + 2 * half
                dve.tensor_scalar(den[:, :], o4[:, :, DH], EPS_DEN, None, ALU.max).then_inc(o_den, 1)
                dve.wait_ge(o_den, i + 1)
                dve.reciprocal(rden[:, :], den[:, :]).then_inc(o_den, 1)
                dve.wait_ge(o_den, i + 2)
                dve.tensor_tensor(on[:, 2 * half:2 * half + 2, :].rearrange("p c (h j) -> p (c h) j", h=2),
                                  o4[:, :, 0:DH], rden[:, :].unsqueeze(2).broadcast_to([P, 4, DH]),
                                  ALU.mult).then_inc(o_sb, 1)

            def states(g):
                dve.wait_ge(u_mm, g + 1)
                for c in range(CH - 1):
                    for h in range(2):
                        hs, js = slice(h * DH, (h + 1) * DH), slice(h * DV1, (h + 1) * DV1)
                        u = bkF[hs, c * DV1:(c + 1) * DV1]
                        if c == 0:
                            ins = dve.tensor_copy(state[hs, 0, js], u)
                        else:
                            ins = dve.tensor_tensor(state[hs, c, js], u, state[hs, c - 1, js], ALU.add)
                    if c < CH - 2:
                        ins.then_inc(s_part, 1)
                        dve.wait_ge(s_part, 2 * g + c + 1)
                ins.then_inc(s_sb, 1)

            def step(b, par, p, first, last):
                g = b * PAIRS + p
                nxt = not (last and p == PAIRS - 1)
                for h in range(2):
                    dve.wait_ge(sc_mm, 2 * g + h + 1)
                    dve.tensor_tensor(am[h], bank_chunks((bkE, bkF)[h]),
                                      causal[:, :].unsqueeze(1).broadcast_to([P, CH, P]), ALU.mult).then_inc(a_msk, 1)
                if not first:
                    if p == 3:
                        low2(b - 1)
                    if p == 6:
                        norm3(b - 1)
                states(g)
                if nxt:
                    q_phis(g + 1, (p + 1) % 2)
                if p == 2 and not last:
                    front_apply(b + 1)
                if not (first and p == 0):
                    ot_low(g)
                if nxt:
                    k_phis(g + 1, (p + 1) % 2)
                if p == 7 and not first:
                    top2(b - 1)
                if p == 4 and not first:
                    split_g(b - 1, (2, 3))
                if not first:
                    if p == 1:
                        residual1(b - 1, bkE)
                    if p == 2:
                        norm2(b - 1)
                    if p == 5:
                        residual2(b - 1, bkE)
                normalise(g, bkG, 0)
                if p == 2 and not last:
                    front_low(b + 1, 1 - par)
                normalise(g, bkH, 1)
                if p == 0 and not last:
                    front_stats(b + 1)
                if not first:
                    if p == 3:
                        split_g(b - 1, (0, 1))
                    if p == 6:
                        logits(b - 1, bkF)
                    if p == 7:
                        place(b - 1, bkF)
                if last:
                    dve.wait_ge(w1hi, p + 1)
                    low(w1[1][:, p * F:(p + 1) * F], stage[:, p % 2, :], w1[0][:, p * F:(p + 1) * F]).then_inc(w1lo, 1)

            def sequence(b, par, first, last):
                for p in range(PAIRS):
                    step(b, par, p, first, last)

            dve.memset(state[:, :, :], 0.0)
            dve.memset(neg_half[:, :], -0.5).then_inc(nh_set, 1)
            dve.memset(den[:, :], 1.0).then_inc(cnt_sb, 1)
            front_stats(0)
            front_apply(0)
            for n, w in enumerate((wq, wk)):
                dve.wait_ge(whi, n + 1)
                low(w[1][:, :], v_aug[:, n * 1024:(n + 1) * 1024], w[0][:, :]).then_inc(wlo, 1)
            front_low(0, 0)
            for n, w in ((2, wv), (3, wo)):
                dve.wait_ge(whi, n + 1)
                low(w[1][:, :], v_aug[:, n * 1024:(n + 1) * 1024], w[0][:, :]).then_inc(wlo, 1)
            dve.wait_ge(wlo, 4)
            dve.memset(va[:, :, :, DH:DV1], 1.0).then_inc(cst_dve, 1)
            for n, w in enumerate((wf1, wf2)):
                dve.wait_ge(whi, n + 5)
                low(w[1][:, :], stage[:, n, :], w[0][:, :]).then_inc(wlo, 1)
            q_phis(0, 0)
            k_phis(0, 0)
            dve.wait_ge(cst, CST_ALL)
            dve.tensor_scalar(base[:, :], iota_e[:, :], float(REGION), None, ALU.mult)
            dve.tensor_copy(pads[:, :, D].bitcast(U32), padf[:, E:2 * E]).then_inc(pads_dmy, 1)
            dve.wait_ge(dmy_st, 32)
            sequence(0, 0, True, False)
            with dve.Fori(1, B - 2, 2) as b:
                sequence(b, 1, False, False)
                sequence(b + 1, 0, False, False)
            sequence(B - 1, 1, False, True)

            b = B - 1
            ot_low(B * PAIRS)
            residual1(b, bkF)
            norm2(b)
            low2(b)
            split_g(b, (0, 1))
            split_g(b, (2, 3))
            residual2(b, bkY)
            norm3(b)
            logits(b, bkB)
            top2(b)
            place(b, bkG)

            n = [0]

            def then(ins):
                n[0] += 1
                ins.then_inc(plan, 1)
                dve.wait_ge(plan, n[0])

            EB = [P, TILES + AHEAD, E]
            then(dve.scalar_tensor_tensor(out=cnt[:, :], in0=iota_e[:, :], scalar=-float(REGION), in1=base[:, :],
                                          op0=ALU.mult, op1=ALU.add))
            then(dve.tensor_tensor(gt32[:, :, :], cnt[:, :].unsqueeze(2).broadcast_to([P, E, 32]),
                                   m32[:, :].unsqueeze(1).broadcast_to([P, E, 32]), ALU.is_gt))
            then(dve.tensor_reduce(nt[:, :], gt32[:, :, :], AX.X, ALU.add))
            then(dve.tensor_tensor_scan(ntc[:, :], one_e[:, :], nt[:, :], 0.0, ALU.mult, ALU.add))
            then(dve.tensor_tensor(le[:, :, :], ntc[:, :].unsqueeze(1).broadcast_to(EB),
                                   tidx[:, :].unsqueeze(2).broadcast_to(EB), ALU.is_le))
            then(dve.tensor_reduce(en[:, :], le[:, :, :], AX.X, ALU.add))
            then(dve.tensor_tensor(le[:, :, :], le[:, :, :], nt[:, :].unsqueeze(1).broadcast_to(EB), ALU.mult))
            then(dve.tensor_reduce(cx[:, :], le[:, :, :], AX.X, ALU.add))
            then(dve.tensor_tensor(cx[:, :], tidx[:, :], cx[:, :], ALU.subtract))
            then(dve.tensor_scalar(cx[:, :], cx[:, :], float(P), None, ALU.mult))
            dve.scalar_tensor_tensor(out=tile_r[:, :], in0=en[:, :], scalar=float(REGION), in1=cx[:, :],
                                     op0=ALU.mult, op1=ALU.add)
            then(dve.memset(pads[:, :, :], 0.0))
            then(dve.tensor_copy(pads[:, :, D].bitcast(U32), padf[:, 0:E]))
            then(dve.tensor_scalar(padi[:, :], base[:, :], pcol[:, 0:1], None, ALU.add))
            then(dve.tensor_scalar(tile_e[:, :], en[:, :], float(E - 1), None, ALU.min))

            X, L, M, Y = bank[0:2], bank[2:4], bank[4:6], bank[6:8]

            def expert(t):
                return dve.value_load(tile_e[0:1, bass.ds(t, 1)], min_val=0, max_val=E - 1)

            def rows_lo(t, k):
                dve.wait_ge(xt_hi, t + 1)
                low(xT[k % 2][1][:, :], X[k % 2][:, 0:P], xT[k % 2][0][:, :]).then_inc(xt_lo, 1)

            def bias1(t, k, e, reuse):
                if reuse:
                    dve.wait_ge(ht_mm, t - 1)
                dve.wait_ge(l1_mm, t + 1)
                dve.tensor_tensor(hb[k % 2], L[k % 2][:, :], b1_rows[:, bass.ds(e * F, F)], ALU.add).then_inc(hb_sb, 1)

            def bias2(t, k, e, reuse):
                if reuse:
                    dve.wait_ge(yw_sb, t - 1)
                dve.wait_ge(l2_mm, t + 1)
                dve.tensor_tensor(yb[k % 2], Y[k % 2][:, 0:D], b2_rows[:, bass.ds(e * D, D)], ALU.add
                                  ).then_inc(yb_sb, 1)

            def round_(t0, first):
                e = {} if first else {-1: expert(t0 - 1)}
                e[0] = expert(t0)
                for k in range(RING):
                    e[k + 1] = expert(t0 + k + 1)
                    rows_lo(t0 + k + 2, k)
                    bias1(t0 + k + 1, k + 1, e[k + 1], not (first and k == 0))
                    if not (first and k == 0):
                        bias2(t0 + k - 1, k - 1, e[k - 1], not (first and k <= 2))

            dve.wait_ge(ld_b1, 16)
            dve.wait_ge(ld_b2, 16)
            rows_lo(0, 0)
            rows_lo(1, 1)
            bias1(0, 0, expert(0), False)
            round_(0, True)
            with dve.Fori(RING, TILES - RING + 1, RING) as t:
                round_(t, False)
            bias2(TILES - 1, RING - 1, expert(TILES - 1), True)

            def group(i, k, reuse):
                if reuse:
                    dve.wait_ge(c_out, (i - 1) * CH)
                dve.wait_ge(z_sum, i + 1)
                x3_of = chunks(x3_all[:, bass.ds(i * T, T)])
                dve.tensor_tensor(sc[k], x3_of, zs[k], ALU.add).then_inc(c_sb, 1)
                dve.wait_ge(c_sb, i + 1)
                for c in range(CH):
                    ins = dve.bn_stats(stats[k][:, c, :], sc[k][:, c, :])
                ins.then_inc(c_st, 1)
                apart(dve)
                dve.wait_ge(c_st, i + 1)
                for c in range(CH):
                    ins = dve.bn_aggr(mv[k][:, c, :], stats[k][:, c, :])
                ins.then_inc(c_mv, 1)

            def bias_of(i, k):
                dve.wait_ge(c_r, i + 1)
                dve.scalar_tensor_tensor(out=nmr[k][:, :], in0=mv[k][:, :, 0], scalar=-1.0, in1=rs_c[k][:, :], op0=ALU.mult,
                                         op1=ALU.mult).then_inc(c_nb, 1)

            dve.wait_ge(ld_x3, 16)
            group(0, 0, False)
            group(1, 1, False)
            bias_of(0, 0)
            bias_of(1, 1)
            with dve.Fori(2, B - 1, 2) as i:
                for k in range(2):
                    group(i + k, k, True)
                for k in range(2):
                    bias_of(i + k, k)

        @block.gpsimd
        def _(pool):
            def count(v):
                return v if isinstance(v, int) else pool.snap(pool.to_reg(v))

            def rstds(k, i):
                nth = count(i + 1)
                apart(pool)
                pool.wait_ge(ln_mv[k], nth)
                pool.tensor_scalar(ve[k][:, :], mv[k][:, :, 1], EPS_LN, 1.0, ALU.add, ALU.mult).then_inc(ln_ve[k], 1)
                apart(pool)
                pool.wait_ge(ln_ve[k], nth)
                pool.tensor_tensor(rstd[k][:, :], ve[k][:, :], neg_half[:, :], ALU.pow).then_inc(ln_r[k], 1)

            def twice(b):
                nth = count(b + 1)
                apart(pool)
                pool.wait_ge(x1_sb, nth)
                pool.tensor_tensor(xx1, x1, xres, ALU.add).then_inc(xx_sb, 1)

            def scatter(b):
                nth, stored = count(b + 1), count(16 * (b + 1))
                apart(pool)
                pool.wait_ge(ln_x[2], nth)
                pool.tensor_copy(routed[:, :, 1, 0:D], routed[:, :, 0, 0:D]).then_inc(dup_sb, 1)
                apart(pool)
                pool.wait_ge(rt_sb, nth)
                pool.wait_ge(dup_sb, nth)
                pool.wait_ge(x3_st, stored)
                for c in range(CH):
                    for k in range(2):
                        pool.indirect_dma_start(rows_d, bass.IndirectOffsetOnAxis(slot[:, k, c:c + 1], 0),
                                                routed[:, c, k, :], None).then_inc(sct, 16)
                pool.wait_ge(sct, count(2 * CH * 16 * (b + 1)))

            pool.wait_ge(nh_set, 1)
            rstds(0, 0)

            n = [0]

            def then(ins, wait=True):
                n[0] += 1
                ins.then_inc(cst, 1)
                if wait:
                    pool.wait_ge(cst, n[0])

            then(pool.memset(ident[:, :], 0.0))
            then(pool.affine_select(out=ident[:, :], in_=ident[:, :], compare_op=ALU.not_equal, fill=1.0, base=0,
                                    pattern=[[-1, P]], channel_multiplier=1), False)
            then(pool.memset(causal[:, :], 1.0))
            then(pool.affine_select(out=causal[:, :], in_=causal[:, :], compare_op=ALU.is_ge, fill=0.0, base=0,
                                    pattern=[[1, P]], channel_multiplier=-1), False)
            then(pool.memset(ones_b[:, :], 1.0))
            then(pool.affine_select(out=before[:, :], in_=ones_b[:, :], compare_op=ALU.is_gt, fill=0.0, base=0,
                                    pattern=[[1, P]], channel_multiplier=-1), False)
            fl = dict(allow_small_or_imprecise_dtypes=True)
            then(pool.iota(iota_e[:, :], [[1, E]], base=0, channel_multiplier=0, **fl), False)
            then(pool.iota(dest[:, :, :], [[2 * P, CH], [1, 2]], base=0, channel_multiplier=2, **fl), False)
            then(pool.iota(m32[:, :], [[P, 32]], base=0, channel_multiplier=0, **fl), False)
            then(pool.iota(tidx[:, :], [[1, TILES + AHEAD]], base=0, channel_multiplier=0, **fl), False)
            then(pool.iota(pcol[:, :], [[0, 1]], base=0, channel_multiplier=1, **fl), False)
            then(pool.iota(padf[:, :], [[P, 2 * E]], base=PAD_DEST, channel_multiplier=1, **fl), False)
            then(pool.memset(one_e[:, :], 1.0), False)
            then(pool.memset(routed[:, :, :, D + 2:ROW], 0.0), False)
            then(pool.memset(pads[:, :, :], 0.0), False)
            pool.wait_ge(cst, n[0])
            assert n[0] == CST_ALL

            def sequence(b, first, last):
                if not last:
                    rstds(0, b + 1)
                if not first:
                    rstds(1, b - 1)
                    twice(b - 1)
                    rstds(2, b - 1)
                    scatter(b - 1)

            sequence(0, True, False)
            with pool.Fori(1, B - 1) as b:
                sequence(b, False, False)
            sequence(B - 1, False, True)
            rstds(1, B - 1)
            twice(B - 1)
            rstds(2, B - 1)
            scatter(B - 1)

            def store(t, k):
                nth = count(t + 1)
                apart(pool)
                pool.wait_ge(yw_sb, nth)
                pool.indirect_dma_start(res_d, bass.IndirectOffsetOnAxis(xg[k][:, D:D + 1].bitcast(U32), 0),
                                        yw[k], None).then_inc(res_st[k], 16)

            with pool.Fori(0, TILES - RING + 1, RING) as t:
                for k in range(RING):
                    store(t + k, k)

            def group(i):
                pool.wait_ge(ld_z[i % ZBUF], 16 * (i // ZBUF + 1))
                if i >= 2:
                    pool.wait_ge(c_sb, i - 1)
                zg = z[i % ZBUF]
                pool.tensor_tensor(zs[i % 2], zg[:, :, 0, :], zg[:, :, 1, :], ALU.add).then_inc(z_sum, 1)

            def rs(i, k):
                nth = count(i + 1)
                apart(pool)
                pool.wait_ge(c_mv, nth)
                pool.tensor_scalar(ve[k][:, :], mv[k][:, :, 1], EPS_LN, 1.0, ALU.add, ALU.mult).then_inc(c_ve, 1)
                pool.wait_ge(c_ve, nth)
                pool.tensor_tensor(rs_c[k][:, :], ve[k][:, :], neg_half[:, :], ALU.pow).then_inc(c_r, 1)

            group(0)
            for i in range(B):
                if i + 1 < B:
                    group(i + 1)
                rs(i, i % 2)


_INS = ["L0_attn_x", "L0_attn_ln1_g", "L0_attn_ln1_b", "L0_attn_Wq", "L0_attn_Wk", "L0_attn_Wv", "L0_attn_Wo",
        "L0_attn_ln2_g", "L0_attn_ln2_b", "L0_attn_Wf1", "L0_attn_Wf2", "L0_ffn_gate_w", "L0_ffn_gate_b",
        "L0_ffn_w1", "L0_ffn_b1", "L0_ffn_w2", "L0_ffn_b2"]


def kernel(**inputs):
    import numpy as np
    import concourse.bacc as bacc
    from concourse.bass_utils import run_bass_kernel_spmd

    nc = bacc.Bacc("TRN2", target_bir_lowering=False, num_devices=1)
    arrays, args = {}, []
    for name in _INS:
        a = np.ascontiguousarray(inputs[name])
        arrays[f"in_{name}"] = a
        args.append(nc.dram_tensor(f"in_{name}", a.shape, mybir.dt.from_np(a.dtype), kind="ExternalInput").ap())
    args.append(nc.dram_tensor("out", (B, T, D), F32, kind="ExternalOutput").ap())
    build(nc, *args)
    r = run_bass_kernel_spmd(nc, [arrays], core_ids=[0])
    return r.results[0]["out"]
```

```python
from contextlib import ExitStack

import concourse.bass as bass
from concourse import mybir

F32 = mybir.dt.float32
F32R = mybir.dt.float32r
BF16 = mybir.dt.bfloat16
U32 = mybir.dt.uint32
I32 = mybir.dt.int32
ALU = mybir.AluOpType
ACT = mybir.ActivationFunctionType
AX = mybir.AxisListType

P = 128
B, T, D = 8, 512, 128
CH = T // P
H, DH = 16, 64
PAIRS = H // 2
DV1 = DH + 1
NF = 4
F = NF * P
E = 8
TOKENS = B * T
EPS_LN = 1e-5
EPS_DEN = 1e-6

REGION = TOKENS + P
DUMMY = 10
ROW = 132
TILES = 72
RING = 8
EARLY = 40
AHEAD = 2
PAIR_ROWS = 2 * TOKENS
PAD_DEST = PAIR_ROWS
DUMMY_DEST = PAD_DEST + E * P
ZBUF = 4
WORK = 19
RESULTS = DUMMY_DEST + E * P
TWO_ROWS = 2 * T * (B - 2)


def build(nc, x_d, ln1_g, ln1_b, wq_d, wk_d, wv_d, wo_d, ln2_g, ln2_b, wf1_d, wf2_d,
          gate_w, gate_b, w1_d, b1_d, w2_d, b2_d, out_d):
    rows_d = nc.dram_tensor("routed_rows", (E * REGION + DUMMY * P, ROW), F32, kind="Internal").ap()
    res_d = nc.dram_tensor("expert_results", (RESULTS, D), F32, kind="Internal").ap()
    x3_d = nc.dram_tensor("moe_input", (TOKENS, D), F32, kind="Internal").ap()

    with ExitStack() as ctx:
        def sb(name, shape, dt=F32):
            return ctx.enter_context(nc.sbuf_tensor(name, shape, dt))

        def sem(name):
            return ctx.enter_context(nc.semaphore(name))

        wq = [sb(f"wq_{k}", [P, H * DH], F32R) for k in ("hi", "lo")]
        wk = [sb(f"wk_{k}", [P, H * DH], F32R) for k in ("hi", "lo")]
        wv = [sb(f"wv_{k}", [P, H * DH], F32R) for k in ("hi", "lo")]
        wo = [sb(f"wo_{k}", [P, PAIRS * D], F32R) for k in ("hi", "lo")]
        wf1 = [sb(f"wf1_{k}", [P, F], F32R) for k in ("hi", "lo")]
        wf2 = [sb(f"wf2_{k}", [P, F], F32R) for k in ("hi", "lo")]
        w1 = [sb(f"w1_{k}", [P, E * F], F32R) for k in ("hi", "lo")]
        w2 = sb("w2", [P, E * F])
        b1_rows = sb("b1_rows", [P, E * F])
        stage = sb("stage", [P, 2, F])
        b2_rows = stage[:, :, :].rearrange("p a f -> p (a f)")
        ident = sb("ident", [P, P])
        causal = sb("causal", [P, P])
        before = sb("before", [P, P], BF16)
        ones_b = sb("ones_b", [P, P], BF16)
        cols = sb("cols", [P, 4])
        neg_half = sb("neg_half", [P, CH])
        iota_e = sb("iota_e", [P, E])
        gw = sb("gw", [P, E])
        gb = sb("gb", [P, E])
        v_aug = sb("v_aug", [P, CH * H * DV1])
        va = v_aug[:, :].rearrange("p (c h j) -> p c h j", c=CH, h=H)
        hT = [[sb(f"hT{n}_{k}", [P, T], F32R) for k in ("hi", "lo")] for n in range(2)]
        h2T = [sb(f"h2T_{k}", [P, T], F32R) for k in ("hi", "lo")]
        gT = [sb(f"gT_{k}", [P, NF, T], F32R) for k in ("hi", "lo")]
        oT = [sb(f"oT_{k}", [P, T], F32R) for k in ("hi", "lo")]
        state = sb("state", [P, CH - 1, 2 * DV1])
        routed = sb("routed", [P, CH, 2, ROW])
        work = sb("work", [P, WORK * T])
        spot = [0]

        def take(n, back=None):
            if back is not None:
                spot[0] = back
            a = spot[0]
            spot[0] += n
            return work[:, a:a + n]

        def chunks(ap):
            return ap.rearrange("p (c d) -> p c d", c=CH)

        qT = [take(T) for _ in range(2)]
        kT = [take(T) for _ in range(2)]
        ktok = chunks(take(T))
        am = [chunks(take(T)) for _ in range(2)]
        on = chunks(take(T))
        e_q, e_k = take(T), take(T)
        xln = chunks(take(T))
        xres = chunks(take(T))
        h32 = take(T)
        g32 = [take(T) for _ in range(2)]
        behind = spot[0]
        x1 = chunks(take(T))
        xx1 = chunks(take(T))
        colT = take(T)
        pads = take(E * ROW, behind).rearrange("p (e w) -> p e w", e=E)
        assert EARLY * P <= TWO_ROWS - E * P
        xg = [take(ROW, 8 * T if n == 0 else None) for n in range(RING)]
        ring_end = spot[0]
        gt32 = take(E * 32).rearrange("p (e m) -> p e m", e=E)
        le = take(EARLY * E, ring_end).rearrange("p (t e) -> p t e", e=E)
        assert TILES + AHEAD - EARLY <= EARLY and spot[0] <= 11 * T
        hb = [take(F, 0 if n == 0 else None) for n in range(2)]
        hTe = [take(F) for _ in range(2)]
        yb = [take(D) for _ in range(2)]
        yw = [take(D) for _ in range(RING)]
        assert spot[0] <= 8 * T
        x3_all = take(B * T, ring_end)
        xc = x3_all.rearrange("p (b c d) -> p b c d", b=B, c=CH)
        assert spot[0] <= WORK * T
        z = [v_aug[:, n * 2 * T:(n + 1) * 2 * T].rearrange("p (c k d) -> p c k d", c=CH, k=2) for n in range(ZBUF)]
        sc = [chunks(take(T, 0 if n == 0 else None)) for n in range(2)]
        oc = [chunks(take(T)) for _ in range(2)]
        zs = [chunks(take(T)) for _ in range(2)]
        xT = [[sb(f"xT{n}_{k}", [P, P], F32R) for k in ("hi", "lo")] for n in range(2)]
        stats = [sb(f"stats{n}", [P, CH, 6]) for n in range(3)]
        mv = [sb(f"mv{n}", [P, CH, 2]) for n in range(3)]
        ve = [sb(f"ve{n}", [P, CH]) for n in range(3)]
        rstd = [sb(f"rstd{n}", [P, CH]) for n in range(3)]
        den = sb("den", [P, 4])
        rden = sb("rden", [P, 4])
        lg = sb("lg", [P, CH, E])
        lmax = sb("lmax", [P, CH])
        pe_ = sb("gate_exp", [P, CH, E])
        top = sb("top", [P, CH, 8])
        topi = sb("topi", [P, CH, 8], U32)
        wsum = sb("wsum", [P, CH])
        onehot = sb("onehot", [P, 2, CH, E])
        chosen = sb("chosen", [P, CH, E], BF16)
        base = sb("base", [P, E])
        rank = sb("rank", [P, CH, E])
        prod = sb("prod", [P, 2, CH, E])
        slot_f = sb("slot_f", [P, 2, CH])
        slot = sb("slot", [P, 2, CH], U32)
        dest = sb("dest", [P, CH, 2])
        cnt = sb("cnt", [P, E])
        early = sb("early", [P, E + 1])
        low_c = sb("low_c", [P, E])
        high_c = sb("high_c", [P, E])
        nt = sb("nt", [P, E])
        ntc = sb("ntc", [P, E])
        one_e = sb("one_e", [P, E])
        m32 = sb("m32", [P, 32])
        tidx = sb("tidx", [P, TILES + AHEAD])
        en = sb("en", [P, TILES + AHEAD])
        cx = sb("cx", [P, TILES + AHEAD])
        tile_e = sb("tile_e", [P, TILES + AHEAD], I32)
        tile_r = sb("tile_r", [P, TILES + AHEAD], I32)
        padi = sb("padi", [P, E], U32)
        pcol = sb("pcol", [P, 1])
        padf = sb("padf", [P, 2 * E])
        rs_c = [sb(f"rs_c{n}", [P, CH]) for n in range(2)]
        nmr = [sb(f"nmr{n}", [P, CH]) for n in range(2)]

        bank = [ctx.enter_context(nc.psum_tensor(f"bank{n}", [P, 512], F32)) for n in range(8)]
        bkA, bkB, bkC, bkE, bkF, bkG, bkH, bkY = bank

        ld_stage = [sem(f"ld_stage{n}") for n in range(2)]
        ld_wq, ld_wk, ld_wvo, ld_small, ld_w2_b1, ld_b2 = (
            sem(n) for n in ("ld_wq", "ld_wk", "ld_wvo", "ld_small", "ld_w2_b1", "ld_b2"))
        ld_xln, ld_xres = sem("ld_xln"), sem("ld_xres")
        cst, cst_dve, whi, wlo, w1hi, w1lo = (sem(n) for n in ("cst", "cst_dve", "whi", "wlo", "w1hi", "w1lo"))
        q_mm, k_mm, v_mm, sc_mm, kt_mm, u_mm, o_mm, ot_mm, wo_mm = (
            sem(n) for n in ("q_mm", "k_mm", "v_mm", "sc_mm", "kt_mm", "u_mm", "o_mm", "ot_mm", "wo_mm"))
        q_relu, q_exp, k_relu, k_exp, v_sb, kt_sb, ot_hi, yT_sb = (
            sem(n) for n in ("q_relu", "q_exp", "k_relu", "k_exp", "v_sb", "kt_sb", "ot_hi", "yT_sb"))
        q_phi, k_phi, a_msk, s_part, s_sb, o_den, o_sb, ot_lo = (
            sem(n) for n in ("q_phi", "k_phi", "a_msk", "s_part", "s_sb", "o_den", "o_sb", "ot_lo"))
        ln_st, ln_mv, ln_ve, ln_r, ln_x = ([sem(f"{a}{n}") for n in range(3)]
                                           for a in ("ln_st", "ln_mv", "ln_ve", "ln_r", "ln_x"))
        f1_mm, yt_mm, h2_mm, ff1_mm, ff2_mm, y2_mm, x3_mm, gate_mm, rank_mm = (
            sem(n) for n in ("f1_mm", "yt_mm", "h2_mm", "ff1_mm", "ff2_mm", "y2_mm", "x3_mm", "gate_mm", "rank_mm"))
        h32_sb, h_hi, h_lo, x1_sb, xx_sb, h232_sb, h2_hi, h2_lo, gelu_sb, g_hi, g_lo = (
            sem(n) for n in ("h32_sb", "h_hi", "h_lo", "x1_sb", "xx_sb", "h232_sb", "h2_hi", "h2_lo", "gelu_sb",
                             "g_hi", "g_lo"))
        y2_sb, s3_sb, x3T_sb, lg_sb, lg_st, ex_sb, tp, rk, cnt_sb, rt_sb, dup_sb, x3_st, sct = (
            sem(n) for n in ("y2_sb", "s3_sb", "x3T_sb", "lg_sb", "lg_st", "ex_sb", "tp", "rk", "cnt_sb", "rt_sb", "dup_sb",
                             "x3_st", "sct"))
        plan, nh_set, pads_dmy, dmy_st, pad_st = (sem(n) for n in ("plan", "nh_set", "pads_dmy", "dmy_st", "pad_st"))
        ld_xg = [sem(f"ld_xg{n}") for n in range(RING)]
        res_st = [sem(f"res_st{n}") for n in range(RING)]
        xt_mm, l1_mm, ht_mm, l2_mm, xt_hi, xt_lo, hb_sb, ht_a, yb_sb, yw_sb = (
            sem(n) for n in ("xt_mm", "l1_mm", "ht_mm", "l2_mm", "xt_hi", "xt_lo", "hb_sb", "ht_a", "yb_sb",
                             "yw_sb"))
        ld_x3 = sem("ld_x3")
        ld_z = [sem(f"ld_z{n}") for n in range(ZBUF)]
        z_sum, c_sb, c_st, c_mv, c_ve, c_r, c_nm, c_out = (
            sem(n) for n in ("z_sum", "c_sb", "c_st", "c_mv", "c_ve", "c_r", "c_nm", "c_out"))
        out_st = [sem(f"out_st{n}") for n in range(2)]

        def x_of(b):
            return x_d[bass.ds(b, 1), :, :].rearrange("o (c p) d -> p (o c) d", p=P)

        CST_ALL = 15
        PLAN_EARLY = 17
        PLAN_DONE = PLAN_EARLY + 18
        TP_STEPS = 4
        RK_STEPS = 5

        def apart(eng):
            eng.wait_ge(nh_set, 1)

        block = ctx.enter_context(nc.Block())

        @block.sync
        def _(sp):
            sp.dma_start(xln, x_of(0)).then_inc(ld_xln, 16)
            sp.dma_start(v_aug[:, 0:1024], wq_d).then_inc(ld_wq, 16)
            sp.dma_start(v_aug[:, 1024:2048], wk_d).then_inc(ld_wk, 16)
            sp.dma_start(stage[:, 0, :], wf1_d).then_inc(ld_stage[0], 16)
            sp.dma_start(stage[:, 1, :].rearrange("p (t n) -> p t n", t=NF),
                         wf2_d.rearrange("(t p) n -> p t n", p=P)).then_inc(ld_stage[1], 16)
            def sequence(b, first, last):
                if not last:
                    sp.wait_ge(f1_mm, b + 1)
                    sp.dma_start(xln, x_of(b + 1)).then_inc(ld_xln, 16)
                if not first:
                    sp.wait_ge(xx_sb, b)
                sp.dma_start(xres, x_of(b)).then_inc(ld_xres, 16)
                if not first and not last:
                    store_x3(b - 1)

            def store_x3(b):
                sp.wait_ge(ln_x[2], b + 1)
                sp.dma_start(x3_d[bass.ds(b * T, T), :].rearrange("(c p) d -> p c d", p=P),
                             routed[:, :, 0, 0:D]).then_inc(x3_st, 16)

            sequence(0, True, False)
            sp.wait_ge(wlo, 6)
            for e in range(2):
                sp.dma_start(stage[:, e, :], w1_d[e]).then_inc(ld_stage[e], 16)
            sp.dma_start(w2[:, :].rearrange("p (e t n) -> p e t n", e=E, t=NF),
                         w2_d.rearrange("e (t p) n -> p e t n", p=P)).then_inc(ld_w2_b1, 16)
            sp.dma_start(b1_rows[:, :], b1_d.rearrange("e f -> (e f)").partition_broadcast(P)).then_inc(ld_w2_b1, 16)
            with sp.Fori(1, B - 1) as b:
                sequence(b, False, False)
            sequence(B - 1, False, True)
            for e in range(2, E):
                sp.wait_ge(w1lo, e - 1)
                sp.dma_start(stage[:, e % 2, :], w1_d[e]).then_inc(ld_stage[e % 2], 16)
            store_x3(B - 2)

            def load_tile(t0, n, reuse):
                at = sp.value_load(tile_r[0:1, bass.ds(t0 + n, 1)], min_val=0, max_val=E * REGION + (DUMMY - 1) * P)
                if reuse:
                    sp.wait_ge(res_st[n], t0 * (16 // RING))
                sp.dma_start(xg[n], rows_d[bass.ds(at, P), :]).then_inc(ld_xg[n], 16)

            sp.wait_ge(plan, PLAN_EARLY)
            sp.wait_ge(sct, 16 * 2 * CH * (B - 2))
            sp.wait_ge(k_phi, PAIRS * B)
            for t in range(EARLY):
                load_tile(t - t % RING, t % RING, t >= RING)
                if t == RING - 1:
                    sp.wait_ge(w1lo, E)
                    sp.dma_start(b2_rows, b2_d.rearrange("e f -> (e f)").partition_broadcast(P)).then_inc(ld_b2, 16)
                if t == 28:
                    store_x3(B - 1)

            sp.wait_ge(plan, PLAN_DONE)
            for e in range(E):
                at = sp.value_load(padi[0:1, e:e + 1], min_val=0, max_val=E * REGION - P)
                sp.dma_start(rows_d[bass.ds(at, P), :], pads[:, e, :]).then_inc(pad_st, 16)
            sp.wait_ge(sct, 16 * 2 * CH * B)
            sp.wait_ge(pad_st, 16 * E)
            sp.wait_ge(dmy_st, 32)
            for n in range(RING):
                load_tile(EARLY, n, True)
            with sp.Fori(EARLY + RING, TILES - RING + 1, RING) as t:
                for n in range(RING):
                    load_tile(t, n, True)
            for n in range(AHEAD):
                load_tile(TILES, n, True)

            for n in range(RING):
                sp.wait_ge(res_st[n], 16 * (TILES // RING))

            def load_group(i):
                if i >= ZBUF:
                    sp.wait_ge(z_sum, i - ZBUF + 1)
                sp.dma_start(z[i % ZBUF], res_d[i * 2 * T:(i + 1) * 2 * T, :].rearrange(
                    "(c p k) d -> p c k d", p=P, k=2)).then_inc(ld_z[i % ZBUF], 16)

            def store_group(i):
                sp.wait_ge(c_out, (i + 1) * CH)
                sp.dma_start(out_d[i].rearrange("(c p) d -> p c d", p=P), oc[i % 2]).then_inc(out_st[i % 2], 16)

            for i in range(B + ZBUF):
                if i < B:
                    load_group(i)
                if i >= ZBUF:
                    store_group(i - ZBUF)
            for n in range(2):
                sp.wait_ge(out_st[n], 16 * (B // 2))

        @block.tensor
        def _(pe):
            def split3(out, w, wcols, m, mcols, first=True, last=True):
                pe.matmul(out, w[0][:, wcols], m[0][:, mcols], start=first, stop=False)
                pe.matmul(out, w[1][:, wcols], m[0][:, mcols], start=False, stop=False)
                return pe.matmul(out, w[0][:, wcols], m[1][:, mcols], start=False, stop=last)

            def blk(c, n=P):
                return slice(c * n, (c + 1) * n)

            ALLT = slice(0, T)

            def turn(out, src):
                for c in range(CH):
                    mm = pe.transpose(out[:, blk(c)], src(c), ident[:, :])
                return mm

            def q_proj(par, p):
                split3(bkA[:, :], wq, blk(p), hT[par], ALLT).then_inc(q_mm, 1)

            def k_proj_high(par, p):
                pe.matmul(bkB[:, :], wk[0][:, blk(p)], hT[par][0][:, ALLT], start=True, stop=False)

            def k_proj_rest(par, p):
                pe.matmul(bkB[:, :], wk[1][:, blk(p)], hT[par][0][:, ALLT], start=False, stop=False)
                pe.matmul(bkB[:, :], wk[0][:, blk(p)], hT[par][1][:, ALLT], start=False, stop=True).then_inc(k_mm, 1)

            def v_proj(par, half, c, bk=bkC):
                h, out = hT[par], bk[:, :]
                pe.matmul(out, h[0][:, blk(c)], wv[0][:, blk(half, 512)], start=True, stop=False)
                pe.matmul(out, h[1][:, blk(c)], wv[0][:, blk(half, 512)], start=False, stop=False)
                pe.matmul(out, h[0][:, blk(c)], wv[1][:, blk(half, 512)], start=False, stop=True).then_inc(v_mm, 1)

            def front_t(b):
                pe.wait_ge(ln_x[0], b + 1)
                turn(bkE, lambda c: xln[:, c, :]).then_inc(f1_mm, 1)

            def otr():
                turn(bkC, lambda c: on[:, c, :]).then_inc(ot_mm, 1)

            def wo_acc(p):
                split3(bkY[:, :], wo, blk(p), oT, ALLT, first=(p == 0), last=(p == PAIRS - 1)).then_inc(wo_mm, 1)

            def y_t(b, out):
                pe.wait_ge(yT_sb, b + 1)
                turn(out, lambda c: colT[:, blk(c)]).then_inc(yt_mm, 1)

            def h2_t(b, out):
                pe.wait_ge(ln_x[1], b + 1)
                turn(out, lambda c: x1[:, c, :]).then_inc(h2_mm, 1)

            def ffn1(b, f, out):
                if f == 0:
                    pe.wait_ge(h2_lo, b + 1)
                split3(out[:, :], wf1, blk(f), h2T, ALLT).then_inc(ff1_mm, 1)

            def ffn2(b, out):
                for f in range(NF):
                    pe.wait_ge(g_lo, b * NF + f + 1)
                    g = [gT[0][:, f, :], gT[1][:, f, :]]
                    mm = split3(out[:, :], wf2, blk(f), g, ALLT, first=(f == 0), last=(f == NF - 1))
                mm.then_inc(ff2_mm, 1)

            def y2_t(b, out):
                pe.wait_ge(y2_sb, b + 1)
                turn(out, lambda c: colT[:, blk(c)]).then_inc(y2_mm, 1)

            def x3_t(b, out):
                pe.wait_ge(ln_x[2], b + 1)
                turn(out, lambda c: routed[:, c, 0, 0:D]).then_inc(x3_mm, 1)

            def gate(b, out):
                pe.wait_ge(x3T_sb, b + 1)
                for c in range(CH):
                    mm = pe.matmul(out[:, blk(c, E)], colT[:, blk(c)], gw[:, :], start=True, stop=True)
                mm.then_inc(gate_mm, 1)

            def ranks(b, out):
                pe.wait_ge(tp, (b + 1) * TP_STEPS)
                flat = chosen[:, :, :].rearrange("p c e -> p (c e)")
                pe.matmul(out[:, 0:CH * E], before[:, :], flat, start=True, stop=False)
                for c in range(1, CH):
                    pe.matmul(out[:, c * E:CH * E], ones_b[:, :], flat[:, 0:(CH - c) * E], start=False,
                              stop=(c == CH - 1))
                for c in range(CH):
                    mm = pe.matmul(out[:, CH * E:(CH + 1) * E], ones_b[:, :], chosen[:, c, :], start=(c == 0),
                                   stop=(c == CH - 1))
                mm.then_inc(rank_mm, 1)

            def step(b, par, p, first, last):
                g = b * PAIRS + p
                cur = p % 2
                begin = first and p == 0
                nxt = not (last and p == PAIRS - 1)
                npar = par if p < PAIRS - 1 else 1 - par

                pe.wait_ge(q_phi, g + 1)
                pe.wait_ge(k_phi, g + 1)
                if p == 3 and not last:
                    pe.wait_ge(h32_sb, b + 2)
                f_read = []
                if not first:
                    e_read = {2: [(x1_sb, b)], 4: [(gelu_sb, b * NF - 2)], 6: [(s3_sb, b)], 7: [(x3T_sb, b)]}.get(p, [])
                    f_read = {0: [(cnt_sb, b)], 3: [(h232_sb, b)], 5: [(y2_sb, b)], 7: [(lg_sb, b)]}.get(p, [])
                    for what, count in e_read:
                        pe.wait_ge(what, count)
                for h in range(2):
                    if h == 1:
                        for what, count in f_read:
                            pe.wait_ge(what, count)
                    hs = slice(h * DH, (h + 1) * DH)
                    for c in range(CH):
                        mm = pe.matmul((bkE, bkF)[h][:, blk(c)], kT[cur][hs, blk(c)], qT[cur][hs, blk(c)],
                                       start=True, stop=True)
                    mm.then_inc(sc_mm, 1)
                pe.wait_ge(v_sb, 2 * CH * B if last and p > CH else CH + g)
                turn(bkC, lambda c: kT[cur][:, blk(c)]).then_inc(kt_mm, 1)
                if p == 4 and not first:
                    pe.wait_ge(gelu_sb, b * NF)
                if nxt:
                    q_proj(npar, (p + 1) % PAIRS)
                    k_proj_high(npar, (p + 1) % PAIRS)
                pe.wait_ge(a_msk, 2 * g + 2)
                pe.wait_ge(kt_sb, g + 1)
                pe.wait_ge(v_sb, 2 * CH * b + (CH if p < PAIRS // 2 else 2 * CH))
                for c in range(CH - 1):
                    for h in range(2):
                        hs = slice(h * DH, (h + 1) * DH)
                        mm = pe.matmul(bkF[hs, blk(c, DV1)], ktok[:, c, hs],
                                       va[:, c, 2 * p + h, :], start=True, stop=True)
                mm.then_inc(u_mm, 1)
                if nxt:
                    k_proj_rest(npar, (p + 1) % PAIRS)
                if not begin:
                    pe.wait_ge(o_sb, 2 * g)
                    otr()

                def outputs(c, out):
                    if c > 0:
                        pe.matmul(out[:, 0:2 * DV1], qT[cur][:, blk(c)], state[:, c - 1, :], start=True, stop=False)
                    for h in range(2):
                        mm = pe.matmul(out[:, blk(h, DV1)], am[h][:, c, :], va[:, c, 2 * p + h, :],
                                       start=(c == 0), stop=(c == 0 or h == 1))
                    return mm

                outputs(0, bkG[:, 0:130])
                if not first:
                    if p == 1:
                        y_t(b - 1, bkE)
                    if p == 3:
                        ffn1(b - 1, 0, bkE)
                    if p == 5:
                        y2_t(b - 1, bkE)
                    if p == 6:
                        x3_t(b - 1, bkE)
                pe.wait_ge(s_sb, g + 1)
                if not first and p == 3:
                    ffn1(b - 1, 1, bkF)
                outputs(1, bkG[:, 130:260]).then_inc(o_mm, 1)
                outputs(2, bkH[:, 0:130])
                outputs(3, bkH[:, 130:260]).then_inc(o_mm, 1)
                if p == 2 and not last:
                    front_t(b + 1)
                if p == 6 and not first:
                    gate(b - 1, bkF)
                if not begin:
                    pe.wait_ge(ot_lo, g)
                    if p == 1 and not first:
                        pe.wait_ge(yT_sb, b)
                    wo_acc((p - 1) % PAIRS)
                if not first:
                    if p == 2:
                        h2_t(b - 1, bkF)
                    if p == 4:
                        ffn2(b - 1, bkF)
                if p < CH:
                    v_proj(par, 1, p)
                elif not last:
                    pe.wait_ge(h_lo, b + 2)
                    v_proj(1 - par, 0, p - CH)
                if p == 7 and not first:
                    ranks(b - 1, bkF)
                if p == 3 and not first:
                    pe.wait_ge(q_phi, g + 2)
                    ffn1(b - 1, 2, bkA)
                    pe.wait_ge(k_phi, g + 2)
                    ffn1(b - 1, 3, bkB)

            def sequence(b, par, first, last):
                for p in range(PAIRS):
                    step(b, par, p, first, last)

            pe.wait_ge(cst, 2)
            front_t(0)
            pe.wait_ge(cst, CST_ALL)
            pe.wait_ge(h_lo, 1)
            pe.wait_ge(wlo, 1)
            q_proj(0, 0)
            pe.wait_ge(wlo, 2)
            k_proj_high(0, 0)
            k_proj_rest(0, 0)
            pe.wait_ge(wlo, 3)
            for c in range(CH):
                v_proj(0, 0, c, (bkC, bkE, bkF, bkG)[c])
            pe.wait_ge(v_sb, CH)
            sequence(0, 0, True, False)
            with pe.Fori(1, B - 2, 2) as b:
                sequence(b, 1, False, False)
                sequence(b + 1, 0, False, False)
            sequence(B - 1, 1, False, True)

            X, L, M, Y, R, S = bank[0], bank[2:4], bank[4:6], bank[6], bank[1], bank[7]

            def expert(t):
                return pe.value_load(tile_e[0:1, bass.ds(t, 1)], min_val=0, max_val=E - 1)

            def later(t, k):
                return not isinstance(t, int) or t >= k

            def rows_t(t0, n):
                if n >= RING:
                    t0, n = t0 + RING, n - RING
                if later(t0 + n, 1):
                    pe.wait_ge(xt_lo, t0 + n)
                pe.wait_ge(ld_xg[n], t0 * (16 // RING) + 16)
                pe.transpose(X[:, 0:P], xg[n][:, 0:D], ident[:, :]).then_inc(xt_mm, 1)

            def layer1(t, n, e):
                if later(t, 2):
                    pe.wait_ge(hb_sb, t - 1)
                pe.wait_ge(xt_lo, t + 1)
                a, out = xT[n % 2], L[n % 2][:, :]
                pe.matmul(out, a[0][:, :], w1[0][:, bass.ds(e * F, F)], start=True, stop=False)
                pe.matmul(out, a[1][:, :], w1[0][:, bass.ds(e * F, F)], start=False, stop=False)
                pe.matmul(out, a[0][:, :], w1[1][:, bass.ds(e * F, F)], start=False, stop=True).then_inc(l1_mm, 1)

            def hidden_t(t, n):
                if later(t, 2):
                    pe.wait_ge(ht_a, t - 1)
                pe.wait_ge(hb_sb, t + 1)
                for f in range(NF):
                    mm = pe.transpose(M[n % 2][:, blk(f)], hb[n % 2][:, blk(f)], ident[:, :])
                mm.then_inc(ht_mm, 1)

            def layer2(t, n, e):
                if later(t, 1):
                    pe.wait_ge(yb_sb, t)
                pe.wait_ge(ht_a, t + 1)
                for f in range(NF):
                    mm = pe.matmul(Y[:, 0:D], hTe[n % 2][:, blk(f)], w2[:, bass.ds(e * F + f * D, D)],
                                   start=(f == 0), stop=(f == NF - 1))
                mm.then_inc(l2_mm, 1)

            b = B - 1

            def ffn1_first():
                ffn1(b, 0, R)
                ffn1(b, 1, S)

            def ffn1_second():
                pe.wait_ge(gelu_sb, b * NF + 2)
                ffn1(b, 2, R)
                ffn1(b, 3, S)

            def ffn2_tail():
                pe.wait_ge(gelu_sb, (b + 1) * NF)
                ffn2(b, R)

            def x3_tail():
                pe.wait_ge(y2_sb, B)
                x3_t(b, R)

            def gate_tail():
                pe.wait_ge(s3_sb, B)
                gate(b, S)

            tail = {0: lambda: y_t(b, R), 6: lambda: h2_t(b, S), 9: ffn1_first, 11: ffn1_second, 15: ffn2_tail,
                    17: lambda: y2_t(b, S), 22: x3_tail, 24: gate_tail, 28: lambda: ranks(b, R)}

            pe.wait_ge(plan, PLAN_EARLY)
            e = {0: expert(0)}
            rows_t(0, 0)
            pe.wait_ge(o_sb, 2 * B * PAIRS)
            otr()
            rows_t(0, 1)
            pe.wait_ge(ot_lo, B * PAIRS)
            wo_acc(PAIRS - 1)
            pe.wait_ge(cnt_sb, B)
            pe.wait_ge(ld_w2_b1, 32)
            pe.wait_ge(w1lo, E)
            layer1(0, 0, e[0])
            for t in range(EARLY):
                t0, n = t - t % RING, t % RING
                if t + 1 < EARLY:
                    e[t + 1] = expert(t + 1)
                if t + 2 < EARLY:
                    rows_t(t0, n + 2)
                if t + 1 < EARLY:
                    layer1(t + 1, n + 1, e[t + 1])
                hidden_t(t, n)
                if t > 0:
                    layer2(t - 1, n - 1, e[t - 1])
                if t in tail:
                    tail[t]()

            pe.wait_ge(plan, PLAN_DONE)
            rows_t(EARLY, 0)
            rows_t(EARLY, 1)
            layer1(EARLY, 0, expert(EARLY))
            with pe.Fori(EARLY, TILES - RING + 1, RING) as t0:
                e = {}
                for n in range(RING):
                    e[n + 1] = expert(t0 + n + 1)
                    rows_t(t0, n + 2)
                    layer1(t0 + n + 1, n + 1, e[n + 1])
                    hidden_t(t0 + n, n)
                    if n < 2:
                        e[n - 1] = expert(t0 + n - 1)
                    layer2(t0 + n - 1, n - 1, e[n - 1])
            layer2(TILES - 1, RING - 1, expert(TILES - 1))

        @block.scalar
        def _(act):
            def copy(out, src):
                return act.activation(out, src, ACT.Copy)

            def y_copy(b):
                act.wait_ge(wo_mm, PAIRS * (b + 1))
                copy(colT, bkY[:, :]).then_inc(yT_sb, 1)

            def front_scale(b, reuse):
                act.wait_ge(f1_mm, b + 1)
                if reuse:
                    act.wait_ge(h_lo, b)
                act.activation(h32, bkE[:, :], ACT.Identity, bias=cols[:, 1:2], scale=cols[:, 0:1]).then_inc(h32_sb, 1)

            def front_high(b, par):
                act.wait_ge(h32_sb, b + 1)
                copy(hT[par][0][:, :], h32).then_inc(h_hi, 1)

            def scale2(b, src, fronts):
                act.wait_ge(h2_mm, b + 1)
                act.wait_ge(h_lo, fronts)
                act.activation(h32, src[:, :], ACT.Identity, bias=cols[:, 3:4], scale=cols[:, 2:3]).then_inc(h232_sb, 1)

            def h2_copy(b):
                act.wait_ge(h232_sb, b + 1)
                copy(h2T[0][:, :], h32).then_inc(h2_hi, 1)

            def gelus(b, fs, banks):
                for f in fs:
                    if f >= 2:
                        act.wait_ge(g_lo, b * NF + f - 1)
                    act.wait_ge(ff1_mm, b * NF + f + 1)
                    act.activation(g32[f % 2], banks[f][:, :], ACT.Gelu).then_inc(gelu_sb, 1)

            def y2_copy(b, src):
                act.wait_ge(ff2_mm, b + 1)
                copy(colT, src[:, :]).then_inc(y2_sb, 1)

            def x3_copy(b, src):
                act.wait_ge(x3_mm, b + 1)
                copy(colT, src[:, :]).then_inc(x3T_sb, 1)

            def gate_exp(b):
                act.wait_ge(lg_st, 2 * (b + 1))
                act.activation(pe_[:, :, :], lg[:, :, :], ACT.Exp).then_inc(ex_sb, 1)

            def ot_high(g):
                act.wait_ge(ot_mm, g)
                copy(oT[0][:, :], bkC[:, :]).then_inc(ot_hi, 1)

            def q_exps(g):
                act.wait_ge(q_mm, g + 1)
                act.activation(e_q, bkA[:, :], ACT.Relu, scale=-1.0).then_inc(q_relu, 1)
                act.wait_ge(q_relu, g + 1)
                act.activation(e_q, e_q, ACT.Exp, scale=-1.0).then_inc(q_exp, 1)

            def k_exps(g):
                act.wait_ge(k_mm, g + 1)
                act.activation(e_k, bkB[:, :], ACT.Relu, scale=-1.0).then_inc(k_relu, 1)
                act.wait_ge(k_relu, g + 1)
                act.activation(e_k, e_k, ACT.Exp, scale=-1.0).then_inc(k_exp, 1)

            def v_copy(n, half, c, bk=bkC):
                act.wait_ge(v_mm, n)
                copy(va[:, c, half * 8:(half + 1) * 8, 0:DH],
                     bk[:, :].rearrange("p (h j) -> p h j", h=8)).then_inc(v_sb, 1)

            def step(b, par, p, first, last):
                g = b * PAIRS + p
                act.wait_ge(kt_mm, g + 1)
                copy(ktok, bkC[:, :].rearrange("p (c d) -> p c d", c=CH)).then_inc(kt_sb, 1)
                if not (last and p == PAIRS - 1):
                    act.wait_ge(q_phi, g + 1)
                    q_exps(g + 1)
                if not (first and p == 0):
                    ot_high(g)
                if not (last and p == PAIRS - 1):
                    act.wait_ge(k_phi, g + 1)
                    k_exps(g + 1)
                if p == 2 and not last:
                    front_scale(b + 1, True)
                    front_high(b + 1, 1 - par)
                if not first:
                    if p == 0:
                        y_copy(b - 1)
                    if p == 3:
                        gelus(b - 1, (0, 1), {0: bkE, 1: bkF})
                    if p == 2:
                        scale2(b - 1, bkF, B if last else b + 2)
                    if p == 4:
                        y2_copy(b - 1, bkF)
                    if p == 6:
                        x3_copy(b - 1, bkE)
                if p < CH:
                    v_copy(g + CH + 1, 1, p)
                elif not last:
                    v_copy(g + CH + 1, 0, p - CH)
                if not first:
                    if p == 2:
                        h2_copy(b - 1)
                    if p == 3:
                        gelus(b - 1, (2, 3), {2: bkA, 3: bkB})
                    if p == 6:
                        gate_exp(b - 1)
                if last:
                    act.wait_ge(ld_stage[p % 2], 16 * (p // 2 + 2))
                    copy(w1[0][:, p * F:(p + 1) * F], stage[:, p % 2, :]).then_inc(w1hi, 1)

            def sequence(b, par, first, last):
                for p in range(PAIRS):
                    step(b, par, p, first, last)

            act.dma_start(cols[:, 0:1], ln1_g.rearrange("(p o) -> p o", o=1)).then_inc(ld_small, 16)
            act.dma_start(cols[:, 1:2], ln1_b.rearrange("(p o) -> p o", o=1)).then_inc(ld_small, 16)
            act.dma_start(cols[:, 2:3], ln2_g.rearrange("(p o) -> p o", o=1)).then_inc(ld_small, 16)
            act.dma_start(cols[:, 3:4], ln2_b.rearrange("(p o) -> p o", o=1)).then_inc(ld_small, 16)
            act.dma_start(gw[:], gate_w).then_inc(ld_small, 16)
            act.dma_start(gb[:], gate_b.partition_broadcast(P)).then_inc(ld_small, 16)
            act.dma_start(v_aug[:, 2048:3072], wv_d).then_inc(ld_wvo, 16)
            act.dma_start(v_aug[:, 3072:4096].rearrange("p (t n) -> p t n", t=PAIRS),
                          wo_d.rearrange("(t p) n -> p t n", p=P)).then_inc(ld_wvo, 16)
            for n, w in enumerate((wq, wk, wv, wo)):
                act.wait_ge(*((ld_wq, 16), (ld_wk, 16), (ld_wvo, 32), (ld_wvo, 32))[n])
                copy(w[0][:, :], v_aug[:, n * 1024:(n + 1) * 1024]).then_inc(whi, 1)
                if n == 0:
                    act.wait_ge(ld_small, 16 * 6)
                    front_scale(0, False)
                    front_high(0, 0)
            for n, w in enumerate((wf1, wf2)):
                act.wait_ge(ld_stage[n], 16)
                copy(w[0][:, :], stage[:, n, :]).then_inc(whi, 1)
            q_exps(0)
            k_exps(0)
            act.wait_ge(cst_dve, 1)
            for c in range(CH):
                v_copy(c + 1, 0, c, (bkC, bkE, bkF, bkG)[c])
            sequence(0, 0, True, False)
            with act.Fori(1, B - 2, 2) as b:
                sequence(b, 1, False, False)
                sequence(b + 1, 0, False, False)
            sequence(B - 1, 1, False, True)

            X, M, R, S = bank[0], bank[4:6], bank[1], bank[7]
            b = B - 1

            def rows_hi(t, n):
                if not isinstance(t, int) or t >= 2:
                    act.wait_ge(l1_mm, t - 1)
                act.wait_ge(xt_mm, t + 1)
                copy(xT[n % 2][0][:, :], X[:, 0:P]).then_inc(xt_hi, 1)

            def hidden_relu(t, n):
                if not isinstance(t, int) or t >= 2:
                    act.wait_ge(l2_mm, t - 1)
                act.wait_ge(ht_mm, t + 1)
                act.activation(hTe[n % 2][:, 0:F], M[n % 2][:, 0:F], ACT.Relu).then_inc(ht_a, 1)

            def weigh(t, n):
                act.wait_ge(yb_sb, t + 1)
                act.activation(yw[n], yb[n % 2], ACT.Copy, scale=xg[n][:, D + 1:D + 2]).then_inc(yw_sb, 1)

            def h2_tail():
                scale2(b, S, B)
                h2_copy(b)

            tail = {7: h2_tail, 10: lambda: gelus(b, (0, 1), {0: R, 1: S}), 13: lambda: gelus(b, (2, 3), {2: R, 3: S}),
                    16: lambda: y2_copy(b, R), 23: lambda: x3_copy(b, R), 26: lambda: gate_exp(b)}

            rows_hi(0, 0)
            ot_high(B * PAIRS)
            rows_hi(1, 1)
            y_copy(b)
            for t in range(EARLY):
                if t + 2 < EARLY:
                    rows_hi(t + 2, (t + 2) % RING)
                hidden_relu(t, t % RING)
                if t > 0:
                    weigh(t - 1, (t - 1) % RING)
                if t in tail:
                    tail[t]()

            rows_hi(EARLY, 0)
            rows_hi(EARLY + 1, 1)
            act.wait_ge(x3_st, 16 * B)
            act.wait_ge(pad_st, 16 * E)
            act.wait_ge(plan, PLAN_DONE)
            for i in range(B):
                act.dma_start(xc[:, i, :, :], x3_d[i * T:(i + 1) * T, :].rearrange("(c p) d -> p c d", p=P)
                              ).then_inc(ld_x3, 16)
            with act.Fori(EARLY, TILES - RING + 1, RING) as t:
                for n in range(RING):
                    rows_hi(t + n + 2, (n + 2) % RING)
                    hidden_relu(t + n, n)
                    weigh(t + n - 1, (n - 1) % RING)
            weigh(TILES - 1, RING - 1)

            def group(i0, n, reuse):
                act.wait_ge(c_r, i0 * 2 + 2 * n + 2)
                if reuse:
                    act.wait_ge(out_st[n], i0 * 8)
                for c in range(CH):
                    act.activation(oc[n][:, c, :], sc[n][:, c, :], ACT.Identity, bias=nmr[n][:, c:c + 1],
                                   scale=rs_c[n][:, c:c + 1]).then_inc(c_out, 1)

            for n in range(2):
                group(0, n, False)
            with act.Fori(2, B - 1, 2) as i:
                for n in range(2):
                    group(i, n, True)

        @block.vector
        def _(dve):
            def f32(ap):
                return ap.bitcast(F32)

            def low(out, whole, high):
                return dve.tensor_tensor(out, whole, f32(high), ALU.subtract)

            def ln_stats(k, src, i):
                for c in range(CH):
                    ins = dve.bn_stats(stats[k][:, c, :], src[:, c, :])
                ins.then_inc(ln_st[k], 1)
                apart(dve)
                dve.wait_ge(ln_st[k], i + 1)
                for c in range(CH):
                    ins = dve.bn_aggr(mv[k][:, c, :], stats[k][:, c, :])
                ins.then_inc(ln_mv[k], 1)

            def ln_apply(k, out, src, i):
                dve.wait_ge(ln_r[k], i + 1)
                for c in range(CH):
                    ins = dve.tensor_scalar(out(c), src[:, c, :], mv[k][:, c, 0:1], rstd[k][:, c:c + 1],
                                            ALU.subtract, ALU.mult)
                ins.then_inc(ln_x[k], 1)

            def bank_chunks(bk):
                return bk[:, :].rearrange("p (c d) -> p c d", c=CH)

            def front_stats(b):
                dve.wait_ge(ld_xln, 16 * (b + 1))
                ln_stats(0, xln, b)

            def front_apply(b):
                ln_apply(0, lambda c: xln[:, c, :], xln, b)

            def front_low(b, par):
                dve.wait_ge(h_hi, b + 1)
                dve.wait_ge(h32_sb, b + 1)
                low(hT[par][1][:, :], h32, hT[par][0][:, :]).then_inc(h_lo, 1)

            def residual1(b, src):
                dve.wait_ge(yt_mm, b + 1)
                dve.wait_ge(ld_xres, 16 * (b + 1))
                dve.tensor_tensor(x1, bank_chunks(src), xres, ALU.add).then_inc(x1_sb, 1)

            def stats1(b):
                dve.wait_ge(x1_sb, b + 1)
                ln_stats(1, x1, b)

            def norm2(b):
                dve.wait_ge(xx_sb, b + 1)
                ln_apply(1, lambda c: x1[:, c, :], x1, b)

            def low2(b):
                dve.wait_ge(h2_hi, b + 1)
                dve.wait_ge(h232_sb, b + 1)
                low(h2T[1][:, :], h32, h2T[0][:, :]).then_inc(h2_lo, 1)

            def split_g(b, fs):
                for f in fs:
                    dve.wait_ge(gelu_sb, b * NF + f + 1)
                    dve.tensor_copy(gT[0][:, f, :], g32[f % 2]).then_inc(g_hi, 1)
                for f in fs:
                    dve.wait_ge(g_hi, b * NF + f + 1)
                    low(gT[1][:, f, :], g32[f % 2], gT[0][:, f, :]).then_inc(g_lo, 1)

            def residual2(b, src):
                dve.wait_ge(y2_mm, b + 1)
                dve.tensor_tensor(xx1, bank_chunks(src), xx1, ALU.add).then_inc(s3_sb, 1)

            def stats2(b):
                dve.wait_ge(s3_sb, b + 1)
                ln_stats(2, xx1, b)

            def norm3(b):
                ln_apply(2, lambda c: routed[:, c, 0, 0:D], xx1, b)

            def logits(b, src):
                dve.wait_ge(gate_mm, b + 1)
                dve.tensor_tensor(lg[:, :, :], src[:, 0:CH * E].rearrange("p (c e) -> p c e", c=CH),
                                  gb[:, :].unsqueeze(1).broadcast_to([P, CH, E]), ALU.add
                                  ).then_inc(lg_sb, 1)
                dve.wait_ge(lg_sb, b + 1)
                dve.tensor_reduce(lmax[:, :], lg[:, :, :], AX.X, ALU.max).then_inc(lg_st, 1)
                dve.wait_ge(lg_st, 2 * b + 1)
                dve.tensor_tensor(lg[:, :, :], lg[:, :, :], lmax[:, :].unsqueeze(2).broadcast_to([P, CH, E]),
                                  ALU.subtract).then_inc(lg_st, 1)

            def top2(b):
                apart(dve)
                dve.wait_ge(ex_sb, b + 1)
                for c in range(CH):
                    ins = dve.max(top[:, c, :], pe_[:, c, :])
                ins.then_inc(tp, 1)
                apart(dve)
                dve.wait_ge(tp, TP_STEPS * b + 1)
                for c in range(CH):
                    ins = dve.max_index(topi[:, c, :], top[:, c, :], pe_[:, c, :])
                dve.tensor_tensor(wsum[:, :], top[:, :, 0], top[:, :, 1], ALU.add).then_inc(tp, 1)
                dve.wait_ge(tp, TP_STEPS * b + 2)
                dve.reciprocal(wsum[:, :], wsum[:, :])
                for k in range(2):
                    ins = dve.tensor_tensor(onehot[:, k, :, :],
                                            topi[:, :, k:k + 1].broadcast_to([P, CH, E]),
                                            iota_e[:, :].unsqueeze(1).broadcast_to([P, CH, E]), ALU.is_equal)
                ins.then_inc(tp, 1)
                dve.wait_ge(tp, TP_STEPS * b + 3)
                dve.tensor_tensor(routed[:, :, :, D + 1], top[:, :, 0:2],
                                  wsum[:, :].unsqueeze(2).broadcast_to([P, CH, 2]), ALU.mult)
                dve.tensor_tensor(chosen[:, :, :], onehot[:, 0, :, :], onehot[:, 1, :, :], ALU.add).then_inc(tp, 1)

            def place(b, src):
                dve.wait_ge(rank_mm, b + 1)
                dve.tensor_tensor(rank[:, :, :], src[:, 0:CH * E].rearrange("p (c e) -> p c e", c=CH),
                                  base[:, :].unsqueeze(1).broadcast_to([P, CH, E]), ALU.add).then_inc(rk, 1)
                dve.tensor_copy(routed[:, :, :, D].bitcast(U32), dest[:, :, :]).then_inc(rk, 1)
                dve.wait_ge(rk, RK_STEPS * b + 1)
                dve.tensor_tensor(base[:, :], src[:, CH * E:(CH + 1) * E], base[:, :], ALU.add).then_inc(cnt_sb, 1)
                dve.tensor_tensor(prod[:, :, :, :], onehot[:, :, :, :],
                                  rank[:, :, :].unsqueeze(1).broadcast_to([P, 2, CH, E]), ALU.mult).then_inc(rk, 1)
                dve.wait_ge(rk, RK_STEPS * b + 2)
                dve.tensor_scalar(dest[:, :, :], dest[:, :, :], float(2 * T), None, ALU.add).then_inc(rk, 1)
                dve.wait_ge(rk, RK_STEPS * b + 3)
                dve.tensor_reduce(slot_f[:, :, :], prod[:, :, :, :], AX.X, ALU.add).then_inc(rk, 1)
                dve.wait_ge(rk, RK_STEPS * b + 5)
                dve.tensor_copy(slot[:, :, :], slot_f[:, :, :]).then_inc(rt_sb, 1)

            def phi(out, pre, e):
                return dve.scalar_tensor_tensor(out=out, in0=pre[:, :], scalar=0.0, in1=e, op0=ALU.max, op1=ALU.add)

            def q_phis(g, gp):
                dve.wait_ge(q_exp, g + 1)
                phi(qT[gp], bkA, e_q).then_inc(q_phi, 1)

            def k_phis(g, gp):
                dve.wait_ge(k_exp, g + 1)
                phi(kT[gp], bkB, e_k).then_inc(k_phi, 1)

            def ot_low(g):
                dve.wait_ge(ot_hi, g)
                low(oT[1][:, :], bkC[:, :], oT[0][:, :]).then_inc(ot_lo, 1)

            def normalise(g, bk, half):
                dve.wait_ge(o_mm, 2 * g + half + 1)
                o4 = bk[:, 0:4 * DV1].rearrange("p (x j) -> p x j", x=4)
                i = 4 * g + 2 * half
                dve.tensor_scalar(den[:, :], o4[:, :, DH], EPS_DEN, None, ALU.max).then_inc(o_den, 1)
                dve.wait_ge(o_den, i + 1)
                dve.reciprocal(rden[:, :], den[:, :]).then_inc(o_den, 1)
                dve.wait_ge(o_den, i + 2)
                dve.tensor_tensor(on[:, 2 * half:2 * half + 2, :].rearrange("p c (h j) -> p (c h) j", h=2),
                                  o4[:, :, 0:DH], rden[:, :].unsqueeze(2).broadcast_to([P, 4, DH]),
                                  ALU.mult).then_inc(o_sb, 1)

            def states(g):
                dve.wait_ge(u_mm, g + 1)
                for c in range(CH - 1):
                    for h in range(2):
                        hs, js = slice(h * DH, (h + 1) * DH), slice(h * DV1, (h + 1) * DV1)
                        u = bkF[hs, c * DV1:(c + 1) * DV1]
                        if c == 0:
                            ins = dve.tensor_copy(state[hs, 0, js], u)
                        else:
                            ins = dve.tensor_tensor(state[hs, c, js], u, state[hs, c - 1, js], ALU.add)
                    if c < CH - 2:
                        ins.then_inc(s_part, 1)
                        dve.wait_ge(s_part, 2 * g + c + 1)
                ins.then_inc(s_sb, 1)

            def step(b, par, p, first, last):
                g = b * PAIRS + p
                nxt = not (last and p == PAIRS - 1)
                for h in range(2):
                    dve.wait_ge(sc_mm, 2 * g + h + 1)
                    dve.tensor_tensor(am[h], bank_chunks((bkE, bkF)[h]),
                                      causal[:, :].unsqueeze(1).broadcast_to([P, CH, P]), ALU.mult).then_inc(a_msk, 1)
                if not first:
                    if p == 3:
                        low2(b - 1)
                    if p == 6:
                        norm3(b - 1)
                states(g)
                if nxt:
                    q_phis(g + 1, (p + 1) % 2)
                if p == 2 and not last:
                    front_apply(b + 1)
                if not (first and p == 0):
                    ot_low(g)
                if nxt:
                    k_phis(g + 1, (p + 1) % 2)
                if p == 7 and not first:
                    top2(b - 1)
                if p == 4 and not first:
                    split_g(b - 1, (2, 3))
                if not first:
                    if p == 1:
                        residual1(b - 1, bkE)
                        stats1(b - 1)
                    if p == 2:
                        norm2(b - 1)
                    if p == 5:
                        residual2(b - 1, bkE)
                        stats2(b - 1)
                normalise(g, bkG, 0)
                if p == 2 and not last:
                    front_low(b + 1, 1 - par)
                normalise(g, bkH, 1)
                if p == 0 and not last:
                    front_stats(b + 1)
                if p == 0 and last:
                    plan_early()
                if not first:
                    if p == 3:
                        split_g(b - 1, (0, 1))
                    if p == 6:
                        logits(b - 1, bkF)
                    if p == 7:
                        place(b - 1, bkF)
                if last:
                    dve.wait_ge(w1hi, p + 1)
                    low(w1[1][:, p * F:(p + 1) * F], stage[:, p % 2, :], w1[0][:, p * F:(p + 1) * F]).then_inc(w1lo, 1)

            planned = [0]

            def then(ins):
                planned[0] += 1
                ins.then_inc(plan, 1)
                dve.wait_ge(plan, planned[0])

            def tiles_by_expert():
                then(dve.tensor_tensor(gt32[:, :, :], cnt[:, :].unsqueeze(2).broadcast_to([P, E, 32]),
                                       m32[:, :].unsqueeze(1).broadcast_to([P, E, 32]), ALU.is_gt))
                then(dve.tensor_reduce(nt[:, :], gt32[:, :, :], AX.X, ALU.add))

            def experts_of(n, weight):
                lt, eb = le[:, 0:n, :], [P, n, E]
                then(dve.tensor_tensor(lt, ntc[:, :].unsqueeze(1).broadcast_to(eb),
                                       tidx[:, 0:n].unsqueeze(2).broadcast_to(eb), ALU.is_le))
                then(dve.tensor_reduce(en[:, 0:n], lt, AX.X, ALU.add))
                then(dve.tensor_tensor(lt, lt, weight.unsqueeze(1).broadcast_to(eb), ALU.mult))

            def rows_of(at, n):
                lt = le[:, 0:n, :]
                then(dve.tensor_reduce(cx[:, 0:n], lt, AX.X, ALU.add))
                then(dve.tensor_tensor(cx[:, 0:n], tidx[:, 0:n], cx[:, 0:n], ALU.subtract))
                if at > 0:
                    then(dve.tensor_scalar(cx[:, 0:n], cx[:, 0:n], early[:, 0:1], float(P), ALU.add, ALU.mult))
                else:
                    then(dve.tensor_scalar(cx[:, 0:n], cx[:, 0:n], float(P), None, ALU.mult))
                then(dve.scalar_tensor_tensor(out=tile_r[:, at:at + n], in0=en[:, 0:n], scalar=float(REGION),
                                              in1=cx[:, 0:n], op0=ALU.mult, op1=ALU.add))
                then(dve.tensor_scalar(tile_e[:, at:at + n], en[:, 0:n], float(E - 1), None, ALU.min))

            def plan_early():
                then(dve.scalar_tensor_tensor(out=cnt[:, :], in0=iota_e[:, :], scalar=-float(REGION), in1=base[:, :],
                                              op0=ALU.mult, op1=ALU.add))
                then(dve.tensor_scalar(cnt[:, :], cnt[:, :], -float(P - 1), None, ALU.add))
                tiles_by_expert()
                then(dve.tensor_tensor_scan(ntc[:, :], one_e[:, :], nt[:, :], 0.0, ALU.mult, ALU.add))
                experts_of(EARLY, nt[:, :])
                rows_of(0, EARLY)
                then(dve.tensor_tensor(low_c[:, :], ntc[:, :], nt[:, :], ALU.subtract))
                then(dve.tensor_scalar(low_c[:, :], low_c[:, :], float(EARLY), None, ALU.min))
                then(dve.tensor_scalar(high_c[:, :], ntc[:, :], float(EARLY), None, ALU.min))
                then(dve.tensor_tensor(early[:, 0:E], high_c[:, :], low_c[:, :], ALU.subtract))
                assert planned[0] == PLAN_EARLY

            def plan_counts():
                then(dve.scalar_tensor_tensor(out=cnt[:, :], in0=iota_e[:, :], scalar=-float(REGION), in1=base[:, :],
                                              op0=ALU.mult, op1=ALU.add))
                tiles_by_expert()
                then(dve.tensor_tensor(nt[:, :], nt[:, :], early[:, 0:E], ALU.subtract))
                then(dve.tensor_tensor_scan(ntc[:, :], one_e[:, :], nt[:, :], 0.0, ALU.mult, ALU.add))
                then(dve.tensor_tensor(low_c[:, :], early[:, 1:E + 1], early[:, 0:E], ALU.subtract))
                then(dve.tensor_tensor(high_c[:, :], nt[:, :], low_c[:, :], ALU.subtract))

            REST = TILES + AHEAD - EARLY

            def plan_padding():
                then(dve.memset(pads[:, :, :], 0.0))
                then(dve.tensor_copy(pads[:, :, D].bitcast(U32), padf[:, 0:E]))
                then(dve.tensor_scalar(padi[:, :], base[:, :], pcol[:, 0:1], None, ALU.add))
                assert planned[0] == PLAN_DONE, planned

            def sequence(b, par, first, last):
                for p in range(PAIRS):
                    step(b, par, p, first, last)

            dve.memset(state[:, :, :], 0.0)
            dve.memset(early[:, E:E + 1], 0.0)
            dve.memset(neg_half[:, :], -0.5).then_inc(nh_set, 1)
            dve.memset(den[:, :], 1.0).then_inc(cnt_sb, 1)
            front_stats(0)
            front_apply(0)
            for n, w in enumerate((wq, wk)):
                dve.wait_ge(whi, n + 1)
                low(w[1][:, :], v_aug[:, n * 1024:(n + 1) * 1024], w[0][:, :]).then_inc(wlo, 1)
                if n == 0:
                    front_low(0, 0)
            dve.wait_ge(cst, CST_ALL)
            dve.tensor_scalar(base[:, :], iota_e[:, :], float(REGION), None, ALU.mult)
            for n, w in ((2, wv), (3, wo)):
                dve.wait_ge(whi, n + 1)
                low(w[1][:, :], v_aug[:, n * 1024:(n + 1) * 1024], w[0][:, :]).then_inc(wlo, 1)
            dve.wait_ge(wlo, 4)
            dve.memset(va[:, :, :, DH:DV1], 1.0).then_inc(cst_dve, 1)
            q_phis(0, 0)
            k_phis(0, 0)
            for n, w in enumerate((wf1, wf2)):
                dve.wait_ge(whi, n + 5)
                low(w[1][:, :], stage[:, n, :], w[0][:, :]).then_inc(wlo, 1)
            dve.wait_ge(dmy_st, 32)
            sequence(0, 0, True, False)
            with dve.Fori(1, B - 2, 2) as b:
                sequence(b, 1, False, False)
                sequence(b + 1, 0, False, False)
            sequence(B - 1, 1, False, True)

            X, L, Y, R, S = bank[0], bank[2:4], bank[6], bank[1], bank[7]
            b = B - 1

            def expert(t):
                return dve.value_load(tile_e[0:1, bass.ds(t, 1)], min_val=0, max_val=E - 1)

            def rows_lo(t, k):
                dve.wait_ge(xt_hi, t + 1)
                low(xT[k % 2][1][:, :], X[:, 0:P], xT[k % 2][0][:, :]).then_inc(xt_lo, 1)

            def bias1(t, k, e):
                if not isinstance(t, int) or t >= 2:
                    dve.wait_ge(ht_mm, t - 1)
                dve.wait_ge(l1_mm, t + 1)
                dve.tensor_tensor(hb[k % 2], L[k % 2][:, :], b1_rows[:, bass.ds(e * F, F)], ALU.add).then_inc(hb_sb, 1)

            def bias2(t, k, e):
                if not isinstance(t, int) or t >= 2:
                    dve.wait_ge(yw_sb, t - 1)
                dve.wait_ge(l2_mm, t + 1)
                dve.tensor_tensor(yb[k % 2], Y[:, 0:D], b2_rows[:, bass.ds(e * D, D)], ALU.add).then_inc(yb_sb, 1)

            tail = {1: lambda: residual1(b, R), 2: lambda: stats1(b), 5: lambda: norm2(b), 8: lambda: low2(b),
                    11: lambda: split_g(b, (0, 1)), 14: lambda: split_g(b, (2, 3)), 18: lambda: residual2(b, S), 19: lambda: stats2(b),
                    21: lambda: norm3(b), 25: lambda: logits(b, S), 27: lambda: top2(b), 29: lambda: place(b, R),
                    30: plan_counts,
                    31: lambda: experts_of(REST, high_c[:, :]), 32: lambda: rows_of(EARLY, REST), 33: plan_padding}

            e = {0: expert(0)}
            rows_lo(0, 0)
            ot_low(B * PAIRS)
            rows_lo(1, 1)
            dve.wait_ge(ld_w2_b1, 32)
            dve.wait_ge(ld_b2, 16)
            bias1(0, 0, e[0])
            for t in range(EARLY):
                if t + 1 < EARLY:
                    e[t + 1] = expert(t + 1)
                if t + 2 < EARLY:
                    rows_lo(t + 2, t)
                if t + 1 < EARLY:
                    bias1(t + 1, t + 1, e[t + 1])
                if t > 0:
                    bias2(t - 1, t - 1, e[t - 1])
                if t in tail:
                    tail[t]()

            rows_lo(EARLY, 0)
            rows_lo(EARLY + 1, 1)
            bias1(EARLY, 0, expert(EARLY))
            with dve.Fori(EARLY, TILES - RING + 1, RING) as t0:
                e = {}
                for k in range(RING):
                    e[k + 1] = expert(t0 + k + 1)
                    rows_lo(t0 + k + 2, k)
                    bias1(t0 + k + 1, k + 1, e[k + 1])
                    if k < 2:
                        e[k - 1] = expert(t0 + k - 1)
                    bias2(t0 + k - 1, k - 1, e[k - 1])
            bias2(TILES - 1, RING - 1, expert(TILES - 1))

            def group(i, k, reuse):
                if reuse:
                    dve.wait_ge(c_out, (i - 1) * CH)
                dve.wait_ge(z_sum, i + 1)
                x3_of = chunks(x3_all[:, bass.ds(i * T, T)])
                dve.tensor_tensor(sc[k], x3_of, zs[k], ALU.add).then_inc(c_sb, 1)
                dve.wait_ge(c_sb, i + 1)
                for c in range(CH):
                    ins = dve.bn_stats(stats[k][:, c, :], sc[k][:, c, :])
                ins.then_inc(c_st, 1)
                apart(dve)
                dve.wait_ge(c_st, i + 1)
                for c in range(CH):
                    ins = dve.bn_aggr(mv[k][:, c, :], stats[k][:, c, :])
                ins.then_inc(c_mv, 1)
                dve.wait_ge(c_mv, i + 1)
                dve.tensor_scalar(nmr[k][:, :], mv[k][:, :, 0], -1.0, None, ALU.mult).then_inc(c_nm, 1)

            dve.wait_ge(ld_x3, 16 * B)
            group(0, 0, False)
            group(1, 1, False)
            with dve.Fori(2, B - 1, 2) as i:
                for k in range(2):
                    group(i + k, k, True)

        @block.gpsimd
        def _(pool):
            def count(v):
                return v if isinstance(v, int) else pool.snap(pool.to_reg(v))

            def rstds(k, i):
                nth = count(i + 1)
                apart(pool)
                pool.wait_ge(ln_mv[k], nth)
                pool.tensor_scalar(ve[k][:, :], mv[k][:, :, 1], EPS_LN, 1.0, ALU.add, ALU.mult).then_inc(ln_ve[k], 1)
                apart(pool)
                pool.wait_ge(ln_ve[k], nth)
                pool.tensor_tensor(rstd[k][:, :], ve[k][:, :], neg_half[:, :], ALU.pow).then_inc(ln_r[k], 1)

            def twice(b):
                nth = count(b + 1)
                apart(pool)
                pool.wait_ge(x1_sb, nth)
                pool.tensor_tensor(xx1, x1, xres, ALU.add).then_inc(xx_sb, 1)

            def duplicate(b):
                nth = count(b + 1)
                apart(pool)
                pool.wait_ge(ln_x[2], nth)
                pool.tensor_copy(routed[:, :, 1, 0:D], routed[:, :, 0, 0:D]).then_inc(dup_sb, 1)

            def scatter_chunk(b, c):
                if c == 0:
                    nth, stored = count(b + 1), count(16 * (b + 1))
                    apart(pool)
                    pool.wait_ge(rt_sb, nth)
                    pool.wait_ge(dup_sb, nth)
                    pool.wait_ge(x3_st, stored)
                for k in range(2):
                    pool.indirect_dma_start(rows_d, bass.IndirectOffsetOnAxis(slot[:, k, c:c + 1], 0),
                                            routed[:, c, k, :], None).then_inc(sct, 16)

            def scatter(b):
                duplicate(b)
                for c in range(CH):
                    scatter_chunk(b, c)
                pool.wait_ge(sct, count(2 * CH * 16 * (b + 1)))

            pool.wait_ge(nh_set, 1)
            n = [0]

            def then(ins, wait=True):
                n[0] += 1
                ins.then_inc(cst, 1)
                if wait:
                    pool.wait_ge(cst, n[0])

            then(pool.memset(ident[:, :], 0.0))
            then(pool.affine_select(out=ident[:, :], in_=ident[:, :], compare_op=ALU.not_equal, fill=1.0, base=0,
                                    pattern=[[-1, P]], channel_multiplier=1), False)
            rstds(0, 0)
            then(pool.memset(causal[:, :], 1.0))
            then(pool.affine_select(out=causal[:, :], in_=causal[:, :], compare_op=ALU.is_ge, fill=0.0, base=0,
                                    pattern=[[1, P]], channel_multiplier=-1), False)
            then(pool.memset(ones_b[:, :], 1.0))
            then(pool.affine_select(out=before[:, :], in_=ones_b[:, :], compare_op=ALU.is_gt, fill=0.0, base=0,
                                    pattern=[[1, P]], channel_multiplier=-1), False)
            fl = dict(allow_small_or_imprecise_dtypes=True)
            then(pool.iota(iota_e[:, :], [[1, E]], base=0, channel_multiplier=0, **fl), False)
            then(pool.iota(dest[:, :, :], [[2 * P, CH], [1, 2]], base=0, channel_multiplier=2, **fl), False)
            then(pool.iota(m32[:, :], [[P, 32]], base=0, channel_multiplier=0, **fl), False)
            then(pool.iota(tidx[:, :], [[1, TILES + AHEAD]], base=0, channel_multiplier=0, **fl), False)
            then(pool.iota(pcol[:, :], [[0, 1]], base=0, channel_multiplier=1, **fl), False)
            then(pool.iota(padf[:, :], [[P, 2 * E]], base=PAD_DEST, channel_multiplier=1, **fl), False)
            then(pool.memset(one_e[:, :], 1.0), False)
            then(pool.memset(routed[:, :, :, D + 2:ROW], 0.0), False)
            then(pool.memset(pads[:, :, :], 0.0), False)
            pool.wait_ge(cst, n[0])
            assert n[0] == CST_ALL
            pool.tensor_copy(pads[:, :, D].bitcast(U32), padf[:, E:2 * E]).then_inc(pads_dmy, 1)
            pool.wait_ge(pads_dmy, 1)
            for block0, blocks in ((0, E), (E, DUMMY - E)):
                at = E * REGION + block0 * P
                pool.dma_start(rows_d[at:at + blocks * P, :].rearrange("(e p) w -> p e w", p=P),
                               pads[:, 0:blocks, :]).then_inc(dmy_st, 16)

            def sequence(b, first, last):
                if not last:
                    rstds(0, b + 1)
                if not first:
                    rstds(1, b - 1)
                    twice(b - 1)
                    rstds(2, b - 1)
                    scatter(b - 1)

            sequence(0, True, False)
            with pool.Fori(1, B - 1) as b:
                sequence(b, False, False)
            sequence(B - 1, False, True)
            def store(t, k):
                nth = count(t + 1)
                apart(pool)
                pool.wait_ge(yw_sb, nth)
                pool.indirect_dma_start(res_d, bass.IndirectOffsetOnAxis(xg[k][:, D:D + 1].bitcast(U32), 0),
                                        yw[k], None).then_inc(res_st[k], 16)

            b = B - 1
            tail = {1: lambda: rstds(1, b), 3: lambda: twice(b), 18: lambda: rstds(2, b), 20: lambda: duplicate(b),
                    28: lambda: scatter_chunk(b, 0), 29: lambda: scatter_chunk(b, 1),
                    30: lambda: scatter_chunk(b, 2), 31: lambda: scatter_chunk(b, 3)}
            for t in range(EARLY):
                store(t, t % RING)
                if t in tail:
                    tail[t]()
            with pool.Fori(EARLY, TILES - RING + 1, RING) as t:
                for k in range(RING):
                    store(t + k, k)

            def group(i):
                pool.wait_ge(ld_z[i % ZBUF], 16 * (i // ZBUF + 1))
                if i >= 2:
                    pool.wait_ge(c_sb, i - 1)
                zg = z[i % ZBUF]
                pool.tensor_tensor(zs[i % 2], zg[:, :, 0, :], zg[:, :, 1, :], ALU.add).then_inc(z_sum, 1)

            def rs(i, k):
                pool.wait_ge(c_nm, i + 1)
                pool.tensor_scalar(ve[k][:, :], mv[k][:, :, 1], EPS_LN, 1.0, ALU.add, ALU.mult).then_inc(c_ve, 1)
                pool.wait_ge(c_ve, i + 1)
                pool.tensor_tensor(rs_c[k][:, :], ve[k][:, :], neg_half[:, :], ALU.pow).then_inc(c_r, 1)
                pool.wait_ge(c_r, 2 * i + 1)
                pool.tensor_tensor(nmr[k][:, :], nmr[k][:, :], rs_c[k][:, :], ALU.mult).then_inc(c_r, 1)

            group(0)
            for i in range(B):
                if i + 1 < B:
                    group(i + 1)
                rs(i, i % 2)


_INS = ["L0_attn_x", "L0_attn_ln1_g", "L0_attn_ln1_b", "L0_attn_Wq", "L0_attn_Wk", "L0_attn_Wv", "L0_attn_Wo",
        "L0_attn_ln2_g", "L0_attn_ln2_b", "L0_attn_Wf1", "L0_attn_Wf2", "L0_ffn_gate_w", "L0_ffn_gate_b",
        "L0_ffn_w1", "L0_ffn_b1", "L0_ffn_w2", "L0_ffn_b2"]


def kernel(**inputs):
    import numpy as np
    import concourse.bacc as bacc
    from concourse.bass_utils import run_bass_kernel_spmd

    nc = bacc.Bacc("TRN2", target_bir_lowering=False, num_devices=1)
    arrays, args = {}, []
    for name in _INS:
        a = np.ascontiguousarray(inputs[name])
        arrays[f"in_{name}"] = a
        args.append(nc.dram_tensor(f"in_{name}", a.shape, mybir.dt.from_np(a.dtype), kind="ExternalInput").ap())
    args.append(nc.dram_tensor("out", (B, T, D), F32, kind="ExternalOutput").ap())
    build(nc, *args)
    r = run_bass_kernel_spmd(nc, [arrays], core_ids=[0])
    return r.results[0]["out"]
```
